# Optimizing a Trainium2 kernel written in Bass

```python
import numpy as np
import jax
import jax.numpy as jnp

def _softmax(x, axis=-1):
    return jax.nn.softmax(x, axis=axis)

def _gelu(x):
    return jax.nn.gelu(x, approximate=True)

def _silu(x):
    return jax.nn.silu(x)

def _sigmoid(x):
    return jax.nn.sigmoid(x)

def _layernorm(x, axis=-1, eps=1e-05):
    m = jnp.mean(x, axis=axis, keepdims=True)
    v = jnp.var(x, axis=axis, keepdims=True)
    return (x - m) / jnp.sqrt(v + eps)

def _scatter_add(tgt, idx, src, axis=0):
    return tgt.at[idx].add(src)

def _segment_sum(src, seg, n):
    return jax.ops.segment_sum(src, seg, n)
kernel_name = 'mk_flamingo_gated_d1_seqx_r2_4315b5'

def setup_inputs(seed: int=0):
    np.random.seed(seed)
    _w = jnp.asarray

    def _rec_inputs():
        import jax
        import jax.numpy as jnp
        _rk = jax.random.key(seed)
        x = 7.22e-05 + 1 * jax.random.normal(jax.random.fold_in(_rk, 1), (2, 2048, 512), jnp.float32)
        _lenS = 2048 - jax.random.randint(jax.random.fold_in(_rk, 7), (2,), 0, max(1, 2048 // 4) + 1, jnp.int32)
        _lenS2 = 154 - jax.random.randint(jax.random.fold_in(_rk, 8), (2,), 0, max(1, 154 // 4) + 1, jnp.int32)
        _ctx_1024P = jax.random.normal(jax.random.fold_in(_rk, 11), (2, 16, 512), jnp.float32)
        _ctx_1024c = jax.random.dirichlet(jax.random.fold_in(_rk, 511), 0.3 * jnp.ones((16,), jnp.float32), (2, 154))
        _ctx_1024t = jnp.einsum('bsk,bkd->bsd', _ctx_1024c, _ctx_1024P)
        _ctx_1024t = _ctx_1024t * jax.lax.rsqrt(jnp.mean(jnp.square(_ctx_1024t)) + 1e-12) * 0.953939
        ctx_1024 = 4.13588e-05 + 0.999923 * (_ctx_1024t + 0.3 * jax.random.normal(jax.random.fold_in(_rk, 611), (2, 154, 512), jnp.float32))
        _g = jax.random.normal(jax.random.fold_in(_rk, 9001), (2, 1), jnp.float32)
        _g = jnp.sign(_g) * jnp.maximum(jnp.abs(_g), 1.0) + (_g == 0) * 1.0
        g_xattn = _g[0]
        g_ffn = _g[1]
        return (x, ctx_1024, g_xattn, g_ffn)
    x, ctx_1024, g_xattn, g_ffn = _rec_inputs()

    def _L0_xattn_setup():
        import jax, jax.numpy as jnp
        import numpy as np
        B, SQ, SKV = (4, 1024, 1024)
        INPUT_DIM, EMBED_DIM, NUM_HEADS = (512, 512, 16)
        HEAD_DIM = EMBED_DIM // NUM_HEADS
        key = jax.random.key(seed)
        kq, kc, kwkv, kwo = jax.random.split(key, 4)

        def xavier(k, shape):
            fan_in, fan_out = shape
            lim = jnp.sqrt(6.0 / (fan_in + fan_out))
            return jax.random.uniform(k, shape, jnp.float32, -lim, lim)
        return {'q': jax.random.normal(kq, (B, SQ, EMBED_DIM), jnp.float32), 'c': jax.random.normal(kc, (B, SKV, INPUT_DIM), jnp.float32), 'W_kv': xavier(kwkv, (INPUT_DIM, 2 * EMBED_DIM)), 'b_kv': jnp.zeros((2 * EMBED_DIM,), jnp.float32), 'W_o': xavier(kwo, (EMBED_DIM, EMBED_DIM)), 'b_o': jnp.zeros((EMBED_DIM,), jnp.float32)}
    _L0_xattn_all = _L0_xattn_setup()
    _L0_xattn_in = {k: v for k, v in _L0_xattn_all.items() if k in ('W_kv', 'b_kv', 'W_o', 'b_o')}
    del _L0_xattn_all

    def _L0_ffn_setup():
        import jax, jax.numpy as jnp
        import numpy as np
        B, S, HID, DFF, E, K = (4, 1024, 512, 2048, 8, 1024)
        key = jax.random.key(seed)
        ks = jax.random.split(key, 4)
        sc_h = 1.0 / np.sqrt(HID)
        sc_f = 1.0 / np.sqrt(DFF)
        return {'x': jax.random.normal(ks[0], (B, S, HID), jnp.float32), 'router_w': jax.random.normal(ks[1], (HID, E), jnp.float32) * sc_h, 'router_b': jnp.zeros((E,), jnp.float32), 'w1': jax.random.normal(ks[2], (E, HID, DFF), jnp.float32) * sc_h, 'b1': jnp.zeros((E, DFF), jnp.float32), 'w2': jax.random.normal(ks[3], (E, DFF, HID), jnp.float32) * sc_f, 'b2': jnp.zeros((E, HID), jnp.float32)}
    _L0_ffn_all = _L0_ffn_setup()
    _L0_ffn_in = {k: v for k, v in _L0_ffn_all.items() if k in ('router_w', 'router_b', 'w1', 'b1', 'w2', 'b2')}
    del _L0_ffn_all
    return {'x': x, 'ctx_1024': ctx_1024, 'g_xattn': g_xattn, 'g_ffn': g_ffn, 'L0_xattn_W_kv': _L0_xattn_in['W_kv'], 'L0_xattn_b_kv': _L0_xattn_in['b_kv'], 'L0_xattn_W_o': _L0_xattn_in['W_o'], 'L0_xattn_b_o': _L0_xattn_in['b_o'], 'L0_ffn_router_w': _L0_ffn_in['router_w'], 'L0_ffn_router_b': _L0_ffn_in['router_b'], 'L0_ffn_w1': _L0_ffn_in['w1'], 'L0_ffn_b1': _L0_ffn_in['b1'], 'L0_ffn_w2': _L0_ffn_in['w2'], 'L0_ffn_b2': _L0_ffn_in['b2']}

def reference(x, ctx_1024, g_xattn, g_ffn, L0_xattn_W_kv, L0_xattn_b_kv, L0_xattn_W_o, L0_xattn_b_o, L0_ffn_router_w, L0_ffn_router_b, L0_ffn_w1, L0_ffn_b1, L0_ffn_w2, L0_ffn_b2):
    import jax
    import jax.numpy as jnp

    def _L0_xattn_ref(q, c, W_kv, b_kv, W_o, b_o):
        import jax, jax.numpy as jnp
        import numpy as np
        B, SQ, SKV = (4, 1024, 1024)
        INPUT_DIM, EMBED_DIM, NUM_HEADS = (512, 512, 16)
        HEAD_DIM = EMBED_DIM // NUM_HEADS
        Bc, Skv, _ = c.shape
        Bq, Sq, embed_dim = q.shape
        kv = c @ W_kv + b_kv
        kv = kv.reshape(Bc, Skv, NUM_HEADS, 2 * HEAD_DIM).transpose(0, 2, 1, 3)
        k, v = jnp.split(kv, 2, axis=-1)
        qh = q.reshape(Bq, Sq, NUM_HEADS, HEAD_DIM).transpose(0, 2, 1, 3)
        scale = 1.0 / jnp.sqrt(jnp.asarray(HEAD_DIM, q.dtype))
        logits = jnp.einsum('bhqd,bhkd->bhqk', qh, k) * scale
        attn = jax.nn.softmax(logits, axis=-1)
        values = jnp.einsum('bhqk,bhkd->bhqd', attn, v)
        values = values.transpose(0, 2, 1, 3).reshape(Bc, Sq, embed_dim)
        out = values @ W_o + b_o
        return out

    def _L0_ffn_ref(x, router_w, router_b, w1, b1, w2, b2):
        import jax, jax.numpy as jnp
        import numpy as np
        B, S, HID, DFF, E, K = (4, 1024, 512, 2048, 8, 1024)
        b, s, h = x.shape
        xf = x.reshape(-1, h)
        logits = xf @ router_w + router_b
        scores = jax.nn.softmax(logits, axis=-1)
        G, idx = jax.lax.top_k(scores.T, K)
        toks = xf[idx]
        h1 = jax.nn.relu(jnp.einsum('ekh,ehf->ekf', toks, w1) + b1[:, None, :])
        eo = jnp.einsum('ekf,efh->ekh', h1, w2) + b2[:, None, :]
        contrib = (eo * G[..., None]).reshape(-1, h)
        y = jnp.zeros_like(xf).at[idx.reshape(-1)].add(contrib)
        return y.reshape(b, s, h)
    x = x + jnp.tanh(g_xattn[0]) * _L0_xattn_ref(_layernorm(x, axis=-1), ctx_1024, L0_xattn_W_kv, L0_xattn_b_kv, L0_xattn_W_o, L0_xattn_b_o)
    x = x + jnp.tanh(g_ffn[0]) * _L0_ffn_ref(_layernorm(x, axis=-1), L0_ffn_router_w, L0_ffn_router_b, L0_ffn_w1, L0_ffn_b1, L0_ffn_w2, L0_ffn_b2)
    return x

_drawn_inputs = setup_inputs


def setup_inputs(seed=0):
    import zlib

    import numpy as np

    out = dict(_drawn_inputs(seed))
    spreads = {'L0_xattn_b_kv': (0.0, 0.1),
     'L0_xattn_b_o': (0.0, 0.1),
     'L0_ffn_router_b': (0.0, 0.359),
     'L0_ffn_b1': (0.0, 0.309),
     'L0_ffn_b2': (0.0, 0.1)}
    factors = {}
    for name, (base, spread) in spreads.items():
        noise = np.random.default_rng([zlib.crc32(name.encode()), seed]).standard_normal(out[name].shape)
        drawn = base * np.exp(spread * noise) if base else spread * noise
        out[name] = jnp.asarray(drawn.astype(out[name].dtype))
    for name, factor in factors.items():
        out[name] = (out[name] * factor).astype(out[name].dtype)
    return out
```

```python
import concourse.bass as bass
from concourse import mybir
from contextlib import ExitStack

F32 = mybir.dt.float32
F32R = mybir.dt.float32r
BF16 = mybir.dt.bfloat16
I32 = mybir.dt.int32
U32 = mybir.dt.uint32
ALU = mybir.AluOpType
ACT = mybir.ActivationFunctionType
AX = mybir.AxisListType

P = 128
B, S, D = 2, 2048, 512
KV = 154
H, DH = 16, 32
E, F, TOPK = 8, 2048, 1024
EPS = 1e-5
SCALE = DH ** -0.5

DC = D // P
HC = P // DH
KR = KV - P
VW = DH + 1
TB = 512
TT = TB // P
PAIRS = S // TB
NT = B * S // P
FC = F // P
BLOCKS = TOPK // TB
SLOTS = TOPK // P
RING = 2
STEPS = BLOCKS * FC
SCORE_BITS = 30
PARTS = 5


class Order:

    def __init__(self, engine, sem):
        self.engine, self.sem, self.base = engine, sem, 0

    def mark(self, instruction):
        instruction.then_inc(self.sem, 1)
        self.base = self.base + 1

    def settled(self):
        self.engine.wait_ge(self.sem, self.base)

    def settled_before(self, met, value):
        self.engine.compute_val(self.base)
        self.engine.wait_ge(met, value)
        self.engine.wait_ge(self.sem, self.base)


def attention_block(nc, io, keep):
    with ExitStack() as ctx:
        def sb(name, shape, dt=F32):
            return ctx.enter_context(nc.sbuf_tensor(name, shape, dt))

        def ps(name, shape):
            return ctx.enter_context(nc.psum_tensor(name, shape, F32))

        def sem(name):
            return ctx.enter_context(nc.semaphore(name))

        ident, logits = keep["ident"], keep["logits"]
        x = sb("x_block", [P, B, TT, D])
        xn = sb("x_normed", [P, TT, D])
        xn2 = sb("x_normed2", [P, TT, D])
        qh = sb("q_hi", [P, B, DC, TB], F32R)
        ql = sb("q_lo", [P, B, DC, TB], F32R)
        pt = sb("probs", [P, 2, HC + 1, TB])
        val = sb("values", [P, TT, D])
        vh = sb("values_hi", [P, DC, TB], F32R)
        vl = sb("values_lo", [P, DC, TB], F32R)
        woh = sb("wo_hi", [P, DC, D], F32R)
        wol = sb("wo_lo", [P, DC, D], F32R)
        kh = sb("k_hi", [P, B, DC, HC, KV], F32R)
        kl = sb("k_lo", [P, B, DC, HC, P], F32R)
        khr = sb("k_rest_hi", [P, B, DC, HC, DH], F32R)
        klr = sb("k_rest_lo", [P, B, DC, HC, DH], F32R)
        vm = sb("v_main", [P, B, H, VW])
        vr = sb("v_rest", [P, B, DC, HC, VW])
        selm = sb("minus_head", [P, H, P], F32R)
        selr = sb("minus_head_rest", [P, DC, HC, DH], F32R)
        mst = sb("max_staged", [P, TT, P], F32R)
        mt = sb("max_T", [P, TB], F32R)
        x2t = sb("x2_T", [P, 2, DC, P])
        ct = sb("ctx_T", [P, B, DC, 2 * P])
        tgbo = sb("gated_b_o", [P, D])
        bvb = sb("b_v", [P, H, DH])
        bk = sb("b_k", [P, DC])
        rw = sb("router_w", [P, DC, E])
        rbb = sb("router_b", [P, E])
        gate = sb("attn_gate", [P, 1])
        tg = sb("attn_tanh", [P, 1])
        neghalf = sb("neg_half", [P, TT])
        eps = sb("eps", [P, TT])
        stats = sb("bn_stats", [P, TT, 6])
        mv = sb("mean_var", [P, TT, 2])
        ve = sb("var_eps", [P, TT])
        rstd = sb("rstd", [P, TT])
        mx = sb("max_logit", [P, TT, H])
        rc = sb("recip_sum", [P, 2, 2, HC])
        wkv = pt[:, :, :, :].rearrange("p a b n -> p (a b n)")[:, 0:DC * 2 * D].rearrange(
            "p (k z n) -> p k z n", k=DC, z=2)
        cx = val[:, :, :].rearrange("p (b z) d -> p b z d", b=B)
        wo_raw = xn
        sel_raw = xn2[:, :, :].rearrange("p t (u n) -> p (t u) n", n=P)
        selr_raw = x2t[:, 0, :, :].rearrange("p c (j r) -> p c j r", j=HC)

        pb = ps("p_max", [P, 2, 512])
        pl = ps("p_logits", [P, 2, 512])
        po = ps("p_values", [P, 2, 512])
        ptr = ps("p_transposed", [P, 512])
        pw = ps("p_out", [P, 512])
        po_t = po[:, :, 0:2 * HC * VW].rearrange("p u (t j w) -> p u t j w", t=2, j=HC)
        router_out = po[:, 1, 512 - TT * E:512]

        s_ctx, s_wkv, s_wo, s_small = sem("ctx_in"), sem("wkv_in"), sem("wo_in"), sem("small_in")
        s_x = [sem(f"x_in{b}") for b in range(B)]
        s_x1st = [sem(f"x1_stored{b}") for b in range(B)]
        s_xn2st = sem("xn2_stored")
        pool_order, dve_order = sem("pool_order"), sem("dve_order")
        consts_ready, sel_ready, sel_split = sem("consts_ready"), sem("sel_ready"), sem("sel_split")
        pre_pe, pre_act, pre_dve = sem("prologue_pe"), sem("prologue_act"), sem("prologue_dve")
        wo_hi_done, tanh_done, bo_done = sem("wo_hi_done"), sem("tanh_done"), sem("bo_done")
        mv1_ready, mv2_ready = sem("mv1_ready"), sem("mv2_ready")
        rstd1_ready, rstd2_ready = sem("rstd1_ready"), sem("rstd2_ready")
        xn_ready, xb_ready, xn2_ready = sem("xn_ready"), sem("xb_ready"), sem("xn2_ready")
        t_full, t_free = sem("transposed_full"), sem("transposed_free")
        hi_done = sem("hi_done")
        b_full, b_free = sem("max_logits_full"), sem("max_logits_free")
        m_ready, mt_ready = sem("max_staged_ready"), sem("max_T_ready")
        l_full, l_free = sem("logits_full"), sem("logits_free")
        o_full, o_free = sem("values_full"), sem("values_free")
        w_full, w_free = sem("out_full"), sem("out_free")
        x2t_ready, r_full = sem("x2T_ready"), sem("router_full")
        UQ, UM, UV, UX, USES = 0, TT, TT + 1, TT + 1 + DC, TT + 1 + DC + TT
        NL = HC + 1
        BU = TT * DC * 2

        xr = io["x"].rearrange("b s d -> (b s) d")
        outr = io["out"].rearrange("b s d -> (b s) d")
        xn2_d = io["xn2_d"]
        block = ctx.enter_context(nc.Block())

        def rows(dram, row):
            return dram[bass.ds(row, TB), :].rearrange("(t p) d -> p t d", p=P)

        @block.sync
        def _(sp):
            for b in range(B):
                sp.dma_start(cx[:, b, 0, :], io["ctx"][b, 0:P, :]).then_inc(s_ctx, 16)
                sp.dma_start(cx[0:KR, b, 1, :], io["ctx"][b, P:KV, :]).then_inc(s_ctx, 16)
            wkv_dram = io["wkv"].rearrange("(k p) (h z d) -> p k z h d", p=P, z=2, d=DH)
            for k in range(DC):
                for z in range(2):
                    sp.dma_start(wkv[:, k, z, :].rearrange("p (h d) -> p h d", d=DH),
                                 wkv_dram[:, k, z, :, :]).then_inc(s_wkv, 16)
            with nc.allow_non_contiguous_dma(reason="512 biases, once"):
                for j in range(HC):
                    bkj = io["bkv"].rearrange("(c j z d) -> j z d c", j=HC, z=2, d=DH)
                    sp.dma_start(bk[j * DH:(j + 1) * DH, :], bkj[j, 0]).then_inc(s_small, 16)
                bv = io["bkv"].rearrange("(o h z d) -> o h z d", o=1, z=2, d=DH)[:, :, 1, :]
                sp.dma_start(bvb[:, :, :], bv.broadcast_to([P, H, DH])).then_inc(s_small, 16)
                sp.dma_start(rbb[:, :], io["rb"].rearrange("(o n) -> o n", o=1).broadcast_to([P, E])).then_inc(s_small, 16)
                sp.dma_start(tgbo[:, :], io["bo"].rearrange("(o n) -> o n", o=1).broadcast_to([P, D])).then_inc(s_small, 16)
                sp.dma_start(gate[:, :], io["g_attn"].rearrange("(o n) -> o n", o=1).broadcast_to([P, 1])).then_inc(s_small, 16)
            sp.dma_start(rw[:, :, :], io["rw"].rearrange("(k p) n -> p k n", p=P)).then_inc(s_small, 16)
            sp.dma_start(wo_raw[:, :, :], io["wo"].rearrange("(k p) n -> p k n", p=P)).then_inc(s_wo, 16)
            with sp.Fori(0, PAIRS) as i:
                stored, stored_xn2 = sp.snap(i * 16), sp.snap(i * (16 * B))
                done = [sp.snap(i * (B * TT) + (b + 1) * TT) for b in range(B)]
                row = [sp.snap(i * TB + b * S) for b in range(B)]
                for v in (stored, stored_xn2, *done, *row, *(r * D for r in row)):
                    sp.compute_val(v)
                for b in range(B):
                    sp.wait_ge(s_ctx, 16 * 2 * B)
                    sp.wait_ge(s_xn2st, stored_xn2)
                    sp.wait_ge(s_x1st[b], stored)
                    sp.dma_start(x[:, b, :, :], rows(xr, row[b])).then_inc(s_x[b], 16)
                for b in range(B):
                    sp.wait_ge(s_ctx, 16 * 2 * B)
                    sp.wait_ge(w_free, done[b])
                    sp.dma_start(rows(outr, row[b]), x[:, b, :, :]).then_inc(s_x1st[b], 16)
                    sp.wait_ge(s_ctx, 16 * 2 * B)
                    sp.wait_ge(xn2_ready, done[b])
                    sp.dma_start(rows(xn2_d, row[b]), xn2[:, :, :]).then_inc(s_xn2st, 16)
            for b in range(B):
                sp.wait_ge(s_x1st[b], 16 * PAIRS)
            sp.wait_ge(s_xn2st, 16 * PAIRS * B)

        @block.gpsimd
        def _(pool):
            order = Order(pool, pool_order)
            order.mark(pool.memset(ident[:, :], 0.0))
            order.mark(pool.memset(sel_raw, 0.0))
            order.mark(pool.memset(selr_raw, 0.0))
            order.settled()
            pool.affine_select(out=ident[:, :], in_=ident[:, :], compare_op=ALU.not_equal, fill=1.0, base=0,
                               pattern=[[-1, P]], channel_multiplier=1).then_inc(consts_ready, 1)
            for half in range(2):
                order.mark(pool.affine_select(out=sel_raw, in_=sel_raw, compare_op=ALU.not_equal, fill=-1.0,
                                              base=-32 * half, pattern=[[-1, H], [0, P]], channel_multiplier=1))
                order.mark(pool.affine_select(out=selr_raw, in_=selr_raw, compare_op=ALU.not_equal, fill=-1.0,
                                              base=-32 * half, pattern=[[-HC, DC], [-1, HC], [0, DH]],
                                              channel_multiplier=1))
                order.settled()
            order.mark(pool.memset(selr_raw[:, :, :, KR:DH], 0.0))
            order.settled()
            order.mark(pool.memset(eps[:, :], EPS))
            pool.memset(neghalf[:, :], -0.5).then_inc(sel_ready, 1)
            start = order.base
            with pool.Fori(0, PAIRS) as i:
                order.base = i * (2 * B) + start
                for b in range(B):
                    for mv_ready, rstd_ready in ((mv1_ready, rstd1_ready), (mv2_ready, rstd2_ready)):
                        pool.wait_ge(mv_ready, i * B + b + 1)
                        order.mark(pool.tensor_tensor(ve[:, :], mv[:, :, 1], eps[:, :], ALU.add))
                        order.settled()
                        pool.tensor_tensor(rstd[:, :], ve[:, :], neghalf[:, :], ALU.pow).then_inc(rstd_ready, 1)
                        if mv_ready is mv1_ready:
                            pool.wait_ge(xn_ready, i * (B * TT) + (b + 1) * TT)
                            pool.wait_ge(bo_done, 1)
                            pool.tensor_tensor(x[:, b, :, :], x[:, b, :, :],
                                               tgbo[:, :].unsqueeze(1).broadcast_to([P, TT, D]),
                                               ALU.add).then_inc(xb_ready, 1)

        @block.scalar
        def _(act):
            act.wait_ge(s_small, 16 * 9)
            act.activation(tg[:, :], gate[:, :], ACT.Tanh).then_inc(tanh_done, 1)
            act.wait_ge(sel_ready, 1)
            act.activation(selm[:, :, :], sel_raw, ACT.Copy).then_inc(sel_split, 1)
            act.activation(selr[:, :, :, :], selr_raw, ACT.Copy).then_inc(sel_split, 1)
            act.wait_ge(s_wo, 16)
            act.activation(woh[:, :, :], wo_raw[:, :, :], ACT.Copy).then_inc(wo_hi_done, 1)
            act.wait_ge(pre_dve, 1)
            for b in range(B):
                act.wait_ge(pre_pe, 4 * b + 1)
                act.activation(ct[:, b, :, 0:P], pb[:, 0, :].rearrange("p (k n) -> p k n", k=DC), ACT.Copy)\
                   .then_inc(pre_act, 1)
                for j in range(HC):
                    act.activation(ct[:, b, :, P + j * DH:P + j * DH + KR],
                                   pb[:, 1, 0:DC * P].rearrange("p (k n) -> p k n", k=DC)[:, :, 0:KR], ACT.Copy)\
                       .then_inc(pre_act, 1)
                act.wait_ge(pre_pe, 4 * b + 2)
                for c in range(DC):
                    for j in range(HC):
                        hr = slice(j * DH, (j + 1) * DH)
                        act.activation(kh[hr, b, c, j, :], pl[hr, c // 2, (c % 2) * KV:(c % 2 + 1) * KV],
                                       ACT.Identity, bias=bk[hr, c:c + 1]).then_inc(pre_act, 1)
            act.sem_inc(l_free, 2)
            with act.Fori(0, PAIRS) as i:
                for b in range(B):
                    def use(k):
                        return i * (B * USES) + b * USES + k + 1
                    for t in range(TT):
                        act.wait_ge(t_full, use(UQ + t))
                        act.activation(qh[:, b, :, t * P:(t + 1) * P],
                                       ptr[:, :].rearrange("p (c n) -> p c n", c=DC), ACT.Copy).then_inc(hi_done, 1)
                    act.wait_ge(t_full, use(UM))
                    act.activation(mt[:, :], ptr[:, :], ACT.Copy).then_inc(t_free, 1)
                    for c in range(DC):
                        for s in range(NL):
                            act.wait_ge(l_full, i * (B * DC * NL) + (b * DC + c) * NL + s + 1)
                            act.activation(pt[:, c % 2, s, :], pl[:, (c * NL + s) % 2, :], ACT.Exp,
                                           scale=SCALE).then_inc(l_free, 1)
                    for c in range(DC):
                        act.wait_ge(t_full, use(UV + c))
                        act.activation(vh[:, c, :], ptr[:, :], ACT.Copy).then_inc(hi_done, 1)
                    for t in range(TT):
                        act.wait_ge(t_full, use(UX + t))
                        act.activation(x2t[:, t % 2, :, :], ptr[:, :].rearrange("p (c n) -> p c n", c=DC),
                                       ACT.Copy).then_inc(t_free, 1)

        @block.vector
        def _(dve):
            order = Order(dve, dve_order)
            dve.memset(kh[:, :, :, :, :].bitcast(F32), 0.0)
            dve.memset(kl[:, :, :, :, :].bitcast(F32), 0.0)
            dve.memset(khr[:, :, :, :, :].bitcast(F32), 0.0)
            dve.memset(klr[:, :, :, :, :].bitcast(F32), 0.0)
            dve.memset(vr[:, :, :, :, :], 0.0)
            dve.memset(vm[:, :, :, DH:VW], 1.0)
            dve.memset(mst[:, :, :].bitcast(F32), 0.0)
            order.mark(dve.memset(ct[:, :, :, P:2 * P], 0.0))
            order.settled()
            for j in range(HC):
                done = dve.memset(vr[j * DH:j * DH + KR, :, :, j, DH:VW], 1.0)
            done.then_inc(pre_dve, 1)
            dve.wait_ge(wo_hi_done, 1)
            dve.wait_ge(s_wo, 16)
            dve.tensor_tensor(wol[:, :, :], wo_raw[:, :, :], woh[:, :, :].bitcast(F32), ALU.subtract).then_inc(pre_dve, 1)
            dve.wait_ge(tanh_done, 1)
            dve.wait_ge(s_small, 16 * 9)
            dve.tensor_scalar(tgbo[:, :], tgbo[:, :], tg[:, 0:1], None, ALU.mult).then_inc(bo_done, 1)
            for b in range(B):
                act_base = b * (1 + HC + DC * HC) + 1 + HC
                dve.wait_ge(pre_act, act_base + DC * HC)
                for c in range(DC):
                    for j in range(HC):
                        hr = slice(j * DH, (j + 1) * DH)
                        at = (c % 2) * KV
                        dve.scalar_tensor_tensor(
                            kl[hr, b, c, j, :], pl[hr, c // 2, at:at + P], bk[hr, c:c + 1],
                            kh[hr, b, c, j, 0:P].bitcast(F32), ALU.add, ALU.subtract)
                        dve.tensor_copy(khr[hr, b, c, j, 0:KR], kh[hr, b, c, j, P:KV].bitcast(F32))
                        done = dve.scalar_tensor_tensor(
                            klr[hr, b, c, j, 0:KR], pl[hr, c // 2, at + P:at + KV], bk[hr, c:c + 1],
                            kh[hr, b, c, j, P:KV].bitcast(F32), ALU.add, ALU.subtract)
                done.then_inc(pre_dve, 1)
                dve.wait_ge(pre_pe, 4 * b + 3)
                dve.tensor_tensor(vm[:, b, :, 0:DH], po[:, 0, :].rearrange("p (h d) -> p h d", d=DH),
                                  bvb[:, :, :], ALU.add).then_inc(pre_dve, 1)
                dve.wait_ge(pre_pe, 4 * b + 4)
                for j in range(HC):
                    kr = slice(j * DH, j * DH + KR)
                    done = dve.tensor_tensor(
                        vr[kr, b, :, j, 0:DH], po[kr, 1, :].rearrange("p (c j d) -> p c j d", j=HC, d=DH)[:, :, j, :],
                        bvb[kr, :, :].rearrange("p (c j) d -> p c j d", j=HC)[:, :, j, :], ALU.add)
                done.then_inc(pre_dve, 1)
            dve.sem_inc(b_free, 2)
            dve.sem_inc(o_free, 2)
            start = order.base
            with dve.Fori(0, PAIRS) as i:
                order.base = i * (B * (TT + 1 + 2 * DC + TT + 1)) + start
                for b in range(B):
                    dve.wait_ge(s_x[b], i * 16 + 16)
                    for t in range(TT):
                        order.mark(dve.bn_stats(stats[:, t, :], x[:, b, t, :]))
                    order.settled_before(s_small, 16 * 9)
                    for t in range(TT):
                        done = dve.bn_aggr(mv[:, t, :], stats[:, t, :])
                    done.then_inc(mv1_ready, 1)
                    dve.wait_ge(rstd1_ready, i * B + b + 1)
                    for t in range(TT):
                        dve.tensor_scalar(xn[:, t, :], x[:, b, t, :], mv[:, t, 0:1], rstd[:, t:t + 1],
                                          ALU.subtract, ALU.mult).then_inc(xn_ready, 1)
                    for t in range(TT):
                        dve.wait_ge(hi_done, i * (B * (TT + DC)) + b * (TT + DC) + t + 1)
                        dve.tensor_tensor(ql[:, b, :, t * P:(t + 1) * P],
                                          ptr[:, :].rearrange("p (c n) -> p c n", c=DC),
                                          qh[:, b, :, t * P:(t + 1) * P].bitcast(F32), ALU.subtract).then_inc(t_free, 1)
                    for t in range(TT):
                        for c in range(DC):
                            for u in range(2):
                                n = (t * DC + c) * 2 + u
                                dve.wait_ge(b_full, i * (B * BU) + b * BU + n + 1)
                                done = dve.tensor_reduce(mx[:, t, c * HC + 2 * u:c * HC + 2 * u + 2],
                                                         pb[:, u, 0:2 * KV].rearrange("p (j n) -> p j n", j=2),
                                                         AX.X, ALU.max)
                                done.then_inc(b_free, 1)
                    dve.wait_ge(b_free, i * (B * BU) + (b + 1) * BU + 2)
                    order.mark(dve.tensor_copy(mst[:, :, 0:H], mx[:, :, :]))
                    order.settled()
                    dve.tensor_tensor(mst[:, :, 32:32 + H], mx[:, :, :], mst[:, :, 0:H].bitcast(F32),
                                      ALU.subtract).then_inc(m_ready, 1)
                    for c in range(DC):
                        for u in range(2):
                            dve.wait_ge(o_full, i * (B * DC * 2) + b * DC * 2 + c * 2 + u + 1)
                            order.mark(dve.reciprocal(rc[:, u, :, :], po_t[:, u, :, :, DH]))
                            order.settled()
                            dve.tensor_tensor(
                                val[:, 2 * u:2 * u + 2, c * P:(c + 1) * P].rearrange("p t (j d) -> p t j d", d=DH),
                                po_t[:, u, :, :, 0:DH], rc[:, u, :, :].unsqueeze(3).broadcast_to([P, 2, HC, DH]),
                                ALU.mult).then_inc(o_free, 1)
                    for c in range(DC):
                        dve.wait_ge(hi_done, i * (B * (TT + DC)) + b * (TT + DC) + TT + c + 1)
                        dve.tensor_tensor(vl[:, c, :], ptr[:, :], vh[:, c, :].bitcast(F32),
                                          ALU.subtract).then_inc(t_free, 1)
                    dve.wait_ge(xb_ready, i * B + b + 1)
                    for t in range(TT):
                        dve.wait_ge(w_full, i * (B * TT) + b * TT + t + 1)
                        dve.scalar_tensor_tensor(x[:, b, t, :], pw[:, :], tg[:, 0:1], x[:, b, t, :],
                                                 ALU.mult, ALU.add).then_inc(w_free, 1)
                        dve.wait_ge(w_free, i * (B * TT) + b * TT + t + 1)
                        order.mark(dve.bn_stats(stats[:, t, :], x[:, b, t, :]))
                    order.settled_before(s_small, 16 * 9)
                    for t in range(TT):
                        done = dve.bn_aggr(mv[:, t, :], stats[:, t, :])
                    done.then_inc(mv2_ready, 1)
                    dve.wait_ge(rstd2_ready, i * B + b + 1)
                    dve.wait_ge(s_xn2st, (i * B + b) * 16)
                    for t in range(TT):
                        dve.tensor_scalar(xn2[:, t, :], x[:, b, t, :], mv[:, t, 0:1], rstd[:, t:t + 1],
                                          ALU.subtract, ALU.mult).then_inc(xn2_ready, 1)
                    dve.wait_ge(r_full, i * B + b + 1)
                    order.mark(dve.tensor_tensor(logits[:, bass.ds(i * TT + b * (S // P), TT), :],
                                                 router_out.rearrange("p (t e) -> p t e", e=E),
                                                 rbb[:, :].unsqueeze(1).broadcast_to([P, TT, E]), ALU.add))

        @block.tensor
        def _(pe):
            pe.wait_ge(consts_ready, 1)
            pe.wait_ge(s_ctx, 16 * 2 * B)
            pe.wait_ge(pre_dve, 1)
            for b in range(B):
                if b:
                    pe.wait_ge(pre_act, 1 + HC)
                for k in range(DC):
                    pe.transpose(pb[:, 0, k * P:(k + 1) * P], cx[:, b, 0, k * P:(k + 1) * P], ident[:, :])
                for k in range(DC):
                    done = pe.transpose(pb[:, 1, k * P:k * P + KR], cx[0:KR, b, 1, k * P:(k + 1) * P],
                                        ident[0:KR, 0:KR])
                done.then_inc(pre_pe, 1)
                pe.wait_ge(pre_act, b * (1 + HC + DC * HC) + 1 + HC)
                pe.wait_ge(s_wkv, 16 * 2 * DC)
                if b:
                    pe.wait_ge(pre_dve, 2 + 1)
                for c in range(DC):
                    for k in range(DC):
                        done = pe.matmul(pl[:, c // 2, (c % 2) * KV:(c % 2 + 1) * KV],
                                         wkv[:, k, 0, c * P:(c + 1) * P], ct[:, b, k, 0:KV],
                                         start=k == 0, stop=k == DC - 1)
                done.then_inc(pre_pe, 1)
                if b:
                    pe.wait_ge(pre_dve, 2 + 3)
                for z in range(2):
                    for k in range(DC):
                        done = pe.matmul(po[:, z, :], ct[:, b, k, z * P:(z + 1) * P], wkv[:, k, 1, :],
                                         start=k == 0, stop=k == DC - 1)
                    done.then_inc(pre_pe, 1)
            pe.wait_ge(pre_dve, 2 + 3 * B)
            pe.wait_ge(sel_split, 2)
            with pe.Fori(0, PAIRS) as i:
                for b in range(B):
                    def bank(k):
                        pe.wait_ge(t_free, i * (B * USES) + b * USES + k)

                    def logits_of(c):
                        for s in range(NL):
                            n = c * NL + s
                            pe.wait_ge(l_free, i * (B * DC * NL) + b * DC * NL + n + 1)
                            if s < HC:
                                khs, kls, sel = kh[:, b, c, s, 0:P], kl[:, b, c, s, :], selm[:, c * HC + s, :]
                            else:
                                khs, kls, sel = (w.rearrange("p j r -> p (j r)") for w in (
                                    khr[:, b, c, :, :], klr[:, b, c, :, :], selr[:, c, :, :]))
                            pe.matmul(pl[:, n % 2, :], khs, qh[:, b, c, :], start=True, stop=False)
                            pe.matmul(pl[:, n % 2, :], khs, ql[:, b, c, :], start=False, stop=False)
                            pe.matmul(pl[:, n % 2, :], kls, qh[:, b, c, :], start=False, stop=False)
                            pe.matmul(pl[:, n % 2, :], sel, mt[:, :], start=False, stop=True).then_inc(l_full, 1)

                    def values_of(c):
                        pe.wait_ge(l_free, i * (B * DC * NL) + (b * DC + c + 1) * NL + 2)
                        for u in range(2):
                            pe.wait_ge(o_free, i * (B * DC * 2) + b * DC * 2 + c * 2 + u + 1)
                            for t2 in range(2):
                                tok = slice((2 * u + t2) * P, (2 * u + t2 + 1) * P)
                                base = t2 * HC * VW
                                for j in range(HC):
                                    pe.matmul(po[:, u, base + j * VW:base + (j + 1) * VW],
                                              pt[:, c % 2, j, tok], vm[:, b, c * HC + j, :],
                                              start=j == 0, stop=False)
                                done = pe.matmul(po[:, u, base:base + HC * VW], pt[:, c % 2, HC, tok],
                                                 vr[:, b, c, :, :].rearrange("p j w -> p (j w)"),
                                                 start=False, stop=True)
                            done.then_inc(o_full, 1)

                    for t in range(TT):
                        pe.wait_ge(xn_ready, i * (B * TT) + b * TT + t + 1)
                        bank(UQ + t)
                        for c in range(DC):
                            done = pe.transpose(ptr[:, c * P:(c + 1) * P], xn[:, t, c * P:(c + 1) * P], ident[:, :])
                        done.then_inc(t_full, 1)
                    for t in range(TT):
                        pe.wait_ge(hi_done, i * (B * (TT + DC)) + b * (TT + DC) + t + 1)
                        for c in range(DC):
                            for u in range(2):
                                n = (t * DC + c) * 2 + u
                                pe.wait_ge(b_free, i * (B * BU) + b * BU + n + 1)
                                pe.matmul(pb[:, u, 0:2 * KV], qh[:, b, c, t * P:(t + 1) * P],
                                          kh[:, b, c, 2 * u:2 * u + 2, 0:KV], start=True, stop=True).then_inc(b_full, 1)
                    pe.wait_ge(m_ready, i * B + b + 1)
                    bank(UM)
                    for t in range(TT):
                        done = pe.transpose(ptr[:, t * P:(t + 1) * P], mst[:, t, :].bitcast(F32), ident[:, :])
                    done.then_inc(t_full, 1)
                    bank(UM + 1)
                    logits_of(0)
                    for c in range(DC):
                        if c + 1 < DC:
                            logits_of(c + 1)
                        values_of(c)
                    for c in range(DC):
                        pe.wait_ge(o_free, i * (B * DC * 2) + b * DC * 2 + c * 2 + 4)
                        bank(UV + c)
                        for t in range(TT):
                            done = pe.transpose(ptr[:, t * P:(t + 1) * P], val[:, t, c * P:(c + 1) * P], ident[:, :])
                        done.then_inc(t_full, 1)
                    bank(UV + DC)
                    for t in range(TT):
                        pe.wait_ge(w_free, i * (B * TT) + b * TT + t)
                        tok = slice(t * P, (t + 1) * P)
                        for c in range(DC):
                            pe.matmul(pw[:, :], vh[:, c, tok], woh[:, c, :], start=c == 0, stop=False)
                            pe.matmul(pw[:, :], vh[:, c, tok], wol[:, c, :], start=False, stop=False)
                            done = pe.matmul(pw[:, :], vl[:, c, tok], woh[:, c, :], start=False, stop=c == DC - 1)
                        done.then_inc(w_full, 1)
                    for t in range(TT):
                        pe.wait_ge(xn2_ready, i * (B * TT) + b * TT + t + 1)
                        bank(UX + t)
                        for c in range(DC):
                            done = pe.transpose(ptr[:, c * P:(c + 1) * P], xn2[:, t, c * P:(c + 1) * P], ident[:, :])
                        done.then_inc(t_full, 1)
                        bank(UX + t + 1)
                        for c in range(DC):
                            done = pe.matmul(router_out[:, t * E:(t + 1) * E], x2t[:, t % 2, c, :], rw[:, c, :],
                                             start=c == 0, stop=c == DC - 1)
                    done.then_inc(r_full, 1)


def waits(engine, met, *others):
    for _, value in others:
        engine.compute_val(value)
    engine.wait_ge(*met)
    for semaphore, value in others:
        engine.wait_ge(semaphore, value)


def experts_block(nc, io, keep):
    with ExitStack() as ctx:
        def sb(name, shape, dt=F32):
            return ctx.enter_context(nc.sbuf_tensor(name, shape, dt))

        def ps(name, shape):
            return ctx.enter_context(nc.psum_tensor(name, shape, F32))

        def sem(name):
            return ctx.enter_context(nc.semaphore(name))

        ident, logits = keep["ident"], keep["logits"]
        wh = sb("weights_hi", [P, FC, 2 * D], F32R)
        wl = sb("weights_lo", [P, FC, 2 * D], F32R)
        raw = sb("weights_raw", [P, RING, 2 * D])
        xh = sb("tokens_hi", [P, BLOCKS, DC, TB], F32R)
        xl = sb("tokens_lo", [P, BLOCKS, DC, TB], F32R)
        hf = sb("hidden", [P, 2, TB])
        hh = sb("hidden_hi", [P, 2, TB], F32R)
        hl = sb("hidden_lo", [P, 2, TB], F32R)
        gath = sb("gathered", [P, 2, D])
        yb = sb("results", [P, TT, D])
        b2b = sb("b2", [P, D])
        b1t = sb("b1_T", [P, E * FC])
        onehot_p = sb("onehot_p", [P, NT // 2, P], BF16)
        onehot_j = sb("onehot_j", [P, NT, SLOTS], BF16)
        carried = sb("carried", [P, NT, PARTS, SLOTS], BF16)
        parts = sb("parts", [P, E, NT, PARTS], BF16)
        pos_p = sb("pos_mod", [P, E, NT], BF16)
        pos_j = sb("pos_div", [P, E, NT], BF16)
        ones = sb("ones", [P, P], BF16)
        before = sb("before", [P, P], BF16)
        iota_p = sb("iota_p", [P, P], BF16)
        iota_j = sb("iota_j", [P, SLOTS], BF16)
        compact = sb("compact", [P, PARTS, SLOTS])
        idx_g = sb("index_gather", [P, SLOTS], I32)
        idx_s = sb("index_scatter", [P, SLOTS], I32)
        gate_g = sb("gate_next", [P, SLOTS])
        gate_s = sb("gate_now", [P, SLOTS])
        gtmp = sb("gate_sum", [P, SLOTS])
        gate = sb("ffn_gate", [P, 1])
        tg = sb("ffn_tanh", [P, 1])
        thr = sb("threshold_bits", [P, E], I32)
        bit = sb("bit", [P, E], I32)
        cand = sb("candidate", [P, E], I32)
        take = sb("taken_bit", [P, E], I32)
        cnt = sb("count", [P, E])
        mask = carried[:, :, :, :].rearrange("p t k j -> p (t k j)")[:, 0:2 * E * NT].rearrange(
            "p (m e t) -> p m e t", m=2, e=E)
        tmp = yb[:, :, :].rearrange("p t d -> p (t d)").rearrange("p (k e t) -> p k e t", e=E, t=NT)
        tmp2 = gath[:, :, :].rearrange("p s d -> p (s d)").rearrange("p (k e t) -> p k e t", e=E, t=NT)
        scores, ex, rest, incl = tmp[:, 0], tmp[:, 1], tmp[:, 2], tmp[:, 3]
        place, seg = tmp[:, 4], tmp[:, 5]
        posi, posi2 = tmp[:, 6].bitcast(I32), tmp[:, 7].bitcast(I32)
        b1_rows = tmp2[:, 0].rearrange("p e t -> p (e t)")[:, 0:P]
        lmax, lsum = tmp2[:, 1].rearrange("p e t -> p (e t)")[:, 0:NT], tmp2[:, 1].rearrange("p e t -> p (e t)")[:, NT:2 * NT]
        ints = tmp2[:, 2].rearrange("p e t -> p (e t)").bitcast(I32)
        ints2 = tmp2[:, 3].rearrange("p e t -> p (e t)").bitcast(I32)

        p1 = ps("p_hidden", [P, 2, 512])
        py = ps("p_results", [P, TT, 512])
        ptr = ps("p_tokens_T", [P, 512])
        pc = ps("p_counts", [P, 512])
        ex_te, scores_te = (v.rearrange("p e t -> p (e t)").rearrange("p (t e) -> p t e", e=E) for v in (ex, rest))

        s_small = sem("small_in2")
        s_raw = [sem(f"raw_in{k}") for k in range(RING)]
        s_b2 = sem("b2_in")
        s_gath = [sem(f"gathered{k}") for k in range(2)]
        s_scat = [sem(f"scattered{k}") for k in range(TT)]
        pool_order, dve_order = sem("pool_order2"), sem("dve_order2")
        consts_ready, b1_full, b1_done, tanh_done = sem("consts_ready2"), sem("b1_full"), sem("b1_done"), sem("tanh_done2")
        shifted, exp_done = sem("shifted"), sem("exp_done")
        mask_ready, counted = sem("mask_ready"), sem("counted")
        w_hi, w_lo = sem("weights_hi_done"), sem("weights_lo_done")
        oh_ready, oh_used = sem("onehot_ready"), sem("onehot_used")
        carried_ready, idx_ready = sem("carried_ready"), sem("index_ready")
        tok_full, tok_hi, tok_free = sem("tokens_full"), sem("tokens_hi_done"), sem("tokens_free")
        up_done, relu_done, lo_done, down_done = sem("up_done"), sem("relu_done"), sem("hidden_lo_done"), sem("down_done")
        y_full, y_free, y_scaled = sem("results_full"), sem("results_free"), sem("results_scaled")

        outr = io["out"].rearrange("b s d -> (b s) d")
        xn2_d = io["xn2_d"]
        block = ctx.enter_context(nc.Block())

        TILE_AT = {1: (1, 3, 5, 7), 0: (FC + 5, FC + 7, FC + 9, FC + 11)}
        HALF_AT = (FC - 6, FC - 2)
        EARLY = FC - 2

        def tile_count(e, tb, q):
            return e * (BLOCKS * TT) + tb * TT + q

        @block.sync
        def _(sp):
            sp.dma_start(b1_rows, io["b1"].rearrange("e (c p) -> (e c) p", p=P)).then_inc(s_small, 16)
            with nc.allow_non_contiguous_dma(reason="one gate"):
                sp.dma_start(gate[:, :], io["g_ffn"].rearrange("(o n) -> o n", o=1).broadcast_to([P, 1])).then_inc(s_small, 16)

            w1r = io["w1"].rearrange("e d f -> (e d) f")
            w2r = io["w2"].rearrange("e f d -> (e f) d")

            def load(e, c):
                waits(sp, (s_small, 32), (w_lo, e * FC + c + 1))
                slot = c % RING
                sp.dma_start(raw[:, slot, 0:D].rearrange("p (k f) -> p k f", k=DC),
                             w1r[bass.ds(e * D, D), c * P:(c + 1) * P].rearrange("(k p) f -> p k f", p=P))\
                    .then_inc(s_raw[slot], 16)
                sp.dma_start(raw[:, slot, D:2 * D], w2r[bass.ds(e * F + c * P, P), :]).then_inc(s_raw[slot], 16)

            def load_b2(e):
                waits(sp, (s_small, 32), (y_free, e * (BLOCKS * TT) + TT))
                sp.dma_start(b2b[:, :], io["b2"][bass.ds(e, 1), :].broadcast_to([P, D])).then_inc(s_b2, 16)

            with sp.Fori(0, E) as e:
                for c in range(FC):
                    load(e, c)
                    if c == EARLY:
                        load_b2(e)
            for slot in range(TT):
                sp.wait_ge(s_scat[slot], 16 * BLOCKS * E)

        @block.gpsimd
        def _(pool):
            order = Order(pool, pool_order)
            order.mark(pool.memset(ones[:, :], 1.0))
            order.mark(pool.memset(before[:, :], 1.0))
            order.mark(pool.memset(seg, 1.0))
            order.mark(pool.iota(ints, [[1, NT], [0, E]], base=0, channel_multiplier=0))
            order.mark(pool.iota(ints2, [[0, E * NT]], base=0, channel_multiplier=1))
            order.mark(pool.iota(posi, [[1, E * NT]], base=0, channel_multiplier=0))
            order.settled()
            order.mark(pool.affine_select(out=before[:, :], in_=before[:, :], compare_op=ALU.is_gt, fill=0.0,
                                          base=0, pattern=[[1, P]], channel_multiplier=-1))
            order.mark(pool.memset(seg[:, :, 0:1], 0.0))
            order.mark(pool.tensor_copy(parts[:, :, :, 0], ints.rearrange("p (t e) -> p e t", e=E)))
            order.mark(pool.tensor_copy(parts[:, :, :, 1], ints2.rearrange("p (e t) -> p e t", e=E)))
            order.mark(pool.tensor_copy(iota_p[:, :], posi.rearrange("p e t -> p (e t)")[:, 0:P]))
            order.mark(pool.tensor_copy(iota_j[:, :], posi.rearrange("p e t -> p (e t)")[:, 0:SLOTS]))
            order.settled()
            pool.sem_inc(consts_ready, 1)
            pool.sem_inc(w_lo, RING)

            def split_low(e, c):
                pool.wait_ge(w_hi, e * FC + c + 1)
                pool.tensor_tensor(wl[:, c, :], raw[:, c % RING, :], wh[:, c, :].bitcast(F32),
                                   ALU.subtract).then_inc(w_lo, 1)

            def gather(e, tb, q):
                n = tile_count(e, tb, q)
                waits(pool, (consts_ready, 1), (idx_ready, e + 1), (tok_full, n + 1))
                pool.indirect_dma_start(gath[:, q % 2, :], None, xn2_d[:, :],
                                        bass.IndirectOffsetOnAxis(ap=idx_g[:, tb * TT + q:tb * TT + q + 1], axis=0))\
                    .then_inc(s_gath[q % 2], 16)

            def scatter(e, tb):
                for t in range(TT):
                    waits(pool, (consts_ready, 1), (y_scaled, tile_count(e, tb, t) + 1),
                          *((s_scat[k], e * (16 * BLOCKS)) for k in range(TT) if tb == 0 and t == 0))
                    pool.indirect_dma_start(outr[:, :], bass.IndirectOffsetOnAxis(
                        ap=idx_s[:, tb * TT + t:tb * TT + t + 1], axis=0), yb[:, t, :], None,
                        compute_op=ALU.add).then_inc(s_scat[t], 16)

            def expert(e, last):
                split_low(e, EARLY)
                split_low(e, EARLY + 1)
                gather(e, 1, 0)
                gather(e, 1, 1)
                gather(e, 1, 2)
                gather(e, 1, 3)
                scatter(e, 0)
                if not last:
                    gather(e + 1, 0, 0)
                    gather(e + 1, 0, 1)
                    for c in range(EARLY):
                        split_low(e + 1, c)
                        if c == 4:
                            gather(e + 1, 0, 2)
                        if c == 6:
                            gather(e + 1, 0, 3)
                scatter(e, 1)

            for c in range(EARLY):
                split_low(0, c)
            for q in range(TT):
                gather(0, 0, q)
            with pool.Fori(0, E - 1) as e:
                expert(e, False)
            expert(E - 1, True)

        @block.scalar
        def _(act):
            def split_high(e, c, lead):
                times = e * (FC // RING) + c // RING + 1
                waits(act, (tanh_done, 1), (s_raw[c % RING], times * 32), (down_done, lead))
                act.activation(wh[:, c, :], raw[:, c % RING, :], ACT.Copy).then_inc(w_hi, 1)

            def relu(e, s):
                waits(act, (tanh_done, 1), (up_done, e * STEPS + s + 1))
                act.activation(hf[:, s % 2, :], p1[:, s % 2, :], ACT.Relu,
                               bias=b1t[:, bass.ds(e * FC + s % FC, 1)]).then_inc(relu_done, 1)

            def tokens_high(e, tb, q):
                act.wait_ge(tok_full, tile_count(e, tb, q) + 2 + 1)
                act.activation(xh[:, tb, :, q * P:(q + 1) * P], ptr[:, :].rearrange("p (c n) -> p c n", c=DC),
                               ACT.Copy).then_inc(tok_hi, 1)

            def scale(e, tb):
                for t in range(TT):
                    act.wait_ge(y_free, tile_count(e, tb, t) + TT + 1)
                    act.activation(yb[:, t, :], yb[:, t, :], ACT.Copy,
                                   scale=gate_s[:, tb * TT + t:tb * TT + t + 1]).then_inc(y_scaled, 1)

            def expert(e, last):
                for s in range(STEPS):
                    if s < STEPS - 1:
                        relu(e, s + 1)
                    elif not last:
                        relu(e + 1, 0)
                    if s < 2:
                        split_high(e, EARLY + s, lead=e * STEPS)
                    for tb, tiles in TILE_AT.items():
                        if s in tiles and (tb == 1 or not last):
                            tokens_high(e + (tb == 0), tb, tiles.index(s))
                    if s >= FC + 2 and not last:
                        c = s - FC - 2
                        split_high(e + 1, c, lead=e * STEPS + FC + c + 1)
                    if s % FC == FC - 1:
                        scale(e, s // FC)

            act.wait_ge(s_small, 32)
            act.activation(tg[:, :], gate[:, :], ACT.Tanh).then_inc(tanh_done, 1)
            act.wait_ge(b1_full, 1)
            act.activation(b1t[:, :], pc[:, 0:E * FC], ACT.Copy).then_inc(b1_done, 1)
            act.wait_ge(shifted, 1)
            act.activation(ex_te, scores_te, ACT.Exp).then_inc(exp_done, 1)
            for c in range(EARLY):
                split_high(0, c, lead=0)
            for q in range(TT):
                tokens_high(0, 0, q)
            relu(0, 0)
            with act.Fori(0, E - 1) as e:
                expert(e, False)
            expert(E - 1, True)

        @block.vector
        def _(dve):
            order = Order(dve, dve_order)

            def link(instruction):
                order.mark(instruction)
                order.settled()

            def per_expert(v):
                return v.unsqueeze(2).broadcast_to([P, E, NT])

            link(dve.tensor_reduce(lmax, logits[:, :, :], AX.X, ALU.max))
            dve.tensor_tensor(scores_te, logits[:, :, :], lmax.unsqueeze(2).broadcast_to([P, NT, E]),
                              ALU.subtract).then_inc(shifted, 1)
            dve.wait_ge(exp_done, 1)
            link(dve.tensor_reduce(lsum, ex_te, AX.X, ALU.add))
            link(dve.reciprocal(lsum, lsum))
            link(dve.tensor_tensor(scores.rearrange("p e t -> p t e"), ex_te,
                                   lsum.unsqueeze(2).broadcast_to([P, NT, E]), ALU.mult))
            dve.wait_ge(consts_ready, 1)
            link(dve.tensor_copy(parts[:, :, :, 2], scores))
            link(dve.tensor_tensor(rest, scores, parts[:, :, :, 2], ALU.subtract))
            link(dve.tensor_copy(parts[:, :, :, 3], rest))
            link(dve.tensor_tensor(ex, rest, parts[:, :, :, 3], ALU.subtract))
            link(dve.tensor_copy(parts[:, :, :, 4], ex))
            order.mark(dve.memset(thr[:, :], 0))
            link(dve.memset(bit[:, :], 1 << (SCORE_BITS - 1)))
            start = order.base
            with dve.Fori(0, SCORE_BITS) as i:
                order.base = i * 5 + start
                link(dve.tensor_tensor(cand[:, :], thr[:, :], bit[:, :], ALU.bitwise_or))
                dve.tensor_tensor(mask[:, 0], scores, per_expert(cand[:, :].bitcast(F32)),
                                  ALU.is_ge).then_inc(mask_ready, 1)
                dve.wait_ge(counted, i + 1)
                link(dve.tensor_reduce(cnt[:, :], pc[:, 0:E * NT].rearrange("p (e t) -> p e t", t=NT), AX.X, ALU.add))
                link(dve.scalar_tensor_tensor(take[:, :], cnt[:, :], float(TOPK), bit[:, :], ALU.is_ge, ALU.mult))
                order.mark(dve.tensor_single_scalar(bit[:, :], bit[:, :], 1, ALU.logical_shift_right))
                link(dve.tensor_tensor(thr[:, :], thr[:, :], take[:, :], ALU.bitwise_or))
            order.base = start + 5 * SCORE_BITS
            thr_f = per_expert(thr[:, :].bitcast(F32))
            dve.tensor_tensor(mask[:, 0], scores, thr_f, ALU.is_gt).then_inc(mask_ready, 1)
            dve.tensor_tensor(mask[:, 1], scores, thr_f, ALU.is_equal).then_inc(mask_ready, 1)
            dve.wait_ge(counted, SCORE_BITS + 2)
            totals = pc[:, :].rearrange("p (m e t) -> p m e t", m=2, e=E)
            within = ptr[:, 0:E * NT].rearrange("p (e t) -> p e t", e=E)

            def flat(v):
                return v.rearrange("p e t -> p (e t)")

            def places(total):
                link(dve.tensor_tensor_scan(flat(incl), flat(seg), flat(total), 0.0, ALU.mult, ALU.add))
                link(dve.tensor_tensor(incl, incl, total, ALU.subtract))
                link(dve.tensor_tensor(place, incl, within, ALU.add))

            link(dve.tensor_reduce(cnt[:, :], totals[:, 0], AX.X, ALU.add))
            link(dve.tensor_scalar(cnt[:, :], cnt[:, :], -1.0, float(TOPK), ALU.mult, ALU.add))
            places(totals[:, 1])
            link(dve.tensor_tensor(place, place, per_expert(cnt[:, :]), ALU.is_lt))
            link(dve.tensor_tensor(place, place, mask[:, 1], ALU.mult))
            dve.tensor_tensor(mask[:, 0], mask[:, 0], place, ALU.add).then_inc(mask_ready, 1)
            dve.wait_ge(counted, SCORE_BITS + 3)
            places(totals[:, 0])
            link(dve.scalar_tensor_tensor(place, place, 1.0, mask[:, 0], ALU.add, ALU.mult))
            link(dve.tensor_scalar(posi, place, 1.0, None, ALU.subtract))
            link(dve.tensor_single_scalar(posi2, posi, 7, ALU.arith_shift_right))
            link(dve.tensor_copy(pos_j[:, :, :], posi2))
            link(dve.tensor_single_scalar(posi, posi, P - 1, ALU.bitwise_and))
            link(dve.tensor_copy(pos_p[:, :, :], posi))
            dve.sem_inc(y_free, TT)

            def carry(e):
                span = pos_j[:, :, :].rearrange("p e t -> p (e t)")[:, bass.ds(e * NT, NT)]
                dve.wait_ge(oh_used, e * 2)
                order.mark(dve.tensor_tensor(onehot_j[:, :, :], iota_j[:, :].unsqueeze(1).broadcast_to([P, NT, SLOTS]),
                                             span.unsqueeze(2).broadcast_to([P, NT, SLOTS]), ALU.is_equal))
                order.settled()
                own = parts[:, :, :, :].rearrange("p e t k -> p (e t) k")[:, bass.ds(e * NT, NT), :]
                dve.tensor_tensor(carried[:, :, :, :], onehot_j[:, :, :].unsqueeze(2).broadcast_to([P, NT, PARTS, SLOTS]),
                                  own.unsqueeze(3).broadcast_to([P, NT, PARTS, SLOTS]),
                                  ALU.mult).then_inc(carried_ready, 1)

            def one_hot(e, half):
                dve.wait_ge(oh_used, e * 2 + half)
                span = pos_p[:, :, :].rearrange("p e t -> p (e t)")[:, bass.ds(e * NT + half * (NT // 2), NT // 2)]
                dve.tensor_tensor(onehot_p[:, :, :], iota_p[:, :].unsqueeze(1).broadcast_to([P, NT // 2, P]),
                                   span.unsqueeze(2).broadcast_to([P, NT // 2, P]),
                                   ALU.is_equal).then_inc(oh_ready, 1)

            def lists(e):
                dve.wait_ge(oh_used, e * 2 + 2)
                order.mark(dve.tensor_copy(compact[:, :, :].rearrange("p k j -> p (k j)"), pc[:, 0:PARTS * SLOTS]))
                order.settled()
                order.mark(dve.tensor_tensor(gtmp[:, :], compact[:, 2, :], compact[:, 3, :], ALU.add))
                order.settled()
                order.mark(dve.tensor_tensor(gate_g[:, :], gtmp[:, :], compact[:, 4, :], ALU.add))
                dve.scalar_tensor_tensor(idx_g[:, :], compact[:, 0, :], float(P), compact[:, 1, :],
                                         ALU.mult, ALU.add).then_inc(idx_ready, 1)

            def hold(e):
                for k in range(TT):
                    dve.wait_ge(s_scat[k], e * (16 * BLOCKS))
                order.mark(dve.tensor_copy(idx_s[:, :], idx_g[:, :]))
                order.mark(dve.tensor_scalar(gate_s[:, :], gate_g[:, :], tg[:, 0:1], None, ALU.mult))
                order.settled()

            def split_hidden(e, s):
                dve.wait_ge(relu_done, e * STEPS + s + 1)
                if not (isinstance(e, int) and e * STEPS + s <= 1):
                    dve.wait_ge(down_done, e * STEPS + (s - 1))
                order.mark(dve.tensor_copy(hh[:, s % 2, :], hf[:, s % 2, :]))
                order.settled()
                dve.tensor_tensor(hl[:, s % 2, :], hf[:, s % 2, :], hh[:, s % 2, :].bitcast(F32),
                                  ALU.subtract).then_inc(lo_done, 1)

            def tokens_low(e, tb, q):
                dve.wait_ge(tok_hi, tile_count(e, tb, q) + 1)
                dve.tensor_tensor(xl[:, tb, :, q * P:(q + 1) * P], ptr[:, :].rearrange("p (c n) -> p c n", c=DC),
                                  xh[:, tb, :, q * P:(q + 1) * P].bitcast(F32), ALU.subtract).then_inc(tok_free, 1)

            def biased(e, tb):
                dve.wait_ge(s_b2, e * 16 + 16)
                for t in range(TT):
                    dve.wait_ge(s_scat[t], e * (16 * BLOCKS) + 16 * tb)
                    if t < TT - 1:
                        dve.wait_ge(y_full, (e * BLOCKS + tb) * (TT - 1) + t + 1)
                    else:
                        dve.wait_ge(down_done, e * STEPS + (tb + 1) * FC)
                    dve.tensor_tensor(yb[:, t, :], py[:, t, :], b2b[:, :], ALU.add).then_inc(y_free, 1)

            ORDERED = STEPS + 2 + 1 + 3
            carry(0)
            one_hot(0, 0)
            one_hot(0, 1)
            lists(0)
            for q in range(TT):
                tokens_low(0, 0, q)
            split_hidden(0, 0)

            def expert(e, last):
                for s in range(STEPS):
                    if s < STEPS - 1:
                        split_hidden(e, s + 1)
                    elif not last:
                        split_hidden(e + 1, 0)
                    for tb, tiles in TILE_AT.items():
                        if s in tiles and (tb == 1 or not last):
                            tokens_low(e + (tb == 0), tb, tiles.index(s))
                    if s == HALF_AT[0] - 1 and not last:
                        carry(e + 1)
                        one_hot(e + 1, 0)
                    if s == HALF_AT[1] - 2 and not last:
                        one_hot(e + 1, 1)
                    if s == HALF_AT[1] - 1:
                        hold(e)
                    if s == HALF_AT[1] and not last:
                        lists(e + 1)
                    if s % FC == FC - 1:
                        biased(e, s // FC)

            start = order.base
            with dve.Fori(0, E - 1) as e:
                order.base = e * ORDERED + start
                expert(e, False)
            order.base = start + ORDERED * (E - 1)
            expert(E - 1, True)

        @block.tensor
        def _(pe):
            pe.wait_ge(s_small, 32)
            pe.transpose(pc[:, 0:E * FC], b1_rows, ident[:, :]).then_inc(b1_full, 1)
            pe.wait_ge(b1_done, 1)
            flat_mask = mask.rearrange("p m e t -> p (m e t)")
            with pe.Fori(0, SCORE_BITS) as i:
                pe.wait_ge(mask_ready, i + 1)
                pe.matmul(pc[:, 0:E * NT], ones[:, :], flat_mask[:, 0:E * NT], start=True, stop=True).then_inc(counted, 1)
            pe.wait_ge(mask_ready, SCORE_BITS + 2)
            pe.matmul(pc[:, :], ones[:, :], flat_mask, start=True, stop=True).then_inc(counted, 1)
            pe.matmul(ptr[:, 0:E * NT], before[:, :], flat_mask[:, E * NT:2 * E * NT], start=True, stop=True).then_inc(counted, 1)
            pe.wait_ge(mask_ready, SCORE_BITS + 3)
            pe.matmul(pc[:, 0:E * NT], ones[:, :], flat_mask[:, 0:E * NT], start=True, stop=True)
            pe.matmul(ptr[:, 0:E * NT], before[:, :], flat_mask[:, 0:E * NT], start=True, stop=True).then_inc(counted, 1)
            pe.sem_inc(tok_full, 2)

            def compaction(e, half):
                pe.wait_ge(oh_ready, e * 2 + half + 1)
                if half == 0:
                    pe.wait_ge(carried_ready, e + 1)
                for t in range(NT // 2):
                    tile = half * (NT // 2) + t
                    done = pe.matmul(pc[:, 0:PARTS * SLOTS], onehot_p[:, t, :],
                                     carried[:, tile, :, :].rearrange("p k j -> p (k j)"),
                                     start=tile == 0, stop=tile == NT - 1)
                done.then_inc(oh_used, 1)

            def transposed(e, tb, q):
                n = tile_count(e, tb, q)
                pe.wait_ge(s_gath[q % 2], (e * (BLOCKS * TT // 2) + (tb * TT + q) // 2 + 1) * 16)
                pe.wait_ge(tok_free, n)
                for c in range(DC):
                    done = pe.transpose(ptr[:, c * P:(c + 1) * P], gath[:, q % 2, c * P:(c + 1) * P], ident[:, :])
                done.then_inc(tok_full, 1)

            def up(e, s):
                tb, c = divmod(s, FC)
                if tb == 0:
                    pe.wait_ge(w_lo, e * FC + c + 1 + RING)
                if c == 0:
                    pe.wait_ge(tok_free, tile_count(e, tb, TT))
                for k in range(DC):
                    cols = slice(k * P, (k + 1) * P)
                    pe.matmul(p1[:, s % 2, :], wh[:, c, cols], xh[:, tb, k, :], start=k == 0, stop=False)
                    pe.matmul(p1[:, s % 2, :], wh[:, c, cols], xl[:, tb, k, :], start=False, stop=False)
                    done = pe.matmul(p1[:, s % 2, :], wl[:, c, cols], xh[:, tb, k, :], start=False, stop=k == DC - 1)
                done.then_inc(up_done, 1)

            def down(e, s):
                tb, c = divmod(s, FC)
                pe.wait_ge(lo_done, e * STEPS + s + 1)
                for t in range(TT):
                    if c == 0:
                        pe.wait_ge(y_free, tile_count(e, tb, t) + 1)
                    tok = slice(t * P, (t + 1) * P)
                    pe.matmul(py[:, t, :], hh[:, s % 2, tok], wh[:, c, D:2 * D], start=c == 0, stop=False)
                    pe.matmul(py[:, t, :], hh[:, s % 2, tok], wl[:, c, D:2 * D], start=False, stop=False)
                    done = pe.matmul(py[:, t, :], hl[:, s % 2, tok], wh[:, c, D:2 * D], start=False, stop=c == FC - 1)
                    if c == FC - 1 and t < TT - 1:
                        done.then_inc(y_full, 1)
                done.then_inc(down_done, 1)

            def expert(e, last):
                for s in range(STEPS):
                    if s < STEPS - 1:
                        up(e, s + 1)
                    elif not last:
                        up(e + 1, 0)
                    for tb, tiles in TILE_AT.items():
                        if s in tiles and (tb == 1 or not last):
                            transposed(e + (tb == 0), tb, tiles.index(s))
                    if s in HALF_AT and not last:
                        compaction(e + 1, HALF_AT.index(s))
                    down(e, s)

            compaction(0, 0)
            compaction(0, 1)
            for q in range(TT):
                transposed(0, 0, q)
            up(0, 0)
            with pe.Fori(0, E - 1) as e:
                expert(e, False)
            expert(E - 1, True)


def build(nc, io):
    with ExitStack() as ctx:
        keep = {"ident": ctx.enter_context(nc.sbuf_tensor("identity", [P, P], F32)),
                "logits": ctx.enter_context(nc.sbuf_tensor("router_logits", [P, NT, E], F32))}
        io["xn2_d"] = nc.dram_tensor("normed_rows", [B * S, D], F32).ap()
        attention_block(nc, io, keep)
        experts_block(nc, io, keep)


_INS = {"x": "x", "ctx": "ctx_1024", "g_attn": "g_xattn", "g_ffn": "g_ffn", "wkv": "L0_xattn_W_kv",
        "bkv": "L0_xattn_b_kv", "wo": "L0_xattn_W_o", "bo": "L0_xattn_b_o", "rw": "L0_ffn_router_w",
        "rb": "L0_ffn_router_b", "w1": "L0_ffn_w1", "b1": "L0_ffn_b1", "w2": "L0_ffn_w2", "b2": "L0_ffn_b2"}


def kernel(**inputs):
    import numpy as np
    import concourse.bacc as bacc
    from concourse.bass_utils import run_bass_kernel_spmd

    nc = bacc.Bacc("TRN2", target_bir_lowering=False, num_devices=1)
    arrays, io = {}, {}
    for short, name in _INS.items():
        a = np.ascontiguousarray(inputs[name])
        arrays[f"in_{short}"] = a
        io[short] = nc.dram_tensor(f"in_{short}", a.shape, mybir.dt.from_np(a.dtype), kind="ExternalInput").ap()
    io["out"] = nc.dram_tensor("out_rows", (B, S, D), F32, kind="ExternalOutput").ap()
    build(nc, io)
    r = run_bass_kernel_spmd(nc, [arrays], core_ids=[0])
    return r.results[0]["out_rows"]
```

```python
import concourse.bass as bass
from concourse import mybir
from contextlib import ExitStack
from itertools import islice

F32 = mybir.dt.float32
F32R = mybir.dt.float32r
BF16 = mybir.dt.bfloat16
I32 = mybir.dt.int32
U32 = mybir.dt.uint32
ALU = mybir.AluOpType
ACT = mybir.ActivationFunctionType
AX = mybir.AxisListType

P = 128
B, S, D = 2, 2048, 512
KV = 154
H, DH = 16, 32
E, F, TOPK = 8, 2048, 1024
EPS = 1e-5
SCALE = DH ** -0.5

DC = D // P
HC = P // DH
KR = KV - P
MR = 32 + H
VW = DH + 1
TB = 512
TT = TB // P
BLKS = B * S // TB
NT = B * S // P
FC = F // P
BLOCKS = TOPK // TB
SLOTS = TOPK // P
RING = 2
STEPS = BLOCKS * FC
SCORE_BITS = 30
PARTS = 5


class Order:

    def __init__(self, engine, sem):
        self.engine, self.sem, self.base = engine, sem, 0

    def mark(self, instruction):
        instruction.then_inc(self.sem, 1)
        self.base = self.base + 1

    def settled(self):
        self.engine.wait_ge(self.sem, self.base)

    def settled_before(self, met, value):
        self.engine.compute_val(self.base)
        self.engine.wait_ge(met, value)
        self.engine.wait_ge(self.sem, self.base)


def attention_block(nc, io, keep):
    with ExitStack() as ctx:
        def sb(name, shape, dt=F32):
            return ctx.enter_context(nc.sbuf_tensor(name, shape, dt))

        def ps(name, shape):
            return ctx.enter_context(nc.psum_tensor(name, shape, F32))

        def sem(name):
            return ctx.enter_context(nc.semaphore(name))

        ident, logits = keep["ident"], keep["logits"]
        xin = sb("x_in", [P, TT, D])
        x = sb("x_block", [P, B, TT, D])
        xn = sb("x_normed", [P, TT, D])
        xn2 = sb("x_normed2", [P, TT, D])
        qh = sb("q_hi", [P, B, DC, TB], F32R)
        ql = sb("q_lo", [P, B, DC, TB], F32R)
        pt = sb("probs", [P, 2, HC + 1, TB])
        val = sb("values", [P, TT, D])
        vh = sb("values_hi", [P, DC, TB], F32R)
        vl = sb("values_lo", [P, DC, TB], F32R)
        woh = sb("wo_hi", [P, DC, D], F32R)
        wol = sb("wo_lo", [P, DC, D], F32R)
        kh = sb("k_hi", [P, B, DC, HC, KV], F32R)
        kl = sb("k_lo", [P, B, DC, HC, P], F32R)
        khr = sb("k_rest_hi", [P, B, DC, HC, DH], F32R)
        klr = sb("k_rest_lo", [P, B, DC, HC, DH], F32R)
        vm = sb("v_main", [P, B, H, VW])
        vr = sb("v_rest", [P, B, DC, HC, VW])
        selm = sb("minus_head", [P, H, P], F32R)
        selr = sb("minus_head_rest", [P, DC, HC, DH], F32R)
        mst = sb("max_staged", [P, TT, MR], F32R)
        mt = sb("max_T", [P, B, TB], F32R)
        x2t = sb("x2_T", [P, 2, DC, P])
        tgbo = sb("gated_b_o", [P, D])
        bk = sb("b_k", [P, DC])
        rw = sb("router_w", [P, DC, E])
        rbb = sb("router_b", [P, E])
        gate = sb("attn_gate", [P, 1])
        tg = sb("attn_tanh", [P, 1])
        neghalf = sb("neg_half", [P, TT])
        eps = sb("eps", [P, TT])
        stats = sb("bn_stats", [P, 2, TT, 6])
        mv = sb("mean_var", [P, 2, TT, 2])
        ve = sb("var_eps", [P, 2, TT])
        rstd = sb("rstd", [P, 2, TT])
        mx = sb("max_logit", [P, TT, H])
        rc = sb("recip_sum", [P, 2, 2, HC])
        wkv = pt[:, :, :, :].rearrange("p a b n -> p (a b n)")[:, 0:DC * 2 * D].rearrange(
            "p (k z n) -> p k z n", k=DC, z=2)
        ct = x[:, 1, :, :].rearrange("p (b k) n -> p b (k n)", b=B).rearrange(
            "p b (k n) -> p b k n", n=2 * P)
        bvb = x[:, 0, 0, :].rearrange("p (h d) -> p h d", d=DH)
        cx = val[:, :, :].rearrange("p (b z) d -> p b z d", b=B)
        wo_raw = xn
        sel_raw = xn2[:, :, :].rearrange("p t (u n) -> p (t u) n", n=P)
        selr_raw = x2t[:, 0, :, :].rearrange("p c (j r) -> p c j r", j=HC)

        pb = ps("p_max", [P, 2, 512])
        pl = ps("p_logits", [P, 2, 512])
        po = ps("p_values", [P, 2, 512])
        ptr = ps("p_transposed", [P, 512])
        pw = ps("p_out", [P, 512])
        po_t = po[:, :, 0:2 * HC * VW].rearrange("p u (t j w) -> p u t j w", t=2, j=HC)
        router_out = pw[:, 0:TT * E]

        s_ctx, s_wkv, s_wo, s_small = sem("ctx_in"), sem("wkv_in"), sem("wo_in"), sem("small_in")
        s_x = sem("x_loaded")
        s_x1st = [sem(f"x1_stored{b}") for b in range(B)]
        s_xn2st = sem("xn2_stored")
        pool_order, dve_order = sem("pool_order"), sem("dve_order")
        consts_ready, sel_ready, sel_split = sem("consts_ready"), sem("sel_ready"), sem("sel_split")
        pre_pe, pre_act, pre_dve = sem("prologue_pe"), sem("prologue_act"), sem("prologue_dve")
        wo_hi_done, tanh_done, bo_done = sem("wo_hi_done"), sem("tanh_done"), sem("bo_done")
        mv1_ready, mv2_ready = sem("mv1_ready"), sem("mv2_ready")
        rstd1_ready, rstd2_ready = sem("rstd1_ready"), sem("rstd2_ready")
        xn_ready, xb_ready, xn2_ready = sem("xn_ready"), sem("xb_ready"), sem("xn2_ready")
        q_full, q_hi, q_free = sem("queries_T_full"), sem("queries_hi_done"), sem("queries_T_free")
        v_full, v_hi, v_free = sem("values_T_full"), sem("values_hi_done"), sem("values_T_free")
        x_full, x_free = sem("normed_T_full"), sem("normed_T_free")
        b_full, b_free = sem("max_logits_full"), sem("max_logits_free")
        m_ready, m_full, mt_ready = sem("max_staged_ready"), sem("max_T_full"), sem("max_T_ready")
        l_full, l_free = sem("logits_full"), sem("logits_free")
        o_full, o_free = sem("values_full"), sem("values_free")
        w_full, w_free = sem("out_full"), sem("out_free")
        r_full, r_free = sem("router_full"), sem("router_free")
        NL = HC + 1
        BU = TT * DC * 2

        xr = io["x"].rearrange("b s d -> (b s) d")
        outr = io["out"].rearrange("b s d -> (b s) d")
        xn2_d = io["xn2_d"]
        block = ctx.enter_context(nc.Block())

        def rows(dram, j, b):
            return dram[bass.ds(j * TB + b * S, TB), :].rearrange("(t p) d -> p t d", p=P)

        def steps(i):
            return [(i * B + 1 + k, i + (1 + k) // B, (1 + k) % B) for k in range(B)]

        TURNS = (BLKS - 2) // B
        MAX_OUT_TILES = 2
        queries_T = (ptr, pb[:, 0], pb[:, 1], ptr)
        out_tile = (pw, po[:, 0], po[:, 1], pw)

        @block.sync
        def _(sp):
            for b in range(B):
                sp.dma_start(cx[:, b, 0, :], io["ctx"][b, 0:P, :]).then_inc(s_ctx, 16)
                sp.dma_start(cx[0:KR, b, 1, :], io["ctx"][b, P:KV, :]).then_inc(s_ctx, 16)
            wkv_dram = io["wkv"].rearrange("(k p) (h z d) -> p k z h d", p=P, z=2, d=DH)
            for k in range(DC):
                for z in range(2):
                    sp.dma_start(wkv[:, k, z, :].rearrange("p (h d) -> p h d", d=DH),
                                 wkv_dram[:, k, z, :, :]).then_inc(s_wkv, 16)
            with nc.allow_non_contiguous_dma(reason="512 biases, once"):
                for j in range(HC):
                    bkj = io["bkv"].rearrange("(c j z d) -> j z d c", j=HC, z=2, d=DH)
                    sp.dma_start(bk[j * DH:(j + 1) * DH, :], bkj[j, 0]).then_inc(s_small, 16)
                bv = io["bkv"].rearrange("(o h z d) -> o h z d", o=1, z=2, d=DH)[:, :, 1, :]
                sp.dma_start(bvb[:, :, :], bv.broadcast_to([P, H, DH])).then_inc(s_small, 16)
                sp.dma_start(rbb[:, :], io["rb"].rearrange("(o n) -> o n", o=1).broadcast_to([P, E])).then_inc(s_small, 16)
                sp.dma_start(tgbo[:, :], io["bo"].rearrange("(o n) -> o n", o=1).broadcast_to([P, D])).then_inc(s_small, 16)
                sp.dma_start(gate[:, :], io["g_attn"].rearrange("(o n) -> o n", o=1).broadcast_to([P, 1])).then_inc(s_small, 16)
            sp.dma_start(rw[:, :, :], io["rw"].rearrange("(k p) n -> p k n", p=P)).then_inc(s_small, 16)
            sp.dma_start(wo_raw[:, :, :], io["wo"].rearrange("(k p) n -> p k n", p=P)).then_inc(s_wo, 16)
            sp.dma_start(xin[:, :, :], rows(xr, 0, 0)).then_inc(s_x, 16)
            sp.wait_ge(xb_ready, 1)
            sp.dma_start(xin[:, :, :], rows(xr, 0, 1)).then_inc(s_x, 16)
            sp.wait_ge(xb_ready, 2)
            sp.dma_start(xin[:, :, :], rows(xr, 1, 0)).then_inc(s_x, 16)

            def store(g, j, b):
                waits(sp, (s_ctx, 16 * 2 * B), (w_free, (g + 1) * TT))
                sp.dma_start(rows(outr, j, b), x[:, b, :, :]).then_inc(s_x1st[b], 16)
                waits(sp, (s_ctx, 16 * 2 * B), (xn2_ready, (g + 1) * TT))
                sp.dma_start(rows(xn2_d, j, b), xn2[:, :, :]).then_inc(s_xn2st, 16)

            def turn(i, last):
                for g, j, b in steps(i):
                    for v in (g * TT, g + 2, j * TB, (j * TB + b * S) * D):
                        sp.compute_val(v)
                for g, j, b in steps(i):
                    before = (g - 1, j + b - 1, 1 - b)
                    store(*before)
                    if last and b == 0:
                        continue
                    waits(sp, (s_ctx, 16 * 2 * B), (xb_ready, g + 2))
                    sp.dma_start(xin[:, :, :], rows(xr, j + 1, b)).then_inc(s_x, 16)

            with sp.Fori(0, TURNS - 1) as i:
                turn(i, False)
            turn(TURNS - 1, True)
            store(BLKS - 2, BLKS // B - 1, 0)
            store(BLKS - 1, BLKS // B - 1, 1)
            for b in range(B):
                sp.wait_ge(s_x1st[b], 16 * (BLKS // B))
            sp.wait_ge(s_xn2st, 16 * BLKS)

        @block.gpsimd
        def _(pool):
            order = Order(pool, pool_order)
            order.mark(pool.memset(ident[:, :], 0.0))
            order.mark(pool.memset(sel_raw, 0.0))
            order.mark(pool.memset(selr_raw, 0.0))
            order.settled()
            pool.affine_select(out=ident[:, :], in_=ident[:, :], compare_op=ALU.not_equal, fill=1.0, base=0,
                               pattern=[[-1, P]], channel_multiplier=1).then_inc(consts_ready, 1)
            for half in range(2):
                order.mark(pool.affine_select(out=sel_raw, in_=sel_raw, compare_op=ALU.not_equal, fill=-1.0,
                                              base=-32 * half, pattern=[[-1, H], [0, P]], channel_multiplier=1))
                order.mark(pool.affine_select(out=selr_raw, in_=selr_raw, compare_op=ALU.not_equal, fill=-1.0,
                                              base=-32 * half, pattern=[[-HC, DC], [-1, HC], [0, DH]],
                                              channel_multiplier=1))
                order.settled()
            order.mark(pool.memset(selr_raw[:, :, :, KR:DH], 0.0))
            order.settled()
            order.mark(pool.memset(eps[:, :], EPS))
            pool.memset(neghalf[:, :], -0.5).then_inc(sel_ready, 1)

            def inverse_deviation(g, ln, mv_ready, rstd_ready):
                pool.wait_ge(mv_ready, g + 1)
                order.mark(pool.tensor_tensor(ve[:, ln, :], mv[:, ln, :, 1], eps[:, :], ALU.add))
                order.settled()
                pool.tensor_tensor(rstd[:, ln, :], ve[:, ln, :], neghalf[:, :], ALU.pow).then_inc(rstd_ready, 1)

            def front(g, j, b):
                inverse_deviation(g, 0, mv1_ready, rstd1_ready)
                pool.wait_ge(xn_ready, (g + 1) * TT)
                if j is not None:
                    pool.wait_ge(s_x1st[b], j * 16)
                    pool.wait_ge(xn2_ready, (g - 1) * TT)
                pool.tensor_tensor(x[:, b, :, :], xin[:, :, :],
                                   tgbo[:, :].unsqueeze(1).broadcast_to([P, TT, D]), ALU.add).then_inc(xb_ready, 1)

            pool.wait_ge(bo_done, 1)
            pool.wait_ge(pre_dve, 2 + 3 * B)
            front(0, None, 0)
            front(1, None, 1)
            inverse_deviation(0, 1, mv2_ready, rstd2_ready)
            start = order.base
            with pool.Fori(0, TURNS) as i:
                order.base = i * (2 * B) + start
                for g, j, b in steps(i):
                    front(g + 1, j + b, 1 - b)
                    inverse_deviation(g, 1, mv2_ready, rstd2_ready)
            order.base = start + TURNS * 2 * B
            inverse_deviation(BLKS - 1, 1, mv2_ready, rstd2_ready)

        @block.scalar
        def _(act):
            act.wait_ge(s_small, 16 * 9)
            act.activation(tg[:, :], gate[:, :], ACT.Tanh).then_inc(tanh_done, 1)
            act.wait_ge(sel_ready, 1)
            act.activation(selm[:, :, :], sel_raw, ACT.Copy).then_inc(sel_split, 1)
            act.activation(selr[:, :, :, :], selr_raw, ACT.Copy).then_inc(sel_split, 1)
            act.wait_ge(s_wo, 16)
            act.activation(woh[:, :, :], wo_raw[:, :, :], ACT.Copy).then_inc(wo_hi_done, 1)
            act.wait_ge(pre_dve, 1)
            for b in range(B):
                act.wait_ge(pre_pe, 4 * b + 1)
                act.activation(ct[:, b, :, 0:P], pb[:, 0, :].rearrange("p (k n) -> p k n", k=DC), ACT.Copy)\
                   .then_inc(pre_act, 1)
                for j in range(HC):
                    act.activation(ct[:, b, :, P + j * DH:P + j * DH + KR],
                                   pb[:, 1, 0:DC * P].rearrange("p (k n) -> p k n", k=DC)[:, :, 0:KR], ACT.Copy)\
                       .then_inc(pre_act, 1)
                act.wait_ge(pre_pe, 4 * b + 2)
                for c in range(DC):
                    for j in range(HC):
                        hr = slice(j * DH, (j + 1) * DH)
                        act.activation(kh[hr, b, c, j, :], pl[hr, c // 2, (c % 2) * KV:(c % 2 + 1) * KV],
                                       ACT.Identity, bias=bk[hr, c:c + 1]).then_inc(pre_act, 1)
            act.sem_inc(l_free, 2)

            def weights(g, c, s):
                act.wait_ge(l_full, g * (DC * NL) + c * NL + s + 1)
                act.activation(pt[:, c % 2, s, :], pl[:, (c * NL + s) % 2, :], ACT.Exp, scale=SCALE).then_inc(l_free, 1)

            def queries_high(g, b, t):
                act.wait_ge(q_full, g * TT + t + 1)
                act.activation(qh[:, b, :, t * P:(t + 1) * P],
                               queries_T[t][:, :].rearrange("p (c n) -> p c n", c=DC), ACT.Copy).then_inc(q_hi, 1)

            def maxima(g, b):
                act.wait_ge(m_full, g + 1)
                act.activation(mt[0:MR, b, :], ptr[0:MR, :], ACT.Copy).then_inc(mt_ready, 1)

            def values_high(g, c):
                act.wait_ge(v_full, g * DC + c + 1)
                act.activation(vh[:, c, :], ptr[:, :], ACT.Copy).then_inc(v_hi, 1)

            def normed(g, t):
                act.wait_ge(x_full, g * TT + t + 1)
                act.activation(x2t[:, t % 2, :, :], ptr[:, :].rearrange("p (c n) -> p c n", c=DC),
                               ACT.Copy).then_inc(x_free, 1)

            def step(g, b, first=False, last=False):
                for c in range(DC):
                    for s in range(NL):
                        if c == 1 and s < TT and not first:
                            normed(g - 1, s)
                        if c == 2 and s < TT and not last:
                            queries_high(g + 1, 1 - b, s)
                        weights(g, c, s)
                    if c == 2:
                        values_high(g, 0)
                for c in range(1, DC):
                    values_high(g, c)
                if not last:
                    maxima(g + 1, 1 - b)

            for t in range(TT):
                queries_high(0, 0, t)
            maxima(0, 0)
            step(0, 0, first=True)
            with act.Fori(0, TURNS) as i:
                for g, j, b in steps(i):
                    step(g, b)
            step(BLKS - 1, 1, last=True)
            for t in range(TT):
                normed(BLKS - 1, t)

        @block.vector
        def _(dve):
            order = Order(dve, dve_order)
            dve.memset(kh[:, :, :, :, :].bitcast(F32), 0.0)
            dve.memset(kl[:, :, :, :, :].bitcast(F32), 0.0)
            dve.memset(khr[:, :, :, :, :].bitcast(F32), 0.0)
            dve.memset(klr[:, :, :, :, :].bitcast(F32), 0.0)
            dve.memset(vr[:, :, :, :, :], 0.0)
            dve.memset(vm[:, :, :, DH:VW], 1.0)
            dve.memset(mst[:, :, :].bitcast(F32), 0.0)
            order.mark(dve.memset(ct[:, :, :, P:2 * P], 0.0))
            order.settled()
            for j in range(HC):
                done = dve.memset(vr[j * DH:j * DH + KR, :, :, j, DH:VW], 1.0)
            done.then_inc(pre_dve, 1)
            dve.wait_ge(wo_hi_done, 1)
            dve.wait_ge(s_wo, 16)
            dve.tensor_tensor(wol[:, :, :], wo_raw[:, :, :], woh[:, :, :].bitcast(F32), ALU.subtract).then_inc(pre_dve, 1)
            dve.wait_ge(tanh_done, 1)
            dve.wait_ge(s_small, 16 * 9)
            dve.tensor_scalar(tgbo[:, :], tgbo[:, :], tg[:, 0:1], None, ALU.mult).then_inc(bo_done, 1)
            for b in range(B):
                act_base = b * (1 + HC + DC * HC) + 1 + HC
                dve.wait_ge(pre_act, act_base + DC * HC)
                for c in range(DC):
                    for j in range(HC):
                        hr = slice(j * DH, (j + 1) * DH)
                        at = (c % 2) * KV
                        dve.scalar_tensor_tensor(
                            kl[hr, b, c, j, :], pl[hr, c // 2, at:at + P], bk[hr, c:c + 1],
                            kh[hr, b, c, j, 0:P].bitcast(F32), ALU.add, ALU.subtract)
                        dve.tensor_copy(khr[hr, b, c, j, 0:KR], kh[hr, b, c, j, P:KV].bitcast(F32))
                        done = dve.scalar_tensor_tensor(
                            klr[hr, b, c, j, 0:KR], pl[hr, c // 2, at + P:at + KV], bk[hr, c:c + 1],
                            kh[hr, b, c, j, P:KV].bitcast(F32), ALU.add, ALU.subtract)
                done.then_inc(pre_dve, 1)
                dve.wait_ge(pre_pe, 4 * b + 3)
                dve.tensor_tensor(vm[:, b, :, 0:DH], po[:, 0, :].rearrange("p (h d) -> p h d", d=DH),
                                  bvb[:, :, :], ALU.add).then_inc(pre_dve, 1)
                dve.wait_ge(pre_pe, 4 * b + 4)
                for j in range(HC):
                    kr = slice(j * DH, j * DH + KR)
                    done = dve.tensor_tensor(
                        vr[kr, b, :, j, 0:DH], po[kr, 1, :].rearrange("p (c j d) -> p c j d", j=HC, d=DH)[:, :, j, :],
                        bvb[kr, :, :].rearrange("p (c j) d -> p c j d", j=HC)[:, :, j, :], ALU.add)
                done.then_inc(pre_dve, 1)
            dve.sem_inc(b_free, 2)
            dve.sem_inc(o_free, 2)

            def norm_queries(g):
                dve.wait_ge(s_x, g * 16 + 16)
                for t in range(TT):
                    order.mark(dve.bn_stats(stats[:, 0, t, :], xin[:, t, :]))
                order.settled_before(s_small, 16 * 9)
                for t in range(TT):
                    done = dve.bn_aggr(mv[:, 0, t, :], stats[:, 0, t, :])
                done.then_inc(mv1_ready, 1)
                dve.wait_ge(rstd1_ready, g + 1)
                for t in range(TT):
                    dve.tensor_scalar(xn[:, t, :], xin[:, t, :], mv[:, 0, t, 0:1], rstd[:, 0, t:t + 1],
                                      ALU.subtract, ALU.mult).then_inc(xn_ready, 1)

            def queries_low(g, b, t):
                dve.wait_ge(q_hi, g * TT + t + 1)
                dve.tensor_tensor(ql[:, b, :, t * P:(t + 1) * P], queries_T[t][:, :].rearrange("p (c n) -> p c n", c=DC),
                                  qh[:, b, :, t * P:(t + 1) * P].bitcast(F32), ALU.subtract).then_inc(q_free, 1)

            def maxima(g, ns):
                for n in ns:
                    h = n * 2 % H
                    dve.wait_ge(b_full, g * BU + n + 1)
                    dve.tensor_reduce(mx[:, n // (2 * DC), h:h + 2], pb[:, n % 2, 0:2 * KV].rearrange("p (j n) -> p j n", j=2),
                                      AX.X, ALU.max).then_inc(b_free, 1)

            def stage_maxima(g):
                dve.wait_ge(b_free, (g + 1) * BU + 2)
                order.mark(dve.tensor_copy(mst[:, :, 0:H], mx[:, :, :]))
                order.settled()
                dve.tensor_tensor(mst[:, :, 32:32 + H], mx[:, :, :], mst[:, :, 0:H].bitcast(F32),
                                  ALU.subtract).then_inc(m_ready, 1)

            def values(g, c, u):
                dve.wait_ge(o_full, g * (DC * 2) + c * 2 + u + 1)
                order.mark(dve.reciprocal(rc[:, u, :, :], po_t[:, u, :, :, DH]))
                order.settled()
                dve.tensor_tensor(
                    val[:, 2 * u:2 * u + 2, c * P:(c + 1) * P].rearrange("p t (j d) -> p t j d", d=DH),
                    po_t[:, u, :, :, 0:DH], rc[:, u, :, :].unsqueeze(3).broadcast_to([P, 2, HC, DH]),
                    ALU.mult).then_inc(o_free, 1)

            def values_low(g, c):
                dve.wait_ge(v_hi, g * DC + c + 1)
                dve.tensor_tensor(vl[:, c, :], ptr[:, :], vh[:, c, :].bitcast(F32), ALU.subtract).then_inc(v_free, 1)

            def residual(g, b, t):
                if t == 0:
                    dve.wait_ge(xb_ready, g + 1)
                dve.wait_ge(w_full, g * TT + t + 1)
                dve.scalar_tensor_tensor(x[:, b, t, :], out_tile[t][:, :], tg[:, 0:1], x[:, b, t, :],
                                         ALU.mult, ALU.add).then_inc(w_free, 1)

            def result_stats(g, b, t):
                dve.wait_ge(w_free, g * TT + t + 1)
                order.mark(dve.bn_stats(stats[:, 1, t, :], x[:, b, t, :]))

            def norm_result(g, b):
                dve.wait_ge(rstd2_ready, g + 1)
                if not (isinstance(g, int) and g == 0):
                    dve.wait_ge(s_xn2st, g * 16)
                for t in range(TT):
                    dve.tensor_scalar(xn2[:, t, :], x[:, b, t, :], mv[:, 1, t, 0:1], rstd[:, 1, t:t + 1],
                                      ALU.subtract, ALU.mult).then_inc(xn2_ready, 1)

            def router(g, j, b):
                dve.wait_ge(r_full, g + 1)
                order.mark(dve.tensor_tensor(logits[:, bass.ds(j * TT + b * (S // P), TT), :],
                                             router_out.rearrange("p (t e) -> p t e", e=E),
                                             rbb[:, :].unsqueeze(1).broadcast_to([P, TT, E]), ALU.add))
                order.settled()
                dve.sem_inc(r_free, 1)

            def step(g, j, b, first=False, last=False):
                n = iter(range(0, BU))
                nxt = g + 1

                def some(count):
                    if not last:
                        maxima(nxt, list(islice(n, count)))

                if not first:
                    norm_result(g - 1, 1 - b)
                if not last:
                    norm_queries(nxt)
                if not first:
                    router(g - 1, j + b - 1, 1 - b)
                values(g, 0, 0)
                values(g, 0, 1)
                if not last:
                    for t in range(TT):
                        queries_low(nxt, 1 - b, t)
                for c in range(1, DC):
                    for u in range(2):
                        some(2)
                        values(g, c, u)
                    values_low(g, c - 1)
                    some(2 * NL if c == 1 else 1)
                values_low(g, DC - 1)
                for t in range(TT):
                    if t < MAX_OUT_TILES:
                        some(DC)
                    if t == MAX_OUT_TILES and not last:
                        stage_maxima(nxt)
                    residual(g, b, t)
                    result_stats(g, b, t)
                order.settled_before(s_small, 16 * 9)
                for t in range(TT):
                    done = dve.bn_aggr(mv[:, 1, t, :], stats[:, 1, t, :])
                done.then_inc(mv2_ready, 1)

            norm_queries(0)
            for t in range(TT):
                queries_low(0, 0, t)
            maxima(0, range(BU))
            stage_maxima(0)
            step(0, 0, 0, first=True)
            start = order.base
            MARKS = B * (TT + 2 * DC + 1 + TT + 1)
            with dve.Fori(0, TURNS) as i:
                order.base = i * MARKS + start
                for g, j, b in steps(i):
                    step(g, j, b)
            order.base = start + TURNS * MARKS
            step(BLKS - 1, BLKS // B - 1, 1, last=True)
            norm_result(BLKS - 1, 1)
            router(BLKS - 1, BLKS // B - 1, 1)

        @block.tensor
        def _(pe):
            pe.wait_ge(consts_ready, 1)
            pe.wait_ge(s_ctx, 16 * 2 * B)
            pe.wait_ge(pre_dve, 1)
            for b in range(B):
                if b:
                    pe.wait_ge(pre_act, 1 + HC)
                for k in range(DC):
                    pe.transpose(pb[:, 0, k * P:(k + 1) * P], cx[:, b, 0, k * P:(k + 1) * P], ident[:, :])
                for k in range(DC):
                    done = pe.transpose(pb[:, 1, k * P:k * P + KR], cx[0:KR, b, 1, k * P:(k + 1) * P],
                                        ident[0:KR, 0:KR])
                done.then_inc(pre_pe, 1)
                pe.wait_ge(pre_act, b * (1 + HC + DC * HC) + 1 + HC)
                pe.wait_ge(s_wkv, 16 * 2 * DC)
                if b:
                    pe.wait_ge(pre_dve, 2 + 1)
                for c in range(DC):
                    for k in range(DC):
                        done = pe.matmul(pl[:, c // 2, (c % 2) * KV:(c % 2 + 1) * KV],
                                         wkv[:, k, 0, c * P:(c + 1) * P], ct[:, b, k, 0:KV],
                                         start=k == 0, stop=k == DC - 1)
                done.then_inc(pre_pe, 1)
                if b:
                    pe.wait_ge(pre_dve, 2 + 3)
                for z in range(2):
                    for k in range(DC):
                        done = pe.matmul(po[:, z, :], ct[:, b, k, z * P:(z + 1) * P], wkv[:, k, 1, :],
                                         start=k == 0, stop=k == DC - 1)
                    done.then_inc(pre_pe, 1)
            pe.wait_ge(pre_dve, 2 + 3 * B)
            pe.wait_ge(sel_split, 2)

            def logits_of(g, b, c, s, beside=lambda: None):
                n = c * NL + s
                pe.wait_ge(l_free, g * (DC * NL) + n + 1)
                if s < HC:
                    khs, kls, sel = kh[:, b, c, s, 0:P], kl[:, b, c, s, :], selm[0:MR, c * HC + s, :]
                else:
                    khs, kls, sel = (w.rearrange("p j r -> p (j r)") for w in (
                        khr[:, b, c, :, :], klr[:, b, c, :, :], selr[0:MR, c, :, :]))
                pe.matmul(pl[:, n % 2, :], khs, qh[:, b, c, :], start=True, stop=False)
                pe.matmul(pl[:, n % 2, :], khs, ql[:, b, c, :], start=False, stop=False)
                beside()
                pe.matmul(pl[:, n % 2, :], kls, qh[:, b, c, :], start=False, stop=False)
                pe.matmul(pl[:, n % 2, :], sel, mt[0:MR, b, :], start=False, stop=True).then_inc(l_full, 1)
                beside()

            def values_of(g, b, c, u, beside=lambda: None):
                pe.wait_ge(l_free, g * (DC * NL) + (c + 1) * NL + 2)
                pe.wait_ge(o_free, g * (DC * 2) + c * 2 + u + 1)
                for t2 in range(2):
                    tok = slice((2 * u + t2) * P, (2 * u + t2 + 1) * P)
                    base = t2 * HC * VW
                    for j in range(HC):
                        pe.matmul(po[:, u, base + j * VW:base + (j + 1) * VW],
                                  pt[:, c % 2, j, tok], vm[:, b, c * HC + j, :], start=j == 0, stop=False)
                        if j == 1:
                            beside()
                    done = pe.matmul(po[:, u, base:base + HC * VW], pt[:, c % 2, HC, tok],
                                     vr[:, b, c, :, :].rearrange("p j w -> p (j w)"), start=False, stop=True)
                done.then_inc(o_full, 1)

            def queries(g, t):
                pe.wait_ge(xn_ready, g * TT + t + 1)
                if t == TT - 1:
                    pe.wait_ge(q_free, g * TT + 1)
                for c in range(DC):
                    done = pe.transpose(queries_T[t][:, c * P:(c + 1) * P], xn[:, t, c * P:(c + 1) * P], ident[:, :])
                done.then_inc(q_full, 1)

            def max_logits(g, b, ns):
                for n in ns:
                    t, c, u = n // (2 * DC), n // 2 % DC, n % 2
                    if c == 0 and u == 0:
                        pe.wait_ge(q_hi, g * TT + t + 1)
                    pe.wait_ge(b_free, g * BU + n + 1)
                    pe.matmul(pb[:, u, 0:2 * KV], qh[:, b, c, t * P:(t + 1) * P],
                              kh[:, b, c, 2 * u:2 * u + 2, 0:KV], start=True, stop=True).then_inc(b_full, 1)

            def maxima(g):
                waits(pe, (consts_ready, 1), (m_ready, g + 1))
                for t in range(TT):
                    done = pe.transpose(ptr[0:MR, t * P:(t + 1) * P], mst[:, t, :].bitcast(F32), ident[:, :])
                done.then_inc(m_full, 1)

            def values_T(g, c):
                pe.wait_ge(o_free, g * (DC * 2) + c * 2 + 4)
                if c:
                    pe.wait_ge(v_free, g * DC + c)
                for t in range(TT):
                    done = pe.transpose(ptr[:, t * P:(t + 1) * P], val[:, t, c * P:(c + 1) * P], ident[:, :])
                done.then_inc(v_full, 1)

            def project(g, t, beside=lambda: None):
                if t == 0 and not (isinstance(g, int) and g == 0):
                    pe.wait_ge(r_free, g)
                if t == TT - 1:
                    pe.wait_ge(w_free, g * TT + 1)
                tok, out = slice(t * P, (t + 1) * P), out_tile[t]
                for c in range(DC):
                    if t == 0:
                        pe.wait_ge(v_free, g * DC + c + 1)
                    pe.matmul(out[:, :], vh[:, c, tok], woh[:, c, :], start=c == 0, stop=False)
                    pe.matmul(out[:, :], vh[:, c, tok], wol[:, c, :], start=False, stop=False)
                    beside()
                    done = pe.matmul(out[:, :], vl[:, c, tok], woh[:, c, :], start=False, stop=c == DC - 1)
                done.then_inc(w_full, 1)

            def normed(g, t):
                pe.wait_ge(xn2_ready, g * TT + t + 1)
                for c in range(DC):
                    done = pe.transpose(ptr[:, c * P:(c + 1) * P], xn2[:, t, c * P:(c + 1) * P], ident[:, :])
                done.then_inc(x_full, 1)

            def router(g, t):
                pe.wait_ge(x_free, g * TT + t + 1)
                if t == 0:
                    pe.wait_ge(w_free, (g + 1) * TT)
                for c in range(DC):
                    done = pe.matmul(router_out[:, t * E:(t + 1) * E], x2t[:, t % 2, c, :], rw[:, c, :],
                                     start=c == 0, stop=c == DC - 1)
                if t == TT - 1:
                    done.then_inc(r_full, 1)

            def step(g, b, first=False, last=False):
                n = iter(range(0, BU))
                nxt = g + 1

                def beside():
                    if not last:
                        max_logits(nxt, 1 - b, list(islice(n, 1)))

                pe.wait_ge(mt_ready, g + 1)
                for s in range(NL):
                    logits_of(g, b, 0, s)
                for s in range(NL):
                    if s < TT and not first:
                        normed(g - 1, s)
                    logits_of(g, b, 1, s)
                    if s < TT and not first:
                        router(g - 1, s)
                for u in range(2):
                    values_of(g, b, 0, u)
                for s in range(NL):
                    if s < TT and not last:
                        queries(nxt, s)
                    logits_of(g, b, 2, s)
                if not last:
                    pe.wait_ge(q_free, (nxt + 1) * TT)
                for c in range(1, DC):
                    for u in range(2):
                        values_of(g, b, c, u, beside)
                    values_T(g, c - 1)
                    if c > 1:
                        beside()
                    if c == 1:
                        for s in range(NL):
                            logits_of(g, b, 3, s, beside)
                values_T(g, DC - 1)
                for t in range(TT):
                    if t < MAX_OUT_TILES:
                        project(g, t, beside)
                    else:
                        project(g, t)
                    if t == MAX_OUT_TILES and not last:
                        maxima(nxt)

            for t in range(TT):
                queries(0, t)
            pe.wait_ge(q_free, TT)
            max_logits(0, 0, range(BU))
            maxima(0)
            step(0, 0, first=True)
            with pe.Fori(0, TURNS) as i:
                for g, j, b in steps(i):
                    step(g, b)
            step(BLKS - 1, 1, last=True)
            for t in range(TT):
                normed(BLKS - 1, t)
                router(BLKS - 1, t)


def waits(engine, met, *others):
    for _, value in others:
        engine.compute_val(value)
    engine.wait_ge(*met)
    for semaphore, value in others:
        engine.wait_ge(semaphore, value)


def experts_block(nc, io, keep):
    with ExitStack() as ctx:
        def sb(name, shape, dt=F32):
            return ctx.enter_context(nc.sbuf_tensor(name, shape, dt))

        def ps(name, shape):
            return ctx.enter_context(nc.psum_tensor(name, shape, F32))

        def sem(name):
            return ctx.enter_context(nc.semaphore(name))

        ident, logits = keep["ident"], keep["logits"]
        wh = sb("weights_hi", [P, FC, 2 * D], F32R)
        wl = sb("weights_lo", [P, FC, 2 * D], F32R)
        raw = sb("weights_raw", [P, RING, 2 * D])
        xh = sb("tokens_hi", [P, BLOCKS, DC, TB], F32R)
        xl = sb("tokens_lo", [P, BLOCKS, DC, TB], F32R)
        hf = sb("hidden", [P, 2, TB])
        hh = sb("hidden_hi", [P, 2, TB], F32R)
        hl = sb("hidden_lo", [P, 2, TB], F32R)
        gath = sb("gathered", [P, 2, D])
        yb = sb("results", [P, TT, D])
        b2b = sb("b2", [P, D])
        b1t = sb("b1_T", [P, E * FC])
        onehot_p = sb("onehot_p", [P, NT // 2, P], BF16)
        onehot_j = sb("onehot_j", [P, NT, SLOTS], BF16)
        carried = sb("carried", [P, NT, PARTS, SLOTS], BF16)
        parts = sb("parts", [P, E, NT, PARTS], BF16)
        pos_p = sb("pos_mod", [P, E, NT], BF16)
        pos_j = sb("pos_div", [P, E, NT], BF16)
        ones = sb("ones", [P, P], BF16)
        before = sb("before", [P, P], BF16)
        iota_p = sb("iota_p", [P, P], BF16)
        iota_j = sb("iota_j", [P, SLOTS], BF16)
        compact = sb("compact", [P, PARTS, SLOTS])
        idx_g = sb("index_gather", [P, SLOTS], I32)
        idx_s = sb("index_scatter", [P, SLOTS], I32)
        gate_g = sb("gate_next", [P, SLOTS])
        gate_s = sb("gate_now", [P, SLOTS])
        gtmp = sb("gate_sum", [P, SLOTS])
        gate = sb("ffn_gate", [P, 1])
        tg = sb("ffn_tanh", [P, 1])
        thr = sb("threshold_bits", [P, E], I32)
        bit = sb("bit", [P, E], I32)
        cand = sb("candidate", [P, E], I32)
        take = sb("taken_bit", [P, E], I32)
        cnt = sb("count", [P, E])
        mask = carried[:, :, :, :].rearrange("p t k j -> p (t k j)")[:, 0:2 * E * NT].rearrange(
            "p (m e t) -> p m e t", m=2, e=E)
        tmp = yb[:, :, :].rearrange("p t d -> p (t d)").rearrange("p (k e t) -> p k e t", e=E, t=NT)
        tmp2 = gath[:, :, :].rearrange("p s d -> p (s d)").rearrange("p (k e t) -> p k e t", e=E, t=NT)
        scores, ex, rest, incl = tmp[:, 0], tmp[:, 1], tmp[:, 2], tmp[:, 3]
        place, seg = tmp[:, 4], tmp[:, 5]
        posi, posi2 = tmp[:, 6].bitcast(I32), tmp[:, 7].bitcast(I32)
        b1_rows = tmp2[:, 0].rearrange("p e t -> p (e t)")[:, 0:P]
        lmax, lsum = tmp2[:, 1].rearrange("p e t -> p (e t)")[:, 0:NT], tmp2[:, 1].rearrange("p e t -> p (e t)")[:, NT:2 * NT]
        ints = tmp2[:, 2].rearrange("p e t -> p (e t)").bitcast(I32)
        ints2 = tmp2[:, 3].rearrange("p e t -> p (e t)").bitcast(I32)

        p1 = ps("p_hidden", [P, 2, 512])
        py = ps("p_results", [P, TT, 512])
        ptr = ps("p_tokens_T", [P, 512])
        pc = ps("p_counts", [P, 512])
        ex_te, scores_te = (v.rearrange("p e t -> p (e t)").rearrange("p (t e) -> p t e", e=E) for v in (ex, rest))

        s_small = sem("small_in2")
        s_raw = [sem(f"raw_in{k}") for k in range(RING)]
        s_b2 = sem("b2_in")
        s_gath = [sem(f"gathered{k}") for k in range(2)]
        s_scat = [sem(f"scattered{k}") for k in range(TT)]
        pool_order, dve_order = sem("pool_order2"), sem("dve_order2")
        consts_ready, b1_full, b1_done, tanh_done = sem("consts_ready2"), sem("b1_full"), sem("b1_done"), sem("tanh_done2")
        shifted, exp_done = sem("shifted"), sem("exp_done")
        mask_ready, counted = sem("mask_ready"), sem("counted")
        w_hi, w_lo = sem("weights_hi_done"), sem("weights_lo_done")
        oh_ready, oh_used = sem("onehot_ready"), sem("onehot_used")
        carried_ready, idx_ready = sem("carried_ready"), sem("index_ready")
        tok_full, tok_hi, tok_free = sem("tokens_full"), sem("tokens_hi_done"), sem("tokens_free")
        up_done, relu_done, lo_done, down_done = sem("up_done"), sem("relu_done"), sem("hidden_lo_done"), sem("down_done")
        y_full, y_free, y_scaled = sem("results_full"), sem("results_free"), sem("results_scaled")

        outr = io["out"].rearrange("b s d -> (b s) d")
        xn2_d = io["xn2_d"]
        block = ctx.enter_context(nc.Block())

        TILE_AT = {1: (4, 6, 8, 10), 0: (FC + 5, FC + 7, FC + 9, FC + 11)}
        HALF_AT = (FC - 7, FC - 3)
        EARLY = FC - 2

        def tile_count(e, tb, q):
            return e * (BLOCKS * TT) + tb * TT + q

        @block.sync
        def _(sp):
            sp.dma_start(b1_rows, io["b1"].rearrange("e (c p) -> (e c) p", p=P)).then_inc(s_small, 16)
            with nc.allow_non_contiguous_dma(reason="one gate"):
                sp.dma_start(gate[:, :], io["g_ffn"].rearrange("(o n) -> o n", o=1).broadcast_to([P, 1])).then_inc(s_small, 16)

            w1r = io["w1"].rearrange("e d f -> (e d) f")
            w2r = io["w2"].rearrange("e f d -> (e f) d")

            def load(e, c):
                waits(sp, (s_small, 32), (w_lo, e * FC + c + 1))
                slot = c % RING
                sp.dma_start(raw[:, slot, 0:D].rearrange("p (k f) -> p k f", k=DC),
                             w1r[bass.ds(e * D, D), c * P:(c + 1) * P].rearrange("(k p) f -> p k f", p=P))\
                    .then_inc(s_raw[slot], 16)
                sp.dma_start(raw[:, slot, D:2 * D], w2r[bass.ds(e * F + c * P, P), :]).then_inc(s_raw[slot], 16)

            def load_b2(e):
                waits(sp, (s_small, 32), (y_free, e * (BLOCKS * TT) + TT))
                sp.dma_start(b2b[:, :], io["b2"][bass.ds(e, 1), :].broadcast_to([P, D])).then_inc(s_b2, 16)

            with sp.Fori(0, E) as e:
                for c in range(FC):
                    load(e, c)
                    if c == EARLY:
                        load_b2(e)
            for slot in range(TT):
                sp.wait_ge(s_scat[slot], 16 * BLOCKS * E)

        @block.gpsimd
        def _(pool):
            order = Order(pool, pool_order)
            order.mark(pool.memset(ones[:, :], 1.0))
            order.mark(pool.memset(before[:, :], 1.0))
            order.mark(pool.memset(seg, 1.0))
            order.mark(pool.iota(ints, [[1, NT], [0, E]], base=0, channel_multiplier=0))
            order.mark(pool.iota(ints2, [[0, E * NT]], base=0, channel_multiplier=1))
            order.mark(pool.iota(posi, [[1, E * NT]], base=0, channel_multiplier=0))
            order.settled()
            order.mark(pool.affine_select(out=before[:, :], in_=before[:, :], compare_op=ALU.is_gt, fill=0.0,
                                          base=0, pattern=[[1, P]], channel_multiplier=-1))
            order.mark(pool.memset(seg[:, :, 0:1], 0.0))
            order.mark(pool.tensor_copy(parts[:, :, :, 0], ints.rearrange("p (t e) -> p e t", e=E)))
            order.mark(pool.tensor_copy(parts[:, :, :, 1], ints2.rearrange("p (e t) -> p e t", e=E)))
            order.mark(pool.tensor_copy(iota_p[:, :], posi.rearrange("p e t -> p (e t)")[:, 0:P]))
            order.mark(pool.tensor_copy(iota_j[:, :], posi.rearrange("p e t -> p (e t)")[:, 0:SLOTS]))
            order.settled()
            pool.sem_inc(consts_ready, 1)
            pool.sem_inc(w_lo, RING)

            def split_low(e, c):
                pool.wait_ge(w_hi, e * FC + c + 1)
                pool.tensor_tensor(wl[:, c, :], raw[:, c % RING, :], wh[:, c, :].bitcast(F32),
                                   ALU.subtract).then_inc(w_lo, 1)

            def gather(e, tb, q):
                n = tile_count(e, tb, q)
                waits(pool, (consts_ready, 1), (idx_ready, e + 1), (tok_full, n + 1))
                pool.indirect_dma_start(gath[:, q % 2, :], None, xn2_d[:, :],
                                        bass.IndirectOffsetOnAxis(ap=idx_g[:, tb * TT + q:tb * TT + q + 1], axis=0))\
                    .then_inc(s_gath[q % 2], 16)

            def scatter(e, tb):
                for t in range(TT):
                    waits(pool, (consts_ready, 1), (y_scaled, tile_count(e, tb, t) + 1),
                          *((s_scat[k], e * (16 * BLOCKS)) for k in range(TT) if tb == 0 and t == 0))
                    pool.indirect_dma_start(outr[:, :], bass.IndirectOffsetOnAxis(
                        ap=idx_s[:, tb * TT + t:tb * TT + t + 1], axis=0), yb[:, t, :], None,
                        compute_op=ALU.add).then_inc(s_scat[t], 16)

            def expert(e, last):
                gather(e, 1, 0)
                gather(e, 1, 1)
                split_low(e, EARLY)
                split_low(e, EARLY + 1)
                gather(e, 1, 2)
                gather(e, 1, 3)
                scatter(e, 0)
                if not last:
                    gather(e + 1, 0, 0)
                    gather(e + 1, 0, 1)
                    for c in range(EARLY):
                        split_low(e + 1, c)
                        if c == 4:
                            gather(e + 1, 0, 2)
                        if c == 6:
                            gather(e + 1, 0, 3)
                scatter(e, 1)

            for c in range(EARLY):
                split_low(0, c)
            for q in range(TT):
                gather(0, 0, q)
            with pool.Fori(0, E - 1) as e:
                expert(e, False)
            expert(E - 1, True)

        @block.scalar
        def _(act):
            def split_high(e, c, lead):
                times = e * (FC // RING) + c // RING + 1
                waits(act, (tanh_done, 1), (s_raw[c % RING], times * 32), (down_done, lead))
                act.activation(wh[:, c, :], raw[:, c % RING, :], ACT.Copy).then_inc(w_hi, 1)

            def relu(e, s):
                waits(act, (tanh_done, 1), (up_done, e * STEPS + s + 1))
                act.activation(hf[:, s % 2, :], p1[:, s % 2, :], ACT.Relu,
                               bias=b1t[:, bass.ds(e * FC + s % FC, 1)]).then_inc(relu_done, 1)

            def tokens_high(e, tb, q):
                act.wait_ge(tok_full, tile_count(e, tb, q) + 2 + 1)
                act.activation(xh[:, tb, :, q * P:(q + 1) * P], ptr[:, :].rearrange("p (c n) -> p c n", c=DC),
                               ACT.Copy).then_inc(tok_hi, 1)

            def scale(e, tb):
                for t in range(TT):
                    act.wait_ge(y_free, tile_count(e, tb, t) + TT + 1)
                    act.activation(yb[:, t, :], yb[:, t, :], ACT.Copy,
                                   scale=gate_s[:, tb * TT + t:tb * TT + t + 1]).then_inc(y_scaled, 1)

            def expert(e, last):
                for s in range(STEPS):
                    if s < STEPS - 1:
                        relu(e, s + 1)
                    elif not last:
                        relu(e + 1, 0)
                    if s < 2:
                        split_high(e, EARLY + s, lead=e * STEPS)
                    for tb, tiles in TILE_AT.items():
                        if s in tiles and (tb == 1 or not last):
                            tokens_high(e + (tb == 0), tb, tiles.index(s))
                    if s >= FC + 2 and not last:
                        c = s - FC - 2
                        split_high(e + 1, c, lead=e * STEPS + FC + c + 1)
                    if s % FC == FC - 1:
                        scale(e, s // FC)

            act.wait_ge(s_small, 32)
            act.activation(tg[:, :], gate[:, :], ACT.Tanh).then_inc(tanh_done, 1)
            act.wait_ge(b1_full, 1)
            act.activation(b1t[:, :], pc[:, 0:E * FC], ACT.Copy).then_inc(b1_done, 1)
            act.wait_ge(shifted, 1)
            act.activation(ex_te, scores_te, ACT.Exp).then_inc(exp_done, 1)
            for c in range(EARLY):
                split_high(0, c, lead=0)
            for q in range(TT):
                tokens_high(0, 0, q)
            relu(0, 0)
            with act.Fori(0, E - 1) as e:
                expert(e, False)
            expert(E - 1, True)

        @block.vector
        def _(dve):
            order = Order(dve, dve_order)

            def link(instruction):
                order.mark(instruction)
                order.settled()

            def per_expert(v):
                return v.unsqueeze(2).broadcast_to([P, E, NT])

            link(dve.tensor_reduce(lmax, logits[:, :, :], AX.X, ALU.max))
            dve.tensor_tensor(scores_te, logits[:, :, :], lmax.unsqueeze(2).broadcast_to([P, NT, E]),
                              ALU.subtract).then_inc(shifted, 1)
            dve.wait_ge(exp_done, 1)
            link(dve.tensor_reduce(lsum, ex_te, AX.X, ALU.add))
            link(dve.reciprocal(lsum, lsum))
            link(dve.tensor_tensor(scores.rearrange("p e t -> p t e"), ex_te,
                                   lsum.unsqueeze(2).broadcast_to([P, NT, E]), ALU.mult))
            dve.wait_ge(consts_ready, 1)
            link(dve.tensor_copy(parts[:, :, :, 2], scores))
            link(dve.tensor_tensor(rest, scores, parts[:, :, :, 2], ALU.subtract))
            link(dve.tensor_copy(parts[:, :, :, 3], rest))
            link(dve.tensor_tensor(ex, rest, parts[:, :, :, 3], ALU.subtract))
            link(dve.tensor_copy(parts[:, :, :, 4], ex))
            order.mark(dve.memset(thr[:, :], 0))
            link(dve.memset(bit[:, :], 1 << (SCORE_BITS - 1)))
            start = order.base
            with dve.Fori(0, SCORE_BITS) as i:
                order.base = i * 5 + start
                link(dve.tensor_tensor(cand[:, :], thr[:, :], bit[:, :], ALU.bitwise_or))
                dve.tensor_tensor(mask[:, 0], scores, per_expert(cand[:, :].bitcast(F32)),
                                  ALU.is_ge).then_inc(mask_ready, 1)
                dve.wait_ge(counted, i + 1)
                link(dve.tensor_reduce(cnt[:, :], pc[:, 0:E * NT].rearrange("p (e t) -> p e t", t=NT), AX.X, ALU.add))
                link(dve.scalar_tensor_tensor(take[:, :], cnt[:, :], float(TOPK), bit[:, :], ALU.is_ge, ALU.mult))
                order.mark(dve.tensor_single_scalar(bit[:, :], bit[:, :], 1, ALU.logical_shift_right))
                link(dve.tensor_tensor(thr[:, :], thr[:, :], take[:, :], ALU.bitwise_or))
            order.base = start + 5 * SCORE_BITS
            thr_f = per_expert(thr[:, :].bitcast(F32))
            dve.tensor_tensor(mask[:, 0], scores, thr_f, ALU.is_gt).then_inc(mask_ready, 1)
            dve.tensor_tensor(mask[:, 1], scores, thr_f, ALU.is_equal).then_inc(mask_ready, 1)
            dve.wait_ge(counted, SCORE_BITS + 2)
            totals = pc[:, :].rearrange("p (m e t) -> p m e t", m=2, e=E)
            within = ptr[:, 0:E * NT].rearrange("p (e t) -> p e t", e=E)

            def flat(v):
                return v.rearrange("p e t -> p (e t)")

            def places(total):
                link(dve.tensor_tensor_scan(flat(incl), flat(seg), flat(total), 0.0, ALU.mult, ALU.add))
                link(dve.tensor_tensor(incl, incl, total, ALU.subtract))
                link(dve.tensor_tensor(place, incl, within, ALU.add))

            link(dve.tensor_reduce(cnt[:, :], totals[:, 0], AX.X, ALU.add))
            link(dve.tensor_scalar(cnt[:, :], cnt[:, :], -1.0, float(TOPK), ALU.mult, ALU.add))
            places(totals[:, 1])
            link(dve.tensor_tensor(place, place, per_expert(cnt[:, :]), ALU.is_lt))
            link(dve.tensor_tensor(place, place, mask[:, 1], ALU.mult))
            dve.tensor_tensor(mask[:, 0], mask[:, 0], place, ALU.add).then_inc(mask_ready, 1)
            dve.wait_ge(counted, SCORE_BITS + 3)
            places(totals[:, 0])
            link(dve.scalar_tensor_tensor(place, place, 1.0, mask[:, 0], ALU.add, ALU.mult))
            link(dve.tensor_scalar(posi, place, 1.0, None, ALU.subtract))
            link(dve.tensor_single_scalar(posi2, posi, 7, ALU.arith_shift_right))
            link(dve.tensor_copy(pos_j[:, :, :], posi2))
            link(dve.tensor_single_scalar(posi, posi, P - 1, ALU.bitwise_and))
            link(dve.tensor_copy(pos_p[:, :, :], posi))
            dve.sem_inc(y_free, TT)

            def carry(e):
                span = pos_j[:, :, :].rearrange("p e t -> p (e t)")[:, bass.ds(e * NT, NT)]
                dve.wait_ge(oh_used, e * 2)
                order.mark(dve.tensor_tensor(onehot_j[:, :, :], iota_j[:, :].unsqueeze(1).broadcast_to([P, NT, SLOTS]),
                                             span.unsqueeze(2).broadcast_to([P, NT, SLOTS]), ALU.is_equal))
                order.settled()
                own = parts[:, :, :, :].rearrange("p e t k -> p (e t) k")[:, bass.ds(e * NT, NT), :]
                dve.tensor_tensor(carried[:, :, :, :], onehot_j[:, :, :].unsqueeze(2).broadcast_to([P, NT, PARTS, SLOTS]),
                                  own.unsqueeze(3).broadcast_to([P, NT, PARTS, SLOTS]),
                                  ALU.mult).then_inc(carried_ready, 1)

            def one_hot(e, half):
                dve.wait_ge(oh_used, e * 2 + half)
                span = pos_p[:, :, :].rearrange("p e t -> p (e t)")[:, bass.ds(e * NT + half * (NT // 2), NT // 2)]
                dve.tensor_tensor(onehot_p[:, :, :], iota_p[:, :].unsqueeze(1).broadcast_to([P, NT // 2, P]),
                                   span.unsqueeze(2).broadcast_to([P, NT // 2, P]),
                                   ALU.is_equal).then_inc(oh_ready, 1)

            def lists(e):
                dve.wait_ge(oh_used, e * 2 + 2)
                order.mark(dve.tensor_copy(compact[:, :, :].rearrange("p k j -> p (k j)"), pc[:, 0:PARTS * SLOTS]))
                order.settled()
                order.mark(dve.tensor_tensor(gtmp[:, :], compact[:, 2, :], compact[:, 3, :], ALU.add))
                order.settled()
                order.mark(dve.tensor_tensor(gate_g[:, :], gtmp[:, :], compact[:, 4, :], ALU.add))
                dve.scalar_tensor_tensor(idx_g[:, :], compact[:, 0, :], float(P), compact[:, 1, :],
                                         ALU.mult, ALU.add).then_inc(idx_ready, 1)

            def hold(e):
                for k in range(TT):
                    dve.wait_ge(s_scat[k], e * (16 * BLOCKS))
                order.mark(dve.tensor_copy(idx_s[:, :], idx_g[:, :]))
                order.mark(dve.tensor_scalar(gate_s[:, :], gate_g[:, :], tg[:, 0:1], None, ALU.mult))
                order.settled()

            def split_hidden(e, s):
                dve.wait_ge(relu_done, e * STEPS + s + 1)
                if not (isinstance(e, int) and e * STEPS + s <= 1):
                    dve.wait_ge(down_done, e * STEPS + (s - 1))
                order.mark(dve.tensor_copy(hh[:, s % 2, :], hf[:, s % 2, :]))
                order.settled()
                dve.tensor_tensor(hl[:, s % 2, :], hf[:, s % 2, :], hh[:, s % 2, :].bitcast(F32),
                                  ALU.subtract).then_inc(lo_done, 1)

            def tokens_low(e, tb, q):
                dve.wait_ge(tok_hi, tile_count(e, tb, q) + 1)
                dve.tensor_tensor(xl[:, tb, :, q * P:(q + 1) * P], ptr[:, :].rearrange("p (c n) -> p c n", c=DC),
                                  xh[:, tb, :, q * P:(q + 1) * P].bitcast(F32), ALU.subtract).then_inc(tok_free, 1)

            def biased(e, tb):
                dve.wait_ge(s_b2, e * 16 + 16)
                for t in range(TT):
                    dve.wait_ge(s_scat[t], e * (16 * BLOCKS) + 16 * tb)
                    if t < TT - 1:
                        dve.wait_ge(y_full, (e * BLOCKS + tb) * (TT - 1) + t + 1)
                    else:
                        dve.wait_ge(down_done, e * STEPS + (tb + 1) * FC)
                    dve.tensor_tensor(yb[:, t, :], py[:, t, :], b2b[:, :], ALU.add).then_inc(y_free, 1)

            ORDERED = STEPS + 2 + 1 + 3
            carry(0)
            one_hot(0, 0)
            one_hot(0, 1)
            lists(0)
            for q in range(TT):
                tokens_low(0, 0, q)
            split_hidden(0, 0)

            def expert(e, last):
                for s in range(STEPS):
                    if s < STEPS - 1:
                        split_hidden(e, s + 1)
                    elif not last:
                        split_hidden(e + 1, 0)
                    for tb, tiles in TILE_AT.items():
                        if s in tiles and (tb == 1 or not last):
                            tokens_low(e + (tb == 0), tb, tiles.index(s))
                    if s == HALF_AT[0] - 3 and not last:
                        carry(e + 1)
                    if s == HALF_AT[0] - 2 and not last:
                        one_hot(e + 1, 0)
                    if s == HALF_AT[1] - 2 and not last:
                        one_hot(e + 1, 1)
                    if s == HALF_AT[1] - 1:
                        hold(e)
                    if s == HALF_AT[1] and not last:
                        lists(e + 1)
                    if s % FC == FC - 1:
                        biased(e, s // FC)

            start = order.base
            with dve.Fori(0, E - 1) as e:
                order.base = e * ORDERED + start
                expert(e, False)
            order.base = start + ORDERED * (E - 1)
            expert(E - 1, True)

        @block.tensor
        def _(pe):
            pe.wait_ge(s_small, 32)
            pe.transpose(pc[:, 0:E * FC], b1_rows, ident[:, :]).then_inc(b1_full, 1)
            pe.wait_ge(b1_done, 1)
            flat_mask = mask.rearrange("p m e t -> p (m e t)")
            with pe.Fori(0, SCORE_BITS) as i:
                pe.wait_ge(mask_ready, i + 1)
                pe.matmul(pc[:, 0:E * NT], ones[:, :], flat_mask[:, 0:E * NT], start=True, stop=True).then_inc(counted, 1)
            pe.wait_ge(mask_ready, SCORE_BITS + 2)
            pe.matmul(pc[:, :], ones[:, :], flat_mask, start=True, stop=True).then_inc(counted, 1)
            pe.matmul(ptr[:, 0:E * NT], before[:, :], flat_mask[:, E * NT:2 * E * NT], start=True, stop=True).then_inc(counted, 1)
            pe.wait_ge(mask_ready, SCORE_BITS + 3)
            pe.matmul(pc[:, 0:E * NT], ones[:, :], flat_mask[:, 0:E * NT], start=True, stop=True)
            pe.matmul(ptr[:, 0:E * NT], before[:, :], flat_mask[:, 0:E * NT], start=True, stop=True).then_inc(counted, 1)
            pe.sem_inc(tok_full, 2)

            def compaction(e, half):
                pe.wait_ge(oh_ready, e * 2 + half + 1)
                if half == 0:
                    pe.wait_ge(carried_ready, e + 1)
                for t in range(NT // 2):
                    tile = half * (NT // 2) + t
                    done = pe.matmul(pc[:, 0:PARTS * SLOTS], onehot_p[:, t, :],
                                     carried[:, tile, :, :].rearrange("p k j -> p (k j)"),
                                     start=tile == 0, stop=tile == NT - 1)
                done.then_inc(oh_used, 1)

            def transposed(e, tb, q):
                n = tile_count(e, tb, q)
                pe.wait_ge(s_gath[q % 2], (e * (BLOCKS * TT // 2) + (tb * TT + q) // 2 + 1) * 16)
                pe.wait_ge(tok_free, n)
                for c in range(DC):
                    done = pe.transpose(ptr[:, c * P:(c + 1) * P], gath[:, q % 2, c * P:(c + 1) * P], ident[:, :])
                done.then_inc(tok_full, 1)

            def up(e, s):
                tb, c = divmod(s, FC)
                if tb == 0:
                    pe.wait_ge(w_lo, e * FC + c + 1 + RING)
                if c == 0:
                    pe.wait_ge(tok_free, tile_count(e, tb, TT))
                for k in range(DC):
                    cols = slice(k * P, (k + 1) * P)
                    pe.matmul(p1[:, s % 2, :], wh[:, c, cols], xh[:, tb, k, :], start=k == 0, stop=False)
                    pe.matmul(p1[:, s % 2, :], wh[:, c, cols], xl[:, tb, k, :], start=False, stop=False)
                    done = pe.matmul(p1[:, s % 2, :], wl[:, c, cols], xh[:, tb, k, :], start=False, stop=k == DC - 1)
                done.then_inc(up_done, 1)

            def down(e, s):
                tb, c = divmod(s, FC)
                pe.wait_ge(lo_done, e * STEPS + s + 1)
                for t in range(TT):
                    if c == 0:
                        pe.wait_ge(y_free, tile_count(e, tb, t) + 1)
                    tok = slice(t * P, (t + 1) * P)
                    pe.matmul(py[:, t, :], hh[:, s % 2, tok], wh[:, c, D:2 * D], start=c == 0, stop=False)
                    pe.matmul(py[:, t, :], hh[:, s % 2, tok], wl[:, c, D:2 * D], start=False, stop=False)
                    done = pe.matmul(py[:, t, :], hl[:, s % 2, tok], wh[:, c, D:2 * D], start=False, stop=c == FC - 1)
                    if c == FC - 1 and t < TT - 1:
                        done.then_inc(y_full, 1)
                done.then_inc(down_done, 1)

            def expert(e, last):
                for s in range(STEPS):
                    if s < STEPS - 1:
                        up(e, s + 1)
                    elif not last:
                        up(e + 1, 0)
                    for tb, tiles in TILE_AT.items():
                        if s in tiles and (tb == 1 or not last):
                            transposed(e + (tb == 0), tb, tiles.index(s))
                    if s in HALF_AT and not last:
                        compaction(e + 1, HALF_AT.index(s))
                    down(e, s)

            compaction(0, 0)
            compaction(0, 1)
            for q in range(TT):
                transposed(0, 0, q)
            up(0, 0)
            with pe.Fori(0, E - 1) as e:
                expert(e, False)
            expert(E - 1, True)


def build(nc, io):
    with ExitStack() as ctx:
        keep = {"ident": ctx.enter_context(nc.sbuf_tensor("identity", [P, P], F32)),
                "logits": ctx.enter_context(nc.sbuf_tensor("router_logits", [P, NT, E], F32))}
        io["xn2_d"] = nc.dram_tensor("normed_rows", [B * S, D], F32).ap()
        attention_block(nc, io, keep)
        experts_block(nc, io, keep)


_INS = {"x": "x", "ctx": "ctx_1024", "g_attn": "g_xattn", "g_ffn": "g_ffn", "wkv": "L0_xattn_W_kv",
        "bkv": "L0_xattn_b_kv", "wo": "L0_xattn_W_o", "bo": "L0_xattn_b_o", "rw": "L0_ffn_router_w",
        "rb": "L0_ffn_router_b", "w1": "L0_ffn_w1", "b1": "L0_ffn_b1", "w2": "L0_ffn_w2", "b2": "L0_ffn_b2"}


def kernel(**inputs):
    import numpy as np
    import concourse.bacc as bacc
    from concourse.bass_utils import run_bass_kernel_spmd

    nc = bacc.Bacc("TRN2", target_bir_lowering=False, num_devices=1)
    arrays, io = {}, {}
    for short, name in _INS.items():
        a = np.ascontiguousarray(inputs[name])
        arrays[f"in_{short}"] = a
        io[short] = nc.dram_tensor(f"in_{short}", a.shape, mybir.dt.from_np(a.dtype), kind="ExternalInput").ap()
    io["out"] = nc.dram_tensor("out_rows", (B, S, D), F32, kind="ExternalOutput").ap()
    build(nc, io)
    r = run_bass_kernel_spmd(nc, [arrays], core_ids=[0])
    return r.results[0]["out_rows"]
```

```python
import concourse.bass as bass
from concourse import mybir
from contextlib import ExitStack
from itertools import islice

F32 = mybir.dt.float32
F32R = mybir.dt.float32r
BF16 = mybir.dt.bfloat16
I32 = mybir.dt.int32
U32 = mybir.dt.uint32
ALU = mybir.AluOpType
ACT = mybir.ActivationFunctionType
AX = mybir.AxisListType

P = 128
B, S, D = 2, 2048, 512
KV = 154
H, DH = 16, 32
E, F, TOPK = 8, 2048, 1024
EPS = 1e-5
SCALE = DH ** -0.5

DC = D // P
HC = P // DH
KR = KV - P
STACK = 3 * DH + 2
MR = 32 + H
VW = DH + 1
TB = 512
TT = TB // P
BLKS = B * S // TB
NT = B * S // P
FC = F // P
BLOCKS = TOPK // TB
SLOTS = TOPK // P
RING = 2
STEPS = BLOCKS * FC
SCORE_BITS = 30
DIGIT = 2
TRIES = (1 << DIGIT) - 1
ROUNDS = SCORE_BITS // DIGIT
UNROLL = 5
HALVES = 2
SUMS = 4
PARTS = 5


class Order:

    def __init__(self, engine, sem):
        self.engine, self.sem, self.base = engine, sem, 0

    def mark(self, instruction):
        instruction.then_inc(self.sem, 1)
        self.base = self.base + 1

    def settled(self):
        self.engine.wait_ge(self.sem, self.base)

    def settled_before(self, met, value):
        self.engine.compute_val(self.base)
        self.engine.wait_ge(met, value)
        self.engine.wait_ge(self.sem, self.base)


def is_zero(count):
    return isinstance(count, int) and count == 0


def is_one(count):
    return isinstance(count, int) and count == 1


def waits(engine, met, *others):
    for _, value in others:
        engine.compute_val(value)
    engine.wait_ge(*met)
    for semaphore, value in others:
        engine.wait_ge(semaphore, value)


def attention_block(nc, io, keep):
    with ExitStack() as ctx:
        def sb(name, shape, dt=F32):
            return ctx.enter_context(nc.sbuf_tensor(name, shape, dt))

        def ps(name, shape):
            return ctx.enter_context(nc.psum_tensor(name, shape, F32))

        def sem(name):
            return ctx.enter_context(nc.semaphore(name))

        ident, logits = keep["ident"], keep["logits"]
        xin = sb("x_in", [P, TT, D])
        x = sb("x_block", [P, B, TT, D])
        xn2 = sb("x_normed2", [P, TT, D])
        qh = sb("q_hi", [P, DC, TB], F32R)
        ql = sb("q_lo", [P, DC, TB], F32R)
        qs = sb("q_stack", [P, H, TB], F32R)
        ks = sb("k_stack", [P, B, H, P], F32R)
        kr = sb("k_rest_stack", [P, B, H, P], F32R)
        pt = sb("probs", [P, 2, HC + 1, TB])
        vh = sb("values_hi", [P, DC, TB], F32R)
        vl = sb("values_lo", [P, DC, TB], F32R)
        woh = sb("wo_hi", [P, DC, D], F32R)
        wol = sb("wo_lo", [P, DC, D], F32R)
        kh = sb("k_hi", [P, B, DC, HC, KV], F32R)
        vm = sb("v_main", [P, B, H, VW])
        vr = sb("v_rest", [P, B, DC, HC, VW])
        mst = sb("max_staged", [P, TT, MR], F32R)
        mt = sb("max_T", [P, TB], F32R)
        x2t = sb("x2_T", [P, DC, TB])
        tgbo = sb("gated_b_o", [P, D])
        rw = sb("router_w", [P, DC, E])
        rb = sb("router_b", [E, 1])
        gate = sb("attn_gate", [P, 1])
        tg = sb("attn_tanh", [P, 1])
        ones = sb("ones_row", [1, KV])
        neghalf = sb("neg_half", [P, TT])
        eps = sb("eps", [P, TT])
        stats = sb("bn_stats", [P, 2, TT, 6])
        mv = sb("mean_var", [P, 2, TT, 2])
        ve = sb("var_eps", [P, 2, TT])
        rstd = sb("rstd", [P, 2, TT])
        mx = sb("max_logit", [P, TT, H])
        rc = sb("recip_sum", [P, 2, 2, HC])
        val = xn2
        pt_flat = pt[:, :, :, :].rearrange("p a b n -> p (a b n)")
        wkv = pt_flat[:, 0:DC * 2 * D].rearrange("p (k h z d) -> p k h z d", k=DC, z=2, d=DH)
        b_kv = pt_flat[0:1, DC * 2 * D:(DC + 1) * 2 * D].rearrange("p (z n) -> p z n", z=2)
        cx = val[:, :, :].rearrange("p (b z) d -> p b z d", b=B)
        wk = val
        ct = x[:, 1, :, :].rearrange("p (b k) n -> p b (k n)", b=B).rearrange(
            "p b (k n) -> p b k n", n=2 * P)
        wo_raw = val
        kc_hi, kc_lo = ([v[:, :, b * 2 * P:b * 2 * P + KV] for b in range(B)] for v in (vh, vl))

        pb = ps("p_max", [P, 2, 512])
        pl = ps("p_logits", [P, 2, 512])
        po = ps("p_values", [P, 2, 512])
        ptr = ps("p_transposed", [P, 512])
        pw = ps("p_out", [P, 512])
        po_t = po[:, :, 0:2 * HC * VW].rearrange("p u (t j w) -> p u t j w", t=2, j=HC)
        router_out = pw[:, 0:TT * E]

        s_ctx, s_wo, s_small = sem("ctx_in"), sem("wo_in"), sem("small_in")
        s_wkv = [sem(f"wkv_in{k}") for k in range(DC)]
        s_x = sem("x_loaded")
        s_x1st = [sem(f"x1_stored{b}") for b in range(B)]
        s_xn2st = sem("xn2_stored")
        pool_order, dve_order = sem("pool_order"), sem("dve_order")
        consts_ready, stacks_ready = sem("consts_ready"), sem("stack_constants_ready")
        s_keys = [sem(f"keys_stacked{b}") for b in range(B)]
        s_qs, s_m = sem("queries_stacked"), sem("maxima_stacked")
        ctx_pad_ready = sem("ctx_pad_ready")
        zeroed, kept = sem("zeroed"), sem("input_kept")
        ctx_T_full, ctx_T_ready, wk_ready = sem("ctx_T_full"), sem("ctx_T_ready"), sem("wk_ready")
        k_full, kh_ready, kl_ready = sem("keys_full"), sem("keys_hi_ready"), sem("keys_lo_ready")
        kv_full, v_ready = sem("context_values_full"), sem("context_values_ready")
        wol_ready = sem("wo_lo_ready")
        wo_hi_done, tanh_done, bo_done = sem("wo_hi_done"), sem("tanh_done"), sem("bo_done")
        mv1_ready, mv2_ready = sem("mv1_ready"), sem("mv2_ready")
        rstd1_ready, rstd2_ready = sem("rstd1_ready"), sem("rstd2_ready")
        xn_ready, xb_ready, xn2_ready = sem("xn_ready"), sem("xb_ready"), sem("xn2_ready")
        q_full, q_hi, q_free = sem("queries_T_full"), sem("queries_hi_done"), sem("queries_T_free")
        v_full, v_hi, v_free = sem("values_T_full"), sem("values_hi_done"), sem("values_T_free")
        x_full, x_free = sem("normed_T_full"), sem("normed_T_free")
        b_full, b_free = sem("max_logits_full"), sem("max_logits_free")
        m_ready, m_full, mt_ready = sem("max_staged_ready"), sem("max_T_full"), sem("max_T_ready")
        l_full, l_free = sem("logits_full"), sem("logits_free")
        o_full, o_free = sem("values_full"), sem("values_free")
        w_full, w_free = sem("out_full"), sem("out_free")
        r_full, r_rows, r_full_T, r_free = (sem(n) for n in (
            "router_full", "router_rows_out", "router_T_full", "router_free"))
        NL = HC + 1
        BU = TT * DC * 2

        xr = io["x"].rearrange("b s d -> (b s) d")
        outr = io["out"].rearrange("b s d -> (b s) d")
        xn2_d = io["xn2_d"]
        block = ctx.enter_context(nc.Block())

        def rows(dram, j, b):
            return dram[bass.ds(j * TB + b * S, TB), :].rearrange("(t p) d -> p t d", p=P)

        def by_chunk(heads):
            return heads.rearrange("p (c j) n -> p c j n", j=HC)

        def steps(i):
            return [(i * B + 1 + k, i + (1 + k) // B, (1 + k) % B) for k in range(B)]

        STACKED_KEYS = 16 * 2 * 3 * HC
        STACKED = 16 * 3 * HC
        SMALL = 6
        TURNS = (BLKS - 2) // B
        TILES_AFTER = ((0, 1), (2,), (3, 4), ())
        ctx_T = (pb, po)
        keys_T = [v[:, :, :].rearrange("p u (c n) -> p (u c) n", c=2) for v in (pl, po)]
        context_values = ((po[:, 0], po[:, 1]), (pw, ptr))
        queries_T = (ptr, pw, ptr, pw)
        normed_T = (ptr, pb[:, 0], pb[:, 1], ptr)
        values_in_T = (ptr, ptr, ptr, pl[:, 1])
        out_tile = (pw, po[:, 0], po[:, 1], pw)

        @block.sync
        def _(sp):
            for b in range(B):
                sp.dma_start(cx[:, b, 0, :], io["ctx"][b, 0:P, :]).then_inc(s_ctx, 16)
                sp.dma_start(cx[0:KR, b, 1, :], io["ctx"][b, P:KV, :]).then_inc(s_ctx, 16)
            b_kv_dram = io["bkv"].rearrange("(o h z d) -> z o h d", o=1, z=2, d=DH)
            with nc.allow_non_contiguous_dma(reason="small rows, once"):
                for z in range(2):
                    sp.dma_start(b_kv[:, z, :].rearrange("p (h d) -> p h d", d=DH), b_kv_dram[z]).then_inc(s_small, 16)
            for k in range(DC):
                sp.dma_start(wkv[:, k, :, :, :].rearrange("p h z d -> p (h z d)"),
                             io["wkv"][k * P:(k + 1) * P, :]).then_inc(s_wkv[k], 16)
            sp.dma_start(xin[:, :, :], rows(xr, 0, 0)).then_inc(s_x, 16)
            with nc.allow_non_contiguous_dma(reason="small rows, once"):
                sp.dma_start(gate[:, :], io["g_attn"].rearrange("(o n) -> o n", o=1).broadcast_to([P, 1])).then_inc(s_small, 16)
                sp.dma_start(tgbo[:, :], io["bo"].rearrange("(o n) -> o n", o=1).broadcast_to([P, D])).then_inc(s_small, 16)
                sp.dma_start(rb[:, :], io["rb"].rearrange("(n o) -> n o", o=1)).then_inc(s_small, 16)
            sp.dma_start(rw[:, :, :], io["rw"].rearrange("(k p) n -> p k n", p=P)).then_inc(s_small, 16)

            def store(g, j, b):
                waits(sp, (s_ctx, 16 * 2 * B), (w_free, (g + 1) * TT))
                sp.dma_start(rows(outr, j, b), x[:, b, :, :]).then_inc(s_x1st[b], 16)
                waits(sp, (s_ctx, 16 * 2 * B), (xn2_ready, (g + 1) * TT))
                sp.dma_start(rows(xn2_d, j, b), xn2[:, :, :]).then_inc(s_xn2st, 16)

            def stack_keys(b):
                sp.wait_ge(stacks_ready, 2)
                sp.wait_ge(kh_ready, b * (1 + HC) + 1)
                sp.wait_ge(kl_ready, b + 1)
                for part, keys in enumerate((kc_hi[b], kc_hi[b], kc_lo[b])):
                    for j in range(HC):
                        heads = keys[j * DH:(j + 1) * DH, :, :].bitcast(F32)
                        at = slice(part * DH, (part + 1) * DH)
                        sp.dma_start(by_chunk(ks[:, b, :, :].bitcast(F32))[at, :, j, :], heads[:, :, 0:P]).then_inc(s_keys[b], 16)
                        sp.dma_start(by_chunk(kr[:, b, :, :].bitcast(F32))[at, :, j, j * DH:j * DH + KR],
                                     heads[:, :, P:KV]).then_inc(s_keys[b], 16)

            def stack_queries(g, *used):
                for part, queries in enumerate((qh, ql, qh)):
                    for j in range(HC):
                        waits(sp, (s_ctx, 16 * 2 * B), (q_free, (g + 1) * TT), *used)
                        sp.dma_start(by_chunk(qs[:, :, :].bitcast(F32))[part * DH:(part + 1) * DH, :, j, :],
                                     queries[j * DH:(j + 1) * DH, :, :].bitcast(F32)).then_inc(s_qs, 16)

            def stack_maxima(g):
                for part, rows_of in enumerate((slice(0, H), slice(32, 32 + H))):
                    waits(sp, (s_ctx, 16 * 2 * B), (mt_ready, g + 1))
                    sp.dma_start(qs[3 * DH + part:3 * DH + part + 1, :, :].bitcast(F32), mt[rows_of, :].bitcast(F32)).then_inc(s_m, 16)

            def load(g, j, b):
                waits(sp, (s_ctx, 16 * 2 * B), (q_free, g * TT))
                sp.dma_start(xin[:, :, :], rows(xr, j, b)).then_inc(s_x, 16)

            def step(g, j, b, last=False):
                if not last:
                    load(g + 2, j + 1, b)
                stack_queries(g + 1, (l_full, (g + 1) * (DC * NL)))
                stack_maxima(g + 1)

            stack_keys(0)
            stack_queries(0)
            load(1, 0, 1)
            sp.wait_ge(k_full, B)
            sp.dma_start(wo_raw[:, :, :], io["wo"].rearrange("(k p) n -> p k n", p=P)).then_inc(s_wo, 16)
            stack_maxima(0)
            stack_keys(1)
            step(0, 0, 0)

            def turn(i, last):
                for g, j, b in steps(i):
                    store(g - 1, j + b - 1, 1 - b)
                    step(g, j, b, last=last and b == 0)

            with sp.Fori(0, TURNS - 1) as i:
                turn(i, False)
            turn(TURNS - 1, True)
            store(BLKS - 2, BLKS // B - 1, 0)
            store(BLKS - 1, BLKS // B - 1, 1)
            for b in range(B):
                sp.wait_ge(s_x1st[b], 16 * (BLKS // B))
            sp.wait_ge(s_xn2st, 16 * BLKS)

        @block.gpsimd
        def _(pool):
            order = Order(pool, pool_order)
            order.mark(pool.memset(ident[:, :], 0.0))
            pool.memset(ones[:, :], 1.0).then_inc(consts_ready, 1)
            order.settled()
            pool.affine_select(out=ident[:, :], in_=ident[:, :], compare_op=ALU.not_equal, fill=1.0, base=0,
                               pattern=[[-1, P]], channel_multiplier=1).then_inc(consts_ready, 1)
            order.mark(pool.memset(neghalf[:, :], -0.5))
            order.mark(pool.memset(eps[:, :], EPS))
            order.settled()

            def inverse_deviation(g, ln, mv_ready, rstd_ready):
                pool.wait_ge(mv_ready, g + 1)
                order.mark(pool.tensor_tensor(ve[:, ln, :], mv[:, ln, :, 1], eps[:, :], ALU.add))
                order.settled()
                pool.tensor_tensor(rstd[:, ln, :], ve[:, ln, :], neghalf[:, :], ALU.pow).then_inc(rstd_ready, 1)

            def residual(g, b):
                if is_zero(g):
                    pool.wait_ge(bo_done, 1)
                pool.wait_ge(kept, (g + 1) * TT)
                pool.tensor_tensor(x[:, b, :, :], x[:, b, :, :],
                                   tgbo[:, :].unsqueeze(1).broadcast_to([P, TT, D]), ALU.add).then_inc(xb_ready, 1)

            inverse_deviation(0, 0, mv1_ready, rstd1_ready)
            residual(0, 0)
            kr_minus = kr[3 * DH:STACK, :, :, :].bitcast(F32).rearrange("p b (c j) n -> p b c j n", j=HC)
            pool.wait_ge(zeroed, B + 1)
            pool.wait_ge(xb_ready, 1)
            for j in range(HC):
                order.mark(pool.memset(kr_minus[:, 0, :, j, j * DH:j * DH + KR], -1.0))
                order.mark(pool.memset(kr_minus[:, 1, :, j, j * DH:j * DH + KR], -1.0))
            order.settled()
            pool.sem_inc(stacks_ready, 1)
            pool.memset(ks[3 * DH:STACK, :, :, :].bitcast(F32), -1.0).then_inc(stacks_ready, 1)
            pool.wait_ge(stacks_ready, 2)
            inverse_deviation(1, 0, mv1_ready, rstd1_ready)
            residual(1, 1)
            inverse_deviation(0, 1, mv2_ready, rstd2_ready)
            start = order.base
            with pool.Fori(0, TURNS) as i:
                order.base = i * (2 * B) + start
                for g, j, b in steps(i):
                    inverse_deviation(g + 1, 0, mv1_ready, rstd1_ready)
                    residual(g + 1, 1 - b)
                    inverse_deviation(g, 1, mv2_ready, rstd2_ready)
            order.base = start + TURNS * 2 * B
            inverse_deviation(BLKS - 1, 1, mv2_ready, rstd2_ready)

        @block.scalar
        def _(act):
            def keys_high(b):
                act.wait_ge(zeroed, b + 1)
                act.wait_ge(k_full, b + 1)
                act.activation(kc_hi[b], keys_T[b][:, :, 0:KV], ACT.Copy).then_inc(kh_ready, 1)
                for j in range(HC):
                    hr = slice(j * DH, (j + 1) * DH)
                    act.activation(kh[hr, b, :, j, :], keys_T[b][hr, :, 0:KV], ACT.Copy).then_inc(kh_ready, 1)

            act.wait_ge(ctx_pad_ready, 1)
            for b in range(B):
                act.wait_ge(ctx_T_full, b + 1)
                act.activation(ct[:, b, :, 0:P], ctx_T[b][:, 0, :].rearrange("p (k n) -> p k n", k=DC), ACT.Copy)\
                   .then_inc(ctx_T_ready, 1)
                rest = ctx_T[b][:, 1, :].rearrange("p (k n) -> p k n", k=DC)[:, :, 0:KR]
                act.activation(ct[:, b, :, P:2 * P].rearrange("p k (j n) -> p k j n", j=HC)[:, :, :, 0:KR],
                               rest.unsqueeze(2).broadcast_to([P, DC, HC, KR]), ACT.Copy).then_inc(ctx_T_ready, 1)
            for k in range(DC):
                act.wait_ge(s_wkv[k], 16)
                act.activation(wk[:, k, :].rearrange("p (h d) -> p h d", d=DH), wkv[:, k, :, 0, :],
                               ACT.Copy).then_inc(wk_ready, 1)
            act.sem_inc(l_free, 2)

            def weights(g, c, s):
                act.wait_ge(l_full, g * (DC * NL) + c * NL + s + 1)
                act.activation(pt[:, c % 2, s, :], pl[:, (c * NL + s) % 2, :], ACT.Exp, scale=SCALE).then_inc(l_free, 1)

            def queries_high(g, t):
                act.wait_ge(q_full, g * TT + t + 1)
                act.activation(qh[:, :, t * P:(t + 1) * P],
                               queries_T[t][:, :].rearrange("p (c n) -> p c n", c=DC), ACT.Copy).then_inc(q_hi, 1)

            def maxima(g):
                act.wait_ge(m_full, g + 1)
                act.activation(mt[0:MR, :], ptr[0:MR, :], ACT.Copy).then_inc(mt_ready, 1)

            def values_high(g, c):
                act.wait_ge(v_full, g * DC + c + 1)
                act.activation(vh[:, c, :], values_in_T[c][:, :], ACT.Copy).then_inc(v_hi, 1)

            def normed(g, t):
                act.wait_ge(x_full, g * TT + t + 1)
                act.activation(x2t[:, :, t * P:(t + 1) * P], normed_T[t][:, :].rearrange("p (c n) -> p c n", c=DC),
                               ACT.Copy).then_inc(x_free, 1)

            def router_rows(g):
                act.wait_ge(r_full, g + 1)
                act.activation(x2t[0:E, 0, :], pw[0:E, :], ACT.Identity, bias=rb[:, :]).then_inc(r_rows, 1)

            def keep_input(g, j, b, t):
                act.wait_ge(s_x, g * 16 + 16)
                if not is_zero(j):
                    act.wait_ge(s_x1st[b], j * 16)
                    act.wait_ge(xn2_ready, (g - 1) * TT)
                elif b == 1:
                    act.wait_ge(kv_full, 2 * B)
                act.activation(x[:, b, t, :], xin[:, t, :], ACT.Copy).then_inc(kept, 1)

            def step(g, j, b, first=False, last=False):
                for s in range(HC):
                    weights(g, 1, s)
                if not first:
                    for t in range(TT):
                        normed(g - 1, t)
                weights(g, 1, HC)
                if not last:
                    for t in range(TT):
                        keep_input(g + 1, j + b, 1 - b, t)
                if not first:
                    router_rows(g - 1)
                for c in range(1, DC):
                    for k in range(TT):
                        if c + 1 < DC:
                            for s in TILES_AFTER[k]:
                                weights(g, c + 1, s)
                        if c == 1 and not last:
                            queries_high(g + 1, k)
                    if first and c == 1:
                        act.wait_ge(s_keys[1], STACKED_KEYS)
                    values_high(g, c - 1)
                values_high(g, DC - 1)
                if not last:
                    maxima(g + 1)
                    for s in range(NL):
                        weights(g + 1, 0, s)

            act.wait_ge(s_small, 16 * SMALL)
            act.activation(tg[:, :], gate[:, :], ACT.Tanh).then_inc(tanh_done, 1)
            for t in range(TT):
                keep_input(0, 0, 0, t)
            keys_high(0)
            for t in range(TT):
                queries_high(0, t)
            keys_high(1)
            maxima(0)
            for s in range(NL):
                weights(0, 0, s)
            act.wait_ge(s_wo, 16)
            act.activation(woh[:, :, :], wo_raw[:, :, :], ACT.Copy).then_inc(wo_hi_done, 1)
            step(0, 0, 0, first=True)
            with act.Fori(0, TURNS) as i:
                for g, j, b in steps(i):
                    step(g, j, b)
            step(BLKS - 1, BLKS // B - 1, 1, last=True)
            for t in range(TT):
                normed(BLKS - 1, t)
            router_rows(BLKS - 1)

        @block.vector
        def _(dve):
            order = Order(dve, dve_order)
            dve.memset(ct[:, :, :, P:2 * P], 0.0).then_inc(ctx_pad_ready, 1)
            dve.memset(kh[:, 0, :, :, :].bitcast(F32), 0.0).then_inc(zeroed, 1)
            dve.memset(mst[:, :, :].bitcast(F32), 0.0)
            dve.wait_ge(tanh_done, 1)
            dve.tensor_scalar(tgbo[:, :], tgbo[:, :], tg[:, 0:1], None, ALU.mult).then_inc(bo_done, 1)
            dve.sem_inc(b_free, 2)
            dve.sem_inc(o_free, 2)

            def keys_low(b):
                dve.wait_ge(kh_ready, (b + 1) * (1 + HC))
                dve.tensor_tensor(kc_lo[b], keys_T[b][:, :, 0:KV], kc_hi[b].bitcast(F32),
                                  ALU.subtract).then_inc(kl_ready, 1)

            def context_values_out(b):
                dve.wait_ge(kv_full, 2 * b + 2)
                main, rest = context_values[b]
                dve.tensor_copy(vm[:, b, :, 0:DH], main[:, :].rearrange("p (h d) -> p h d", d=DH))
                for j in range(HC):
                    kr = slice(j * DH, j * DH + KR)
                    done = dve.tensor_copy(vr[kr, b, :, j, 0:DH],
                                           rest[kr, :].rearrange("p (c j d) -> p c j d", j=HC, d=DH)[:, :, j, :])
                done.then_inc(v_ready, 1)

            def query_stats(g):
                dve.wait_ge(s_x, g * 16 + 16)
                for t in range(TT):
                    order.mark(dve.bn_stats(stats[:, 0, t, :], xin[:, t, :]))
                order.settled_before(s_small, 16 * SMALL)
                for t in range(TT):
                    done = dve.bn_aggr(mv[:, 0, t, :], stats[:, 0, t, :])
                done.then_inc(mv1_ready, 1)

            def norm_queries(g):
                dve.wait_ge(rstd1_ready, g + 1)
                for t in range(TT):
                    dve.wait_ge(kept, g * TT + t + 1)
                    dve.tensor_scalar(xin[:, t, :], xin[:, t, :], mv[:, 0, t, 0:1], rstd[:, 0, t:t + 1],
                                      ALU.subtract, ALU.mult).then_inc(xn_ready, 1)

            def queries_low(g, t):
                dve.wait_ge(q_hi, g * TT + t + 1)
                dve.tensor_tensor(ql[:, :, t * P:(t + 1) * P], queries_T[t][:, :].rearrange("p (c n) -> p c n", c=DC),
                                  qh[:, :, t * P:(t + 1) * P].bitcast(F32), ALU.subtract).then_inc(q_free, 1)

            def maxima(g, ns):
                for n in ns:
                    h = n * 2 % H
                    dve.wait_ge(b_full, g * BU + n + 1)
                    dve.tensor_reduce(mx[:, n // (2 * DC), h:h + 2], pb[:, n % 2, 0:2 * KV].rearrange("p (j n) -> p j n", j=2),
                                      AX.X, ALU.max).then_inc(b_free, 1)

            def stage_maxima(g):
                dve.wait_ge(b_free, (g + 1) * BU + 2)
                order.mark(dve.tensor_copy(mst[:, :, 0:H], mx[:, :, :]))
                order.settled()
                dve.tensor_tensor(mst[:, :, 32:32 + H], mx[:, :, :], mst[:, :, 0:H].bitcast(F32),
                                  ALU.subtract).then_inc(m_ready, 1)

            def values(g, c, u):
                dve.wait_ge(o_full, g * (DC * 2) + c * 2 + u + 1)
                order.mark(dve.reciprocal(rc[:, u, :, :], po_t[:, u, :, :, DH]))
                order.settled()
                dve.tensor_tensor(
                    val[:, 2 * u:2 * u + 2, c * P:(c + 1) * P].rearrange("p t (j d) -> p t j d", d=DH),
                    po_t[:, u, :, :, 0:DH], rc[:, u, :, :].unsqueeze(3).broadcast_to([P, 2, HC, DH]),
                    ALU.mult).then_inc(o_free, 1)

            def values_low(g, c):
                dve.wait_ge(v_hi, g * DC + c + 1)
                dve.tensor_tensor(vl[:, c, :], values_in_T[c][:, :], vh[:, c, :].bitcast(F32), ALU.subtract).then_inc(v_free, 1)

            def residual(g, b, t):
                if t == 0:
                    dve.wait_ge(xb_ready, g + 1)
                dve.wait_ge(w_full, g * TT + t + 1)
                dve.scalar_tensor_tensor(x[:, b, t, :], out_tile[t][:, :], tg[:, 0:1], x[:, b, t, :],
                                         ALU.mult, ALU.add).then_inc(w_free, 1)

            def result_stats(g, b, t):
                dve.wait_ge(w_free, g * TT + t + 1)
                order.mark(dve.bn_stats(stats[:, 1, t, :], x[:, b, t, :]))

            def norm_result(g, b):
                dve.wait_ge(rstd2_ready, g + 1)
                for t in range(TT):
                    dve.tensor_scalar(xn2[:, t, :], x[:, b, t, :], mv[:, 1, t, 0:1], rstd[:, 1, t:t + 1],
                                      ALU.subtract, ALU.mult).then_inc(xn2_ready, 1)

            def router(g, j, b):
                dve.wait_ge(r_full_T, g + 1)
                order.mark(dve.tensor_copy(logits[:, bass.ds(j * TT + b * (S // P), TT), :],
                                           router_out.rearrange("p (t e) -> p t e", e=E)))
                order.settled()
                dve.sem_inc(r_free, 1)

            def step(g, j, b, first=False, last=False):
                n = iter(range(0, BU))
                nxt = g + 1

                def some(count):
                    if not last:
                        maxima(nxt, list(islice(n, count)))

                if not first:
                    norm_result(g - 1, 1 - b)
                if not last:
                    query_stats(nxt)
                if not first:
                    dve.wait_ge(x_free, g * TT)
                    dve.wait_ge(s_xn2st, g * 16)
                values(g, 0, 0)
                values(g, 0, 1)
                if not last:
                    norm_queries(nxt)
                if not first:
                    router(g - 1, j + b - 1, 1 - b)
                for c in range(1, DC):
                    for k in range(TT):
                        if c > 1 or k > 1:
                            some(1)
                        if k % 2:
                            values(g, c, k // 2)
                        if c == 2 or c == 1 and k > 1:
                            some(len(TILES_AFTER[k]))
                        if c == 1 and not last:
                            queries_low(nxt, k)
                            if k == 1:
                                some(1)
                        if c == 3:
                            some(1)
                    if c == 2:
                        some(1)
                    values_low(g, c - 1)
                    if c == 2:
                        some(1)
                values_low(g, DC - 1)
                some(2 * DC)
                if not last:
                    stage_maxima(nxt)
                for t in range(TT):
                    residual(g, b, t)
                    result_stats(g, b, t)
                order.settled_before(s_small, 16 * SMALL)
                for t in range(TT):
                    done = dve.bn_aggr(mv[:, 1, t, :], stats[:, 1, t, :])
                done.then_inc(mv2_ready, 1)

            query_stats(0)
            norm_queries(0)
            dve.memset(kh[:, 1, :, :, :].bitcast(F32), 0.0).then_inc(zeroed, 1)
            dve.memset(kr[0:STACK, :, :, :].bitcast(F32), 0.0).then_inc(zeroed, 1)
            keys_low(0)
            order.mark(dve.memset(vr[:, :, :, :, :], 0.0))
            dve.memset(vm[:, :, :, DH:VW], 1.0)
            order.settled()
            for j in range(HC):
                order.mark(dve.memset(vr[j * DH:j * DH + KR, :, :, j, DH:VW], 1.0))
            context_values_out(0)
            for t in range(TT):
                queries_low(0, t)
            beside_keys = DC * (DC + 1)
            maxima(0, range(beside_keys))
            keys_low(1)
            maxima(0, range(beside_keys, BU))
            context_values_out(1)
            stage_maxima(0)
            dve.wait_ge(wo_hi_done, 1)
            dve.wait_ge(s_wo, 16)
            dve.tensor_tensor(wol[:, :, :], wo_raw[:, :, :], woh[:, :, :].bitcast(F32), ALU.subtract)\
               .then_inc(wol_ready, 1)
            step(0, 0, 0, first=True)
            start = order.base
            MARKS = B * (TT + 2 * DC + 1 + TT + 1)
            with dve.Fori(0, TURNS) as i:
                order.base = i * MARKS + start
                for g, j, b in steps(i):
                    step(g, j, b)
            order.base = start + TURNS * MARKS
            step(BLKS - 1, BLKS // B - 1, 1, last=True)
            norm_result(BLKS - 1, 1)
            router(BLKS - 1, BLKS // B - 1, 1)

        @block.tensor
        def _(pe):
            pe.wait_ge(consts_ready, 2)
            pe.wait_ge(s_ctx, 16 * 2 * B)
            for b in range(B):
                for k in range(DC):
                    pe.transpose(ctx_T[b][:, 0, k * P:(k + 1) * P], cx[:, b, 0, k * P:(k + 1) * P], ident[:, :])
                for k in range(DC):
                    done = pe.transpose(ctx_T[b][:, 1, k * P:k * P + KR], cx[0:KR, b, 1, k * P:(k + 1) * P],
                                        ident[0:KR, 0:KR])
                done.then_inc(ctx_T_full, 1)

            def keys_of(b, beside=lambda: None):
                pe.wait_ge(wk_ready, DC)
                pe.wait_ge(ctx_T_ready, 2 * B)
                pe.wait_ge(s_small, 16 * SMALL)
                for c in range(DC):
                    cols = slice(c * P, (c + 1) * P)
                    for k in range(DC):
                        pe.matmul(keys_T[b][:, c, 0:KV], wk[:, k, cols], ct[:, b, k, 0:KV], start=k == 0, stop=False)
                        beside()
                    done = pe.matmul(keys_T[b][:, c, 0:KV], b_kv[:, 0, cols], ones[:, :], start=False, stop=True)
                    beside()
                done.then_inc(k_full, 1)

            def context_values_of(b, beside=lambda: None):
                for z in range(2):
                    out = context_values[b][z]
                    for k in range(DC):
                        pe.matmul(out[:, :], ct[:, b, k, z * P:(z + 1) * P], wkv[:, k, :, 1, :], start=k == 0, stop=False)
                        beside()
                    done = pe.matmul(out[:, :], ones[:, 0:P], b_kv[:, 1, :], start=False, stop=True)
                    beside()
                    done.then_inc(kv_full, 1)

            def logits_of(g, b, c, s):
                n = c * NL + s
                pe.wait_ge(l_free, g * (DC * NL) + n + 1)
                if s < HC:
                    h = c * HC + s
                    done = pe.matmul(pl[:, n % 2, :], ks[0:STACK, b, h, :], qs[0:STACK, h, :], start=True, stop=True)
                else:
                    for j in range(HC):
                        h = c * HC + j
                        done = pe.matmul(pl[:, n % 2, :], kr[0:STACK, b, h, :], qs[0:STACK, h, :],
                                         start=j == 0, stop=j == HC - 1)
                done.then_inc(l_full, 1)

            def values_of(g, b, c, k, beside=lambda: None):
                u, t2 = divmod(k, 2)
                if k == 0:
                    pe.wait_ge(l_free, g * (DC * NL) + (c + 1) * NL + 2)
                if t2 == 0:
                    pe.wait_ge(o_free, g * (DC * 2) + c * 2 + u + 1)
                tok, base = slice(k * P, (k + 1) * P), t2 * HC * VW
                for j in range(HC):
                    pe.matmul(po[:, u, base + j * VW:base + (j + 1) * VW],
                              pt[:, c % 2, j, tok], vm[:, b, c * HC + j, :], start=j == 0, stop=False)
                    if j == 1:
                        beside()
                done = pe.matmul(po[:, u, base:base + HC * VW], pt[:, c % 2, HC, tok],
                                 vr[:, b, c, :, :].rearrange("p j w -> p (j w)"), start=False, stop=True)
                if t2 == 1:
                    done.then_inc(o_full, 1)

            def queries(g, t):
                pe.wait_ge(xn_ready, g * TT + t + 1)
                if t == 1 and not is_zero(g) and not is_one(g):
                    pe.wait_ge(r_free, g - 1)
                if t > 1:
                    pe.wait_ge(q_free, g * TT + t - 1)
                for c in range(DC):
                    done = pe.transpose(queries_T[t][:, c * P:(c + 1) * P], xin[:, t, c * P:(c + 1) * P], ident[:, :])
                done.then_inc(q_full, 1)

            def max_logits(g, b, ns):
                for n in ns:
                    t, c, u = n // (2 * DC), n // 2 % DC, n % 2
                    if c == 0 and u == 0:
                        pe.wait_ge(q_hi, g * TT + t + 1)
                    pe.wait_ge(b_free, g * BU + n + 1)
                    pe.matmul(pb[:, u, 0:2 * KV], qh[:, c, t * P:(t + 1) * P],
                              kh[:, b, c, 2 * u:2 * u + 2, 0:KV], start=True, stop=True).then_inc(b_full, 1)

            def maxima(g):
                waits(pe, (consts_ready, 1), (m_ready, g + 1))
                for t in range(TT):
                    done = pe.transpose(ptr[0:MR, t * P:(t + 1) * P], mst[:, t, :].bitcast(F32), ident[:, :])
                done.then_inc(m_full, 1)

            def values_T(g, c):
                pe.wait_ge(o_free, g * (DC * 2) + c * 2 + 4)
                if c in (1, 2):
                    pe.wait_ge(v_free, g * DC + c)
                for t in range(TT):
                    done = pe.transpose(values_in_T[c][:, t * P:(t + 1) * P], val[:, t, c * P:(c + 1) * P], ident[:, :])
                done.then_inc(v_full, 1)

            def stacked(g):
                pe.wait_ge(s_qs, g * STACKED + STACKED)
                pe.wait_ge(s_m, g * (16 * 2) + 16 * 2)

            def project(g, t, beside=lambda: None, after=lambda: None, q_blocks=None):
                if t == 0 and q_blocks is not None:
                    pe.wait_ge(q_free, q_blocks * TT)
                if t == 0 and not is_zero(g):
                    pe.wait_ge(r_free, g)
                if t == TT - 1:
                    pe.wait_ge(w_free, g * TT + 1)
                tok, out = slice(t * P, (t + 1) * P), out_tile[t]
                for c in range(DC):
                    if t == 0:
                        pe.wait_ge(v_free, g * DC + c + 1)
                    pe.matmul(out[:, :], vh[:, c, tok], woh[:, c, :], start=c == 0, stop=False)
                    pe.matmul(out[:, :], vh[:, c, tok], wol[:, c, :], start=False, stop=False)
                    beside()
                    beside()
                    done = pe.matmul(out[:, :], vl[:, c, tok], woh[:, c, :], start=False, stop=c == DC - 1)
                    if c == DC - 1:
                        done.then_inc(w_full, 1)
                    after()

            def normed(g, t):
                pe.wait_ge(xn2_ready, g * TT + t + 1)
                if t == TT - 1:
                    pe.wait_ge(x_free, g * TT + 1)
                for c in range(DC):
                    done = pe.transpose(normed_T[t][:, c * P:(c + 1) * P], xn2[:, t, c * P:(c + 1) * P], ident[:, :])
                done.then_inc(x_full, 1)

            def router(g):
                pe.wait_ge(x_free, (g + 1) * TT)
                pe.wait_ge(w_free, (g + 1) * TT)
                for c in range(DC):
                    done = pe.matmul(pw[0:E, :], rw[:, c, :], x2t[:, c, :], start=c == 0, stop=c == DC - 1)
                done.then_inc(r_full, 1)

            def router_T(g):
                waits(pe, (consts_ready, 1), (r_rows, g + 1))
                for t in range(TT):
                    done = pe.transpose(router_out[:, t * E:(t + 1) * E], x2t[0:E, 0, t * P:(t + 1) * P],
                                        ident[0:E, 0:E])
                done.then_inc(r_full_T, 1)

            def step(g, b, first=False, last=False):
                n = iter(range(0, BU))
                nxt = g + 1

                def beside():
                    if not last:
                        max_logits(nxt, 1 - b, list(islice(n, 1)))

                def nothing():
                    pass

                if first:
                    pe.wait_ge(kl_ready, B)
                    pe.wait_ge(kh_ready, B * (1 + HC))
                if not first:
                    pe.wait_ge(w_free, g * TT - 1)
                for k in range(TT):
                    logits_of(g, b, 1, k)
                    values_of(g, b, 0, k)
                if not first:
                    for t in range(TT):
                        normed(g - 1, t)
                logits_of(g, b, 1, HC)
                if not first:
                    router(g - 1)
                for c in range(1, DC):
                    for k in range(TT):
                        values_of(g, b, c, k, beside if c > 1 or k > 1 else nothing)
                        if c == 1 and k == 0 and not first:
                            router_T(g - 1)
                        if c + 1 < DC:
                            for s in TILES_AFTER[k]:
                                logits_of(g, b, c + 1, s)
                                if c == 2 or k > 1:
                                    beside()
                        if c == 1 and not last:
                            queries(nxt, k)
                            if k == 1:
                                beside()
                        if c == 3:
                            beside()
                    if c == 2:
                        beside()
                    if c == 1 and not last:
                        pe.wait_ge(q_free, nxt * TT + TT - 1)
                    values_T(g, c - 1)
                    if c == 2:
                        beside()
                values_T(g, DC - 1)
                if first:
                    pe.wait_ge(wo_hi_done, 1)
                    pe.wait_ge(wol_ready, 1)
                tiles = iter(range(NL))

                def next_logits():
                    s = next(tiles)
                    if s == 0:
                        stacked(nxt)
                        if first:
                            pe.wait_ge(s_keys[1], STACKED_KEYS)
                    logits_of(nxt, 1 - b, 0, s)

                for t in range(TT):
                    if t == TT - 1 and not last:
                        counts = iter((1, 2, 2, 0))
                        project(g, t, nothing, lambda: [next_logits() for _ in range(next(counts))])
                    elif t == 1 and not last:
                        halves = iter((nothing, lambda: maxima(nxt), nothing, nothing))
                        project(g, t, nothing, lambda: next(halves)())
                    else:
                        project(g, t, beside if t == 0 else nothing, q_blocks=None if last else nxt + 1)

            keys_of(0)
            context_values_of(0)
            for t in range(TT):
                queries(0, t)
            pe.wait_ge(q_free, TT)
            pe.wait_ge(kh_ready, 1 + HC)
            pe.wait_ge(v_ready, 1)
            ns = iter(range(BU))

            def beside():
                max_logits(0, 0, list(islice(ns, 1)))

            keys_of(1, beside)
            context_values_of(1, beside)
            max_logits(0, 0, ns)
            pe.wait_ge(v_ready, 2)
            maxima(0)
            pe.wait_ge(s_keys[0], STACKED_KEYS)
            stacked(0)
            for s in range(NL):
                logits_of(0, 0, 0, s)
            step(0, 0, first=True)
            with pe.Fori(0, TURNS) as i:
                for g, j, b in steps(i):
                    step(g, b)
            step(BLKS - 1, 1, last=True)
            for t in range(TT):
                normed(BLKS - 1, t)
            router(BLKS - 1)
            router_T(BLKS - 1)


def experts_block(nc, io, keep):
    with ExitStack() as ctx:
        def sb(name, shape, dt=F32):
            return ctx.enter_context(nc.sbuf_tensor(name, shape, dt))

        def ps(name, shape):
            return ctx.enter_context(nc.psum_tensor(name, shape, F32))

        def sem(name):
            return ctx.enter_context(nc.semaphore(name))

        ident, logits = keep["ident"], keep["logits"]
        wh = sb("weights_hi", [P, FC, 2 * D], F32R)
        wl = sb("weights_lo", [P, FC, 2 * D], F32R)
        raw = sb("weights_raw", [P, RING, 2 * D])
        xh = sb("tokens_hi", [P, BLOCKS, DC, TB], F32R)
        xl = sb("tokens_lo", [P, BLOCKS, DC, TB], F32R)
        hf = sb("hidden", [P, 2, TB])
        hh = sb("hidden_hi", [P, 2, TB], F32R)
        hl = sb("hidden_lo", [P, 2, TB], F32R)
        gath = sb("gathered", [P, 2, D])
        yb = sb("results", [P, TT, D])
        b2b = sb("b2", [P, D])
        b1t = sb("b1_T", [P, E * FC])
        onehot_p = sb("onehot_p", [P, NT // 2, P], BF16)
        onehot_j = sb("onehot_j", [P, NT, SLOTS], BF16)
        carried = sb("carried", [P, NT, PARTS, SLOTS], BF16)
        parts = sb("parts", [P, E, NT, PARTS], BF16)
        pos_p = sb("pos_mod", [P, E, NT], BF16)
        pos_j = sb("pos_div", [P, E, NT], BF16)
        ones = sb("ones", [P, P], BF16)
        before = sb("before", [P, P], BF16)
        iota_p = sb("iota_p", [P, P], BF16)
        iota_j = sb("iota_j", [P, SLOTS], BF16)
        compact = sb("compact", [P, PARTS, SLOTS])
        idx_g = sb("index_gather", [P, SLOTS], I32)
        idx_s = sb("index_scatter", [P, SLOTS], I32)
        gate_g = sb("gate_next", [P, SLOTS])
        gate_s = sb("gate_now", [P, SLOTS])
        gtmp = sb("gate_sum", [P, SLOTS])
        gate = sb("ffn_gate", [P, 1])
        tg = sb("ffn_tanh", [P, 1])
        thr = sb("threshold_bits", [P, E], I32)
        cnt = sb("count", [P, E])
        try_mask = carried[:, :, :, :].rearrange("p t k j -> p (t k j)")[:, 0:TRIES * E * NT].rearrange(
            "p (m e t) -> p m e t", m=TRIES, e=E)
        mask = carried[:, :, :, :].rearrange("p t k j -> p (t k j)")[:, 0:2 * E * NT].rearrange(
            "p (m e t) -> p m e t", m=2, e=E)
        tmp = yb[:, :, :].rearrange("p t d -> p (t d)").rearrange("p (k e t) -> p k e t", e=E, t=NT)
        tmp2 = gath[:, :, :].rearrange("p s d -> p (s d)").rearrange("p (k e t) -> p k e t", e=E, t=NT)
        scores, ex, rest, incl = tmp[:, 0], tmp[:, 1], tmp[:, 2], tmp[:, 3]
        place, seg = tmp[:, 4], tmp[:, 5]
        posi, posi2 = tmp[:, 6].bitcast(I32), tmp[:, 7].bitcast(I32)
        b1_rows = tmp2[:, 0].rearrange("p e t -> p (e t)")[:, 0:P]
        lmax, lsum = tmp2[:, 1].rearrange("p e t -> p (e t)")[:, 0:NT], tmp2[:, 1].rearrange("p e t -> p (e t)")[:, NT:2 * NT]
        small = tmp2[:, 1].rearrange("p e t -> p (e t)")[:, 2 * NT:]
        tries, digits, cand, take = (small[:, k * TRIES * E:(k + 1) * TRIES * E].rearrange("p (m e) -> p m e", e=E)
                                     for k in range(4))
        digits, cand, take = (v.bitcast(I32) for v in (digits, cand, take))
        digit = small[:, 4 * TRIES * E:4 * TRIES * E + E].bitcast(I32)
        ints = tmp2[:, 2].rearrange("p e t -> p (e t)").bitcast(I32)
        ints2 = tmp2[:, 3].rearrange("p e t -> p (e t)").bitcast(I32)

        p1 = ps("p_hidden", [P, 2, 512])
        py = ps("p_results", [P, TT, 512])
        ptr = ps("p_tokens_T", [P, 512])
        pc = ps("p_counts", [P, 512])
        ex_te, scores_te = (v.rearrange("p e t -> p (e t)").rearrange("p (t e) -> p t e", e=E) for v in (ex, rest))

        s_small = sem("small_in2")
        s_raw = [sem(f"raw_in{k}") for k in range(RING)]
        s_b2 = sem("b2_in")
        s_gath = [sem(f"gathered{k}") for k in range(2)]
        s_first = [sem(f"first_gathered{k}") for k in range(TT)]
        s_scat = [sem(f"scattered{k}") for k in range(TT)]
        pool_order, dve_order = sem("pool_order2"), sem("dve_order2")
        consts_ready, b1_full, b1_done, tanh_done = sem("consts_ready2"), sem("b1_full"), sem("b1_done"), sem("tanh_done2")
        shifted, exp_done = sem("shifted"), sem("exp_done")
        scores_ready, parts_ready = sem("scores_ready"), sem("parts_ready")
        mask_ready, counted = sem("mask_ready"), sem("counted")
        w_hi, w_lo = sem("weights_hi_done"), sem("weights_lo_done")
        oh_ready, oh_used = sem("onehot_ready"), sem("onehot_used")
        carried_ready, idx_ready = sem("carried_ready"), sem("index_ready")
        tok_full, tok_hi, tok_free = sem("tokens_full"), sem("tokens_hi_done"), sem("tokens_free")
        expert_added = sem("expert_added")
        up_done, relu_done, lo_done, down_done = sem("up_done"), sem("relu_done"), sem("hidden_lo_done"), sem("down_done")
        y_full, y_free, y_scaled = sem("results_full"), sem("results_free"), sem("results_scaled")

        outr = io["out"].rearrange("b s d -> (b s) d")
        xn2_d = io["xn2_d"]
        block = ctx.enter_context(nc.Block())

        TILE_AT = {1: (4, 6, 8, 10), 0: (FC + 5, FC + 7, FC + 9, FC + 11)}
        tokens_T = {0: (ptr, pc, ptr, pc), 1: (ptr, ptr, ptr, ptr)}
        HALF_AT = (FC - 7, FC - 3)
        EARLY = FC - 2

        def tile_count(e, tb, q):
            return e * (BLOCKS * TT) + tb * TT + q

        @block.sync
        def _(sp):
            sp.dma_start(b1_rows, io["b1"].rearrange("e (c p) -> (e c) p", p=P)).then_inc(s_small, 16)
            with nc.allow_non_contiguous_dma(reason="one gate"):
                sp.dma_start(gate[:, :], io["g_ffn"].rearrange("(o n) -> o n", o=1).broadcast_to([P, 1])).then_inc(s_small, 16)

            w1r = io["w1"].rearrange("e d f -> (e d) f")
            w2r = io["w2"].rearrange("e f d -> (e f) d")

            def load(e, c):
                waits(sp, (s_small, 32), (w_lo, e * FC + c + 1))
                slot = c % RING
                sp.dma_start(raw[:, slot, 0:D].rearrange("p (k f) -> p k f", k=DC),
                             w1r[bass.ds(e * D, D), c * P:(c + 1) * P].rearrange("(k p) f -> p k f", p=P))\
                    .then_inc(s_raw[slot], 16)
                sp.dma_start(raw[:, slot, D:2 * D], w2r[bass.ds(e * F + c * P, P), :]).then_inc(s_raw[slot], 16)

            def load_b2(e):
                waits(sp, (s_small, 32), (y_free, e * (BLOCKS * TT) + TT))
                sp.dma_start(b2b[:, :], io["b2"][bass.ds(e, 1), :].broadcast_to([P, D])).then_inc(s_b2, 16)

            with sp.Fori(0, E) as e:
                for c in range(FC):
                    load(e, c)
                    if c == EARLY:
                        load_b2(e)
            for slot in range(TT):
                sp.wait_ge(s_scat[slot], 16 * BLOCKS * E)

        @block.gpsimd
        def _(pool):
            order = Order(pool, pool_order)
            order.mark(pool.memset(ones[:, :], 1.0))
            order.mark(pool.memset(before[:, :], 1.0))
            order.mark(pool.memset(seg, 1.0))
            order.mark(pool.iota(ints, [[1, NT], [0, E]], base=0, channel_multiplier=0))
            order.mark(pool.iota(ints2, [[0, E * NT]], base=0, channel_multiplier=1))
            order.mark(pool.iota(posi, [[1, E * NT]], base=0, channel_multiplier=0))
            order.settled()
            order.mark(pool.affine_select(out=before[:, :], in_=before[:, :], compare_op=ALU.is_gt, fill=0.0,
                                          base=0, pattern=[[1, P]], channel_multiplier=-1))
            order.mark(pool.memset(seg[:, :, 0:1], 0.0))
            order.mark(pool.tensor_copy(parts[:, :, :, 0], ints.rearrange("p (t e) -> p e t", e=E)))
            order.mark(pool.tensor_copy(parts[:, :, :, 1], ints2.rearrange("p (e t) -> p e t", e=E)))
            order.mark(pool.tensor_copy(iota_p[:, :], posi.rearrange("p e t -> p (e t)")[:, 0:P]))
            order.mark(pool.tensor_copy(iota_j[:, :], posi.rearrange("p e t -> p (e t)")[:, 0:SLOTS]))
            order.settled()
            pool.sem_inc(consts_ready, 1)
            pool.sem_inc(w_lo, RING)
            pool.sem_inc(expert_added, 1)

            def split_low(e, c):
                pool.wait_ge(w_hi, e * FC + c + 1)
                pool.tensor_tensor(wl[:, c, :], raw[:, c % RING, :], wh[:, c, :].bitcast(F32),
                                   ALU.subtract).then_inc(w_lo, 1)

            def gather(e, tb, q):
                n = tile_count(e, tb, q)
                waits(pool, (consts_ready, 1), (idx_ready, e + 1), (tok_full, n + 1))
                pool.indirect_dma_start(gath[:, q % 2, :], None, xn2_d[:, :],
                                        bass.IndirectOffsetOnAxis(ap=idx_g[:, tb * TT + q:tb * TT + q + 1], axis=0))\
                    .then_inc(s_gath[q % 2], 16)

            def scatter(e, tb):
                for t in range(TT):
                    waits(pool, (consts_ready, 1), (y_scaled, tile_count(e, tb, t) + 1))
                    pool.indirect_dma_start(outr[:, :], bass.IndirectOffsetOnAxis(
                        ap=idx_s[:, tb * TT + t:tb * TT + t + 1], axis=0), yb[:, t, :], None,
                        compute_op=ALU.add).then_inc(s_scat[t], 16)

            def expert(e, last):
                gather(e, 1, 0)
                gather(e, 1, 1)
                split_low(e, EARLY)
                split_low(e, EARLY + 1)
                gather(e, 1, 2)
                gather(e, 1, 3)
                scatter(e, 0)
                if not last:
                    gather(e + 1, 0, 0)
                    gather(e + 1, 0, 1)
                    for c in range(EARLY):
                        split_low(e + 1, c)
                        if c == 4:
                            gather(e + 1, 0, 2)
                        if c == 6:
                            gather(e + 1, 0, 3)
                scatter(e, 1)
                for k in range(TT):
                    pool.wait_ge(s_scat[k], e * (16 * BLOCKS) + 16 * BLOCKS)
                pool.sem_inc(expert_added, 1)

            pool.wait_ge(scores_ready, 1)
            for k, (value, left) in enumerate(((scores, rest), (rest, ex), (ex, None))):
                order.mark(pool.tensor_copy(parts[:, :, :, 2 + k], value))
                order.settled()
                if left is not None:
                    order.mark(pool.tensor_tensor(left, value, parts[:, :, :, 2 + k], ALU.subtract))
                    order.settled()
            pool.sem_inc(parts_ready, 1)
            for c in range(EARLY):
                split_low(0, c)
            for q in range(TT):
                pool.wait_ge(idx_ready, 1)
                pool.indirect_dma_start(yb[:, q, :], None, xn2_d[:, :],
                                        bass.IndirectOffsetOnAxis(ap=idx_g[:, q:q + 1], axis=0))\
                    .then_inc(s_first[q], 16)
            with pool.Fori(0, E - 1) as e:
                expert(e, False)
            expert(E - 1, True)

        @block.scalar
        def _(act):
            def split_high(e, c, lead):
                times = e * (FC // RING) + c // RING + 1
                waits(act, (tanh_done, 1), (s_raw[c % RING], times * 32), (down_done, lead + 1))
                act.activation(wh[:, c, :], raw[:, c % RING, :], ACT.Copy).then_inc(w_hi, 1)

            def relu(e, s):
                waits(act, (tanh_done, 1), (up_done, e * STEPS + s + 1))
                act.activation(hf[:, s % 2, :], p1[:, s % 2, :], ACT.Relu,
                               bias=b1t[:, bass.ds(e * FC + s % FC, 1)]).then_inc(relu_done, 1)

            def tokens_high(e, tb, q):
                act.wait_ge(tok_full, tile_count(e, tb, q) + 2 + 1)
                act.activation(xh[:, tb, :, q * P:(q + 1) * P], tokens_T[tb][q][:, :].rearrange("p (c n) -> p c n", c=DC),
                               ACT.Copy).then_inc(tok_hi, 1)

            def scale(e, tb):
                for t in range(TT):
                    act.wait_ge(y_free, tile_count(e, tb, t) + TT + 1)
                    act.activation(yb[:, t, :], yb[:, t, :], ACT.Copy,
                                   scale=gate_s[:, tb * TT + t:tb * TT + t + 1]).then_inc(y_scaled, 1)

            def expert(e, last):
                for s in range(STEPS):
                    if s < STEPS - 1:
                        relu(e, s + 1)
                    elif not last:
                        relu(e + 1, 0)
                    if s < 2:
                        split_high(e, EARLY + s, lead=e * STEPS)
                    for tb, tiles in TILE_AT.items():
                        if s in tiles and (tb == 1 or not last):
                            tokens_high(e + (tb == 0), tb, tiles.index(s))
                    if s >= FC + 2 and not last:
                        c = s - FC - 2
                        split_high(e + 1, c, lead=e * STEPS + FC + c + 1)
                    if s % FC == FC - 1:
                        scale(e, s // FC)

            act.wait_ge(s_small, 32)
            act.activation(tg[:, :], gate[:, :], ACT.Tanh).then_inc(tanh_done, 1)
            act.wait_ge(b1_full, 1)
            act.activation(b1t[:, :], pc[:, 0:E * FC], ACT.Copy).then_inc(b1_done, 1)
            act.wait_ge(shifted, 1)
            act.activation(ex_te, scores_te, ACT.Exp).then_inc(exp_done, 1)
            for c in range(EARLY):
                split_high(0, c, lead=0)
            for q in range(TT):
                tokens_high(0, 0, q)
            relu(0, 0)
            with act.Fori(0, E - 1) as e:
                expert(e, False)
            expert(E - 1, True)

        @block.vector
        def _(dve):
            order = Order(dve, dve_order)

            def link(instruction):
                order.mark(instruction)
                order.settled()

            def per_expert(v):
                return v.unsqueeze(2).broadcast_to([P, E, NT])

            link(dve.tensor_reduce(lmax, logits[:, :, :], AX.X, ALU.max))
            dve.tensor_tensor(scores_te, logits[:, :, :], lmax.unsqueeze(2).broadcast_to([P, NT, E]),
                              ALU.subtract).then_inc(shifted, 1)
            dve.wait_ge(exp_done, 1)
            link(dve.tensor_reduce(lsum, ex_te, AX.X, ALU.add))
            link(dve.reciprocal(lsum, lsum))
            link(dve.tensor_tensor(scores.rearrange("p e t -> p t e"), ex_te,
                                   lsum.unsqueeze(2).broadcast_to([P, NT, E]), ALU.mult))
            dve.wait_ge(consts_ready, 1)
            dve.sem_inc(scores_ready, 1)
            order.mark(dve.memset(thr[:, :], 0))
            for k in range(TRIES):
                order.mark(dve.memset(digits[:, k, :], (k + 1) << (SCORE_BITS - DIGIT)))
            order.settled()
            start = order.base
            with dve.Fori(0, ROUNDS // UNROLL) as i:
                order.base = i * (5 * UNROLL) + start
                for k in range(UNROLL):
                    link(dve.tensor_tensor(cand[:, :, :], thr[:, :].unsqueeze(1).broadcast_to([P, TRIES, E]),
                                           digits[:, :, :], ALU.bitwise_or))
                    for h in range(HALVES):
                        part = slice(h * NT // HALVES, (h + 1) * NT // HALVES)
                        dve.tensor_tensor(
                            try_mask[:, :, :, part],
                            scores[:, :, part].unsqueeze(1).broadcast_to([P, TRIES, E, NT // HALVES]),
                            cand[:, :, :].bitcast(F32).unsqueeze(3).broadcast_to([P, TRIES, E, NT // HALVES]),
                            ALU.is_ge).then_inc(mask_ready, 1)
                    dve.wait_ge(counted, i * UNROLL + (k + 1))
                    link(dve.tensor_reduce(tries.rearrange("p m e -> p (m e)"),
                                           pc[:, 0:TRIES * E * SUMS].rearrange("p (n t) -> p n t", t=SUMS),
                                           AX.X, ALU.add))
                    link(dve.scalar_tensor_tensor(take[:, :, :], tries[:, :, :], float(TOPK), digits[:, :, :],
                                                  ALU.is_ge, ALU.mult))
                    dve.tensor_single_scalar(digits[:, :, :], digits[:, :, :], DIGIT, ALU.logical_shift_right)
                    link(dve.tensor_reduce(digit[:, :], take[:, :, :].rearrange("p m e -> p e m"), AX.X, ALU.max))
                    order.mark(dve.tensor_tensor(thr[:, :], thr[:, :], digit[:, :], ALU.bitwise_or))
                    order.settled()
            order.base = start + 5 * ROUNDS
            thr_f = per_expert(thr[:, :].bitcast(F32))
            dve.tensor_tensor(mask[:, 0], scores, thr_f, ALU.is_gt).then_inc(mask_ready, 1)
            dve.tensor_tensor(mask[:, 1], scores, thr_f, ALU.is_equal).then_inc(mask_ready, 1)
            dve.wait_ge(counted, ROUNDS + 2)
            totals = pc[:, :].rearrange("p (m e t) -> p m e t", m=2, e=E)
            within = ptr[:, 0:E * NT].rearrange("p (e t) -> p e t", e=E)

            def flat(v):
                return v.rearrange("p e t -> p (e t)")

            def places(total):
                link(dve.tensor_tensor_scan(flat(incl), flat(seg), flat(total), 0.0, ALU.mult, ALU.add))
                link(dve.tensor_tensor(incl, incl, total, ALU.subtract))
                link(dve.tensor_tensor(place, incl, within, ALU.add))

            link(dve.tensor_reduce(cnt[:, :], totals[:, 0], AX.X, ALU.add))
            link(dve.tensor_scalar(cnt[:, :], cnt[:, :], -1.0, float(TOPK), ALU.mult, ALU.add))
            places(totals[:, 1])
            link(dve.tensor_tensor(place, place, per_expert(cnt[:, :]), ALU.is_lt))
            link(dve.tensor_tensor(place, place, mask[:, 1], ALU.mult))
            dve.tensor_tensor(mask[:, 0], mask[:, 0], place, ALU.add).then_inc(mask_ready, 1)
            dve.wait_ge(counted, ROUNDS + 3)
            places(totals[:, 0])
            link(dve.scalar_tensor_tensor(place, place, 1.0, mask[:, 0], ALU.add, ALU.mult))
            link(dve.tensor_scalar(posi, place, 1.0, None, ALU.subtract))
            link(dve.tensor_single_scalar(posi2, posi, 7, ALU.arith_shift_right))
            link(dve.tensor_copy(pos_j[:, :, :], posi2))
            link(dve.tensor_single_scalar(posi, posi, P - 1, ALU.bitwise_and))
            link(dve.tensor_copy(pos_p[:, :, :], posi))
            dve.sem_inc(y_free, TT)

            def carry(e):
                span = pos_j[:, :, :].rearrange("p e t -> p (e t)")[:, bass.ds(e * NT, NT)]
                dve.wait_ge(oh_used, e * 2)
                order.mark(dve.tensor_tensor(onehot_j[:, :, :], iota_j[:, :].unsqueeze(1).broadcast_to([P, NT, SLOTS]),
                                             span.unsqueeze(2).broadcast_to([P, NT, SLOTS]), ALU.is_equal))
                order.settled()
                own = parts[:, :, :, :].rearrange("p e t k -> p (e t) k")[:, bass.ds(e * NT, NT), :]
                dve.tensor_tensor(carried[:, :, :, :], onehot_j[:, :, :].unsqueeze(2).broadcast_to([P, NT, PARTS, SLOTS]),
                                  own.unsqueeze(3).broadcast_to([P, NT, PARTS, SLOTS]),
                                  ALU.mult).then_inc(carried_ready, 1)

            def one_hot(e, half):
                dve.wait_ge(oh_used, e * 2 + half)
                span = pos_p[:, :, :].rearrange("p e t -> p (e t)")[:, bass.ds(e * NT + half * (NT // 2), NT // 2)]
                dve.tensor_tensor(onehot_p[:, :, :], iota_p[:, :].unsqueeze(1).broadcast_to([P, NT // 2, P]),
                                   span.unsqueeze(2).broadcast_to([P, NT // 2, P]),
                                   ALU.is_equal).then_inc(oh_ready, 1)

            def lists(e):
                dve.wait_ge(oh_used, e * 2 + 2)
                order.mark(dve.tensor_copy(compact[:, :, :].rearrange("p k j -> p (k j)"), pc[:, 0:PARTS * SLOTS]))
                order.settled()
                order.mark(dve.tensor_tensor(gtmp[:, :], compact[:, 2, :], compact[:, 3, :], ALU.add))
                order.settled()
                order.mark(dve.tensor_tensor(gate_g[:, :], gtmp[:, :], compact[:, 4, :], ALU.add))
                dve.scalar_tensor_tensor(idx_g[:, :], compact[:, 0, :], float(P), compact[:, 1, :],
                                         ALU.mult, ALU.add).then_inc(idx_ready, 1)

            def hold(e):
                dve.wait_ge(expert_added, e + 1)
                order.mark(dve.tensor_copy(idx_s[:, :], idx_g[:, :]))
                order.mark(dve.tensor_scalar(gate_s[:, :], gate_g[:, :], tg[:, 0:1], None, ALU.mult))
                order.settled()

            def split_hidden(e, s):
                dve.wait_ge(relu_done, e * STEPS + s + 1)
                if not (is_zero(e) and s == 0):
                    dve.wait_ge(down_done, e * STEPS + s)
                order.mark(dve.tensor_copy(hh[:, s % 2, :], hf[:, s % 2, :]))
                order.settled()
                dve.tensor_tensor(hl[:, s % 2, :], hf[:, s % 2, :], hh[:, s % 2, :].bitcast(F32),
                                  ALU.subtract).then_inc(lo_done, 1)

            def tokens_low(e, tb, q):
                dve.wait_ge(tok_hi, tile_count(e, tb, q) + 1)
                dve.tensor_tensor(xl[:, tb, :, q * P:(q + 1) * P], tokens_T[tb][q][:, :].rearrange("p (c n) -> p c n", c=DC),
                                  xh[:, tb, :, q * P:(q + 1) * P].bitcast(F32), ALU.subtract).then_inc(tok_free, 1)

            def biased(e, tb):
                dve.wait_ge(s_b2, e * 16 + 16)
                if tb == 0:
                    dve.wait_ge(expert_added, e + 1)
                for t in range(TT):
                    if tb == 1:
                        dve.wait_ge(s_scat[t], e * (16 * BLOCKS) + 16)
                    if t < TT - 1:
                        dve.wait_ge(y_full, (e * BLOCKS + tb) * (TT - 1) + t + 1)
                    else:
                        dve.wait_ge(down_done, e * STEPS + (tb + 1) * FC + 1)
                    dve.tensor_tensor(yb[:, t, :], py[:, t, :], b2b[:, :], ALU.add).then_inc(y_free, 1)

            ORDERED = STEPS + 2 + 1 + 3
            dve.wait_ge(parts_ready, 1)
            carry(0)
            one_hot(0, 0)
            one_hot(0, 1)
            lists(0)
            for q in range(TT):
                tokens_low(0, 0, q)
            split_hidden(0, 0)

            def expert(e, last):
                for s in range(STEPS):
                    if s < STEPS - 1:
                        split_hidden(e, s + 1)
                    elif not last:
                        split_hidden(e + 1, 0)
                    for tb, tiles in TILE_AT.items():
                        if s in tiles and (tb == 1 or not last):
                            tokens_low(e + (tb == 0), tb, tiles.index(s))
                    if s == HALF_AT[0] - 3 and not last:
                        carry(e + 1)
                    if s == HALF_AT[0] - 2 and not last:
                        one_hot(e + 1, 0)
                    if s == HALF_AT[1] - 2 and not last:
                        one_hot(e + 1, 1)
                    if s == HALF_AT[1] - 1:
                        hold(e)
                    if s == HALF_AT[1] and not last:
                        lists(e + 1)
                    if s % FC == FC - 1:
                        biased(e, s // FC)

            start = order.base
            with dve.Fori(0, E - 1) as e:
                order.base = e * ORDERED + start
                expert(e, False)
            order.base = start + ORDERED * (E - 1)
            expert(E - 1, True)

        @block.tensor
        def _(pe):
            pe.sem_inc(down_done, 1)
            pe.wait_ge(s_small, 32)
            pe.transpose(pc[:, 0:E * FC], b1_rows, ident[:, :]).then_inc(b1_full, 1)
            pe.wait_ge(b1_done, 1)
            flat_mask = mask.rearrange("p m e t -> p (m e t)")
            with pe.Fori(0, ROUNDS // UNROLL) as i:
                for k in range(UNROLL):
                    for h in range(HALVES):
                        pe.wait_ge(mask_ready, i * (HALVES * UNROLL) + (k * HALVES + h + 1))
                        for t in range(h * NT // HALVES, (h + 1) * NT // HALVES, SUMS):
                            done = pe.matmul(pc[:, 0:TRIES * E * SUMS], ones[:, :],
                                             try_mask[:, :, :, t:t + SUMS].rearrange("p m e t -> p (m e) t"),
                                             start=t == 0, stop=t == NT - SUMS)
                    done.then_inc(counted, 1)
            pe.wait_ge(mask_ready, HALVES * ROUNDS + 2)
            pe.matmul(pc[:, :], ones[:, :], flat_mask, start=True, stop=True).then_inc(counted, 1)
            pe.matmul(ptr[:, 0:E * NT], before[:, :], flat_mask[:, E * NT:2 * E * NT], start=True, stop=True).then_inc(counted, 1)
            pe.wait_ge(mask_ready, HALVES * ROUNDS + 3)
            pe.matmul(pc[:, 0:E * NT], ones[:, :], flat_mask[:, 0:E * NT], start=True, stop=True)
            pe.matmul(ptr[:, 0:E * NT], before[:, :], flat_mask[:, 0:E * NT], start=True, stop=True).then_inc(counted, 1)
            pe.sem_inc(tok_full, 2)

            def compaction(e, half):
                pe.wait_ge(oh_ready, e * 2 + half + 1)
                if half == 0:
                    pe.wait_ge(carried_ready, e + 1)
                for t in range(NT // 2):
                    tile = half * (NT // 2) + t
                    done = pe.matmul(pc[:, 0:PARTS * SLOTS], onehot_p[:, t, :],
                                     carried[:, tile, :, :].rearrange("p k j -> p (k j)"),
                                     start=tile == 0, stop=tile == NT - 1)
                done.then_inc(oh_used, 1)

            def transposed(e, tb, q):
                n = tile_count(e, tb, q)
                if is_zero(e) and tb == 0:
                    tile = yb[:, q, :]
                    pe.wait_ge(s_first[q], 16)
                else:
                    tile = gath[:, q % 2, :]
                    pe.wait_ge(s_gath[q % 2], (e * (BLOCKS * TT // 2) + ((tb - 1) * TT + q) // 2 + 1) * 16)
                if tb == 1:
                    pe.wait_ge(tok_free, n)
                elif q > 1 or not is_zero(e):
                    pe.wait_ge(tok_free, n - (q > 0))
                for c in range(DC):
                    done = pe.transpose(tokens_T[tb][q][:, c * P:(c + 1) * P], tile[:, c * P:(c + 1) * P], ident[:, :])
                done.then_inc(tok_full, 1)

            def up(e, s):
                tb, c = divmod(s, FC)
                if tb == 0:
                    pe.wait_ge(w_lo, e * FC + c + 1 + RING)
                if c == 0:
                    pe.wait_ge(tok_free, tile_count(e, tb, TT))
                for k in range(DC):
                    cols = slice(k * P, (k + 1) * P)
                    pe.matmul(p1[:, s % 2, :], wh[:, c, cols], xh[:, tb, k, :], start=k == 0, stop=False)
                    pe.matmul(p1[:, s % 2, :], wh[:, c, cols], xl[:, tb, k, :], start=False, stop=False)
                    done = pe.matmul(p1[:, s % 2, :], wl[:, c, cols], xh[:, tb, k, :], start=False, stop=k == DC - 1)
                done.then_inc(up_done, 1)

            def down(e, s):
                tb, c = divmod(s, FC)
                pe.wait_ge(lo_done, e * STEPS + s + 1)
                for t in range(TT):
                    if c == 0:
                        pe.wait_ge(y_free, tile_count(e, tb, t) + 1)
                    tok = slice(t * P, (t + 1) * P)
                    pe.matmul(py[:, t, :], hh[:, s % 2, tok], wh[:, c, D:2 * D], start=c == 0, stop=False)
                    pe.matmul(py[:, t, :], hh[:, s % 2, tok], wl[:, c, D:2 * D], start=False, stop=False)
                    done = pe.matmul(py[:, t, :], hl[:, s % 2, tok], wh[:, c, D:2 * D], start=False, stop=c == FC - 1)
                    if c == FC - 1 and t < TT - 1:
                        done.then_inc(y_full, 1)
                done.then_inc(down_done, 1)

            def expert(e, last):
                for s in range(STEPS):
                    if s < STEPS - 1:
                        up(e, s + 1)
                    elif not last:
                        up(e + 1, 0)
                    for tb, tiles in TILE_AT.items():
                        if s in tiles and (tb == 1 or not last):
                            transposed(e + (tb == 0), tb, tiles.index(s))
                    if s in HALF_AT and not last:
                        compaction(e + 1, HALF_AT.index(s))
                    down(e, s)

            compaction(0, 0)
            compaction(0, 1)
            for q in range(TT):
                transposed(0, 0, q)
            up(0, 0)
            with pe.Fori(0, E - 1) as e:
                expert(e, False)
            expert(E - 1, True)


def build(nc, io):
    with ExitStack() as ctx:
        keep = {"ident": ctx.enter_context(nc.sbuf_tensor("identity", [P, P], F32)),
                "logits": ctx.enter_context(nc.sbuf_tensor("router_logits", [P, NT, E], F32))}
        io["xn2_d"] = nc.dram_tensor("normed_rows", [B * S, D], F32).ap()
        attention_block(nc, io, keep)
        experts_block(nc, io, keep)


_INS = {"x": "x", "ctx": "ctx_1024", "g_attn": "g_xattn", "g_ffn": "g_ffn", "wkv": "L0_xattn_W_kv",
        "bkv": "L0_xattn_b_kv", "wo": "L0_xattn_W_o", "bo": "L0_xattn_b_o", "rw": "L0_ffn_router_w",
        "rb": "L0_ffn_router_b", "w1": "L0_ffn_w1", "b1": "L0_ffn_b1", "w2": "L0_ffn_w2", "b2": "L0_ffn_b2"}


def kernel(**inputs):
    import numpy as np
    import concourse.bacc as bacc
    from concourse.bass_utils import run_bass_kernel_spmd

    nc = bacc.Bacc("TRN2", target_bir_lowering=False, num_devices=1)
    arrays, io = {}, {}
    for short, name in _INS.items():
        a = np.ascontiguousarray(inputs[name])
        arrays[f"in_{short}"] = a
        io[short] = nc.dram_tensor(f"in_{short}", a.shape, mybir.dt.from_np(a.dtype), kind="ExternalInput").ap()
    io["out"] = nc.dram_tensor("out_rows", (B, S, D), F32, kind="ExternalOutput").ap()
    build(nc, io)
    r = run_bass_kernel_spmd(nc, [arrays], core_ids=[0])
    return r.results[0]["out_rows"]
```
